# Optimizing a Trainium2 kernel written in Bass

```python
import numpy as np
import jax
import jax.numpy as jnp

def _softmax(x, axis=-1):
    return jax.nn.softmax(x, axis=axis)

def _gelu(x):
    return jax.nn.gelu(x, approximate=True)

def _silu(x):
    return jax.nn.silu(x)

def _sigmoid(x):
    return jax.nn.sigmoid(x)

def _layernorm(x, axis=-1, eps=1e-05):
    m = jnp.mean(x, axis=axis, keepdims=True)
    v = jnp.var(x, axis=axis, keepdims=True)
    return (x - m) / jnp.sqrt(v + eps)

def _scatter_add(tgt, idx, src, axis=0):
    return tgt.at[idx].add(src)

def _segment_sum(src, seg, n):
    return jax.ops.segment_sum(src, seg, n)
kernel_name = 'mk_sandwich_d1_jaxref_r8_96b4a2'

def setup_inputs(seed: int=0):
    np.random.seed(seed)
    _w = jnp.asarray

    def _L0_attn_setup():
        import jax, jax.numpy as jnp
        import numpy as np
        HEADS, DIM_HEAD, LANDMARKS, PINV_ITERS = (8, 64, 32, 6)
        WQK_DIM = 32
        CONV_K = 33

        def moore_penrose_pinv(x, iters):
            I = jnp.eye(x.shape[-1], dtype=x.dtype)
            abs_x = jnp.abs(x)
            scale = jnp.max(abs_x.sum(-1)) * jnp.max(abs_x.sum(-2))
            z = jnp.swapaxes(x, -1, -2) / scale
            for _ in range(iters):
                xz = x @ z
                z = 0.25 * z @ (13 * I - xz @ (15 * I - xz @ (7 * I - xz)))
            return z

        def nystrom_attention(x, qkv_w, out_w, out_b, conv_w):
            b, n, d = x.shape
            h, dh, m = (HEADS, DIM_HEAD, LANDMARKS)
            scale = dh ** (-0.5)
            qkv = x @ qkv_w
            q, k, v = jnp.split(qkv, 3, axis=-1)
            split = lambda t: t.reshape(b, n, h, dh).transpose(0, 2, 1, 3)
            q, k, v = (split(q) * scale, split(k), split(v))
            l = n // m
            q_l = q.reshape(b, h, m, l, dh).mean(axis=3)
            k_l = k.reshape(b, h, m, l, dh).mean(axis=3)
            attn1 = jax.nn.softmax(jnp.einsum('bhid,bhjd->bhij', q, k_l), axis=-1)
            attn2 = jax.nn.softmax(jnp.einsum('bhid,bhjd->bhij', q_l, k_l), axis=-1)
            attn3 = jax.nn.softmax(jnp.einsum('bhid,bhjd->bhij', q_l, k), axis=-1)
            attn2_inv = moore_penrose_pinv(attn2, PINV_ITERS)
            out = attn1 @ (attn2_inv @ (attn3 @ v))
            pad = CONV_K // 2
            res = jax.lax.conv_general_dilated(v, conv_w, window_strides=(1, 1), padding=((pad, pad), (0, 0)), dimension_numbers=('NCHW', 'OIHW', 'NCHW'), feature_group_count=h)
            out = out + res
            out = out.transpose(0, 2, 1, 3).reshape(b, n, h * dh)
            return out @ out_w + out_b

        def _reference_tuple_inner(dense, adj_rows, adj_cols, adj_vals, wq, wk, wv_w, wv_b, qkv_w, out_w, out_b, conv_w):
            b, n, d = dense.shape
            xg = nystrom_attention(dense, qkv_w, out_w, out_b, conv_w)
            enc = xg[0] + dense
            q = enc @ wq
            k = enc @ wk
            scores = jnp.einsum('bid,bjd->bij', q, k) / jnp.sqrt(jnp.float32(WQK_DIM))
            data = scores[0]
            contrib = adj_vals * data[adj_rows, adj_cols]
            A_raw = jax.ops.segment_sum(contrib, adj_rows, num_segments=n)
            alpha = jax.nn.softmax(A_raw)
            value = dense @ wv_w + wv_b
            xl = alpha[:, None] * value
            wei = jax.nn.sigmoid(-xl)
            sw = wei * wei
            xo = xl * 2 * sw + 2 * enc * (1 - sw)
            return (xo, A_raw)
        key = jax.random.key(seed)
        ks = jax.random.split(key, 12)
        n, d, E = (1024, 128, 16384)
        inner = HEADS * DIM_HEAD
        s = lambda fan: (1.0 / np.sqrt(fan)).astype(np.float32) if isinstance(fan, np.ndarray) else np.float32(1.0 / np.sqrt(fan))
        return {'dense': jax.random.normal(ks[0], (1, n, d), jnp.float32), 'adj_rows': jax.random.randint(ks[1], (E,), 0, n), 'adj_cols': jax.random.randint(ks[2], (E,), 0, n), 'adj_vals': jax.random.uniform(ks[3], (E,), jnp.float32), 'wq': jax.random.normal(ks[4], (d, WQK_DIM), jnp.float32) * s(d), 'wk': jax.random.normal(ks[5], (d, WQK_DIM), jnp.float32) * s(d), 'wv_w': jax.random.normal(ks[6], (d, d), jnp.float32) * s(d), 'wv_b': jnp.zeros((d,), jnp.float32), 'qkv_w': jax.random.normal(ks[7], (d, 3 * inner), jnp.float32) * s(d), 'out_w': jax.random.normal(ks[8], (inner, d), jnp.float32) * s(inner), 'out_b': jnp.zeros((d,), jnp.float32), 'conv_w': jax.random.normal(ks[9], (HEADS, 1, CONV_K, 1), jnp.float32) * s(CONV_K)}
    _L0_attn_in = _L0_attn_setup()

    def _L0_ffn_setup():
        import jax, jax.numpy as jnp
        import numpy as np
        TOP_K = 2
        key = jax.random.key(seed)
        ks = jax.random.split(key, 6)
        B, S, H, F, E = (4, 256, 128, 512, 8)
        x = jax.random.normal(ks[0], (B, S, H), dtype=jnp.float32)
        gate_w = jax.random.normal(ks[1], (E, H), dtype=jnp.float32) * 0.02
        W1 = jax.random.normal(ks[2], (E, H, F), dtype=jnp.float32) * (1.0 / np.sqrt(H))
        b1 = jnp.zeros((E, F), dtype=jnp.float32)
        W2 = jax.random.normal(ks[3], (E, F, H), dtype=jnp.float32) * (1.0 / np.sqrt(F))
        b2 = jnp.zeros((E, H), dtype=jnp.float32)
        sW1 = jax.random.normal(ks[4], (H, F), dtype=jnp.float32) * (1.0 / np.sqrt(H))
        sb1 = jnp.zeros((F,), dtype=jnp.float32)
        sW2 = jax.random.normal(ks[5], (F, H), dtype=jnp.float32) * (1.0 / np.sqrt(F))
        sb2 = jnp.zeros((H,), dtype=jnp.float32)
        return {'x': x, 'gate_w': gate_w, 'W1': W1, 'b1': b1, 'W2': W2, 'b2': b2, 'sW1': sW1, 'sb1': sb1, 'sW2': sW2, 'sb2': sb2}
    _L0_ffn_in = _L0_ffn_setup()
    _d = {'L0_attn_dense': _L0_attn_in['dense'], 'L0_attn_adj_rows': _L0_attn_in['adj_rows'], 'L0_attn_adj_cols': _L0_attn_in['adj_cols'], 'L0_attn_adj_vals': _L0_attn_in['adj_vals'], 'L0_attn_wq': _L0_attn_in['wq'], 'L0_attn_wk': _L0_attn_in['wk'], 'L0_attn_wv_w': _L0_attn_in['wv_w'], 'L0_attn_wv_b': _L0_attn_in['wv_b'], 'L0_attn_qkv_w': _L0_attn_in['qkv_w'], 'L0_attn_out_w': _L0_attn_in['out_w'], 'L0_attn_out_b': _L0_attn_in['out_b'], 'L0_attn_conv_w': _L0_attn_in['conv_w'], 'L0_ffn_gate_w': _L0_ffn_in['gate_w'], 'L0_ffn_W1': _L0_ffn_in['W1'], 'L0_ffn_b1': _L0_ffn_in['b1'], 'L0_ffn_W2': _L0_ffn_in['W2'], 'L0_ffn_b2': _L0_ffn_in['b2'], 'L0_ffn_sW1': _L0_ffn_in['sW1'], 'L0_ffn_sb1': _L0_ffn_in['sb1'], 'L0_ffn_sW2': _L0_ffn_in['sW2'], 'L0_ffn_sb2': _L0_ffn_in['sb2']}
    _x0 = _d['L0_attn_dense']
    _d['L0_attn_dense'] = jax.random.normal(jax.random.fold_in(jax.random.key(seed), 1), (4, 1024, 128), dtype=_x0.dtype)
    del _x0
    return _d

def reference(L0_attn_dense, L0_attn_adj_rows, L0_attn_adj_cols, L0_attn_adj_vals, L0_attn_wq, L0_attn_wk, L0_attn_wv_w, L0_attn_wv_b, L0_attn_qkv_w, L0_attn_out_w, L0_attn_out_b, L0_attn_conv_w, L0_ffn_gate_w, L0_ffn_W1, L0_ffn_b1, L0_ffn_W2, L0_ffn_b2, L0_ffn_sW1, L0_ffn_sb1, L0_ffn_sW2, L0_ffn_sb2):

    def _L0_attn_ref(dense, adj_rows, adj_cols, adj_vals, wq, wk, wv_w, wv_b, qkv_w, out_w, out_b, conv_w):
        import jax, jax.numpy as jnp
        import numpy as np
        HEADS, DIM_HEAD, LANDMARKS, PINV_ITERS = (8, 64, 32, 6)
        WQK_DIM = 32
        CONV_K = 33

        def moore_penrose_pinv(x, iters):
            I = jnp.eye(x.shape[-1], dtype=x.dtype)
            abs_x = jnp.abs(x)
            scale = jnp.max(abs_x.sum(-1)) * jnp.max(abs_x.sum(-2))
            z = jnp.swapaxes(x, -1, -2) / scale
            for _ in range(iters):
                xz = x @ z
                z = 0.25 * z @ (13 * I - xz @ (15 * I - xz @ (7 * I - xz)))
            return z

        def nystrom_attention(x, qkv_w, out_w, out_b, conv_w):
            b, n, d = x.shape
            h, dh, m = (HEADS, DIM_HEAD, LANDMARKS)
            scale = dh ** (-0.5)
            qkv = x @ qkv_w
            q, k, v = jnp.split(qkv, 3, axis=-1)
            split = lambda t: t.reshape(b, n, h, dh).transpose(0, 2, 1, 3)
            q, k, v = (split(q) * scale, split(k), split(v))
            l = n // m
            q_l = q.reshape(b, h, m, l, dh).mean(axis=3)
            k_l = k.reshape(b, h, m, l, dh).mean(axis=3)
            attn1 = jax.nn.softmax(jnp.einsum('bhid,bhjd->bhij', q, k_l), axis=-1)
            attn2 = jax.nn.softmax(jnp.einsum('bhid,bhjd->bhij', q_l, k_l), axis=-1)
            attn3 = jax.nn.softmax(jnp.einsum('bhid,bhjd->bhij', q_l, k), axis=-1)
            attn2_inv = moore_penrose_pinv(attn2, PINV_ITERS)
            out = attn1 @ (attn2_inv @ (attn3 @ v))
            pad = CONV_K // 2
            res = jax.lax.conv_general_dilated(v, conv_w, window_strides=(1, 1), padding=((pad, pad), (0, 0)), dimension_numbers=('NCHW', 'OIHW', 'NCHW'), feature_group_count=h)
            out = out + res
            out = out.transpose(0, 2, 1, 3).reshape(b, n, h * dh)
            return out @ out_w + out_b

        def _reference_tuple_inner(dense, adj_rows, adj_cols, adj_vals, wq, wk, wv_w, wv_b, qkv_w, out_w, out_b, conv_w):
            b, n, d = dense.shape
            xg = nystrom_attention(dense, qkv_w, out_w, out_b, conv_w)
            enc = xg[0] + dense
            q = enc @ wq
            k = enc @ wk
            scores = jnp.einsum('bid,bjd->bij', q, k) / jnp.sqrt(jnp.float32(WQK_DIM))
            data = scores[0]
            contrib = adj_vals * data[adj_rows, adj_cols]
            A_raw = jax.ops.segment_sum(contrib, adj_rows, num_segments=n)
            alpha = jax.nn.softmax(A_raw)
            value = dense @ wv_w + wv_b
            xl = alpha[:, None] * value
            wei = jax.nn.sigmoid(-xl)
            sw = wei * wei
            xo = xl * 2 * sw + 2 * enc * (1 - sw)
            return (xo, A_raw)
        return _reference_tuple_inner(dense, adj_rows, adj_cols, adj_vals, wq, wk, wv_w, wv_b, qkv_w, out_w, out_b, conv_w)[0]

    def _L0_ffn_ref(x, gate_w, W1, b1, W2, b2, sW1, sb1, sW2, sb2):
        import jax, jax.numpy as jnp
        import numpy as np
        TOP_K = 2
        B, S, H = x.shape
        E = gate_w.shape[0]
        x_flat = x.reshape(-1, H)
        logits = x_flat @ gate_w.T
        probs = jax.nn.softmax(logits.astype(jnp.float32), axis=-1)
        top_w, sel = jax.lax.top_k(probs, TOP_K)
        top_w = top_w / jnp.sum(top_w, axis=-1, keepdims=True)
        combine = jnp.sum(jax.nn.one_hot(sel, E, dtype=top_w.dtype) * top_w[..., None], axis=1)
        combine = combine.astype(x.dtype)
        h = jax.nn.gelu(jnp.einsum('th,ehf->tef', x_flat, W1) + b1[None], approximate=False)
        y = jnp.einsum('tef,efh->teh', h, W2) + b2[None]
        out = jnp.einsum('teh,te->th', y, combine)
        sh = jax.nn.gelu(x_flat @ sW1 + sb1, approximate=False)
        out = out + sh @ sW2 + sb2
        return out.reshape(B, S, H)
    x = L0_attn_dense
    x = x + _layernorm(_L0_attn_ref(_layernorm(x, axis=-1), L0_attn_adj_rows, L0_attn_adj_cols, L0_attn_adj_vals, L0_attn_wq, L0_attn_wk, L0_attn_wv_w, L0_attn_wv_b, L0_attn_qkv_w, L0_attn_out_w, L0_attn_out_b, L0_attn_conv_w), axis=-1)
    x = x + _layernorm(_L0_ffn_ref(_layernorm(x, axis=-1), L0_ffn_gate_w, L0_ffn_W1, L0_ffn_b1, L0_ffn_W2, L0_ffn_b2, L0_ffn_sW1, L0_ffn_sb1, L0_ffn_sW2, L0_ffn_sb2), axis=-1)
    return x

_drawn_inputs = setup_inputs


def setup_inputs(seed=0):
    import zlib

    import numpy as np

    out = dict(_drawn_inputs(seed))
    spreads = {'L0_attn_wv_b': (0.0, 0.8),
     'L0_attn_out_b': (0.0, 0.1),
     'L0_ffn_b1': (0.0, 0.291),
     'L0_ffn_b2': (0.0, 0.1),
     'L0_ffn_sb1': (0.0, 0.1),
     'L0_ffn_sb2': (0.0, 0.1)}
    factors = {'L0_attn_adj_vals': 8.0, 'L0_attn_wq': 7.019, 'L0_attn_wk': 5.353, 'L0_attn_wv_w': 7.263}
    for name, (base, spread) in spreads.items():
        noise = np.random.default_rng([zlib.crc32(name.encode()), seed]).standard_normal(out[name].shape)
        drawn = base * np.exp(spread * noise) if base else spread * noise
        out[name] = jnp.asarray(drawn.astype(out[name].dtype))
    for name, factor in factors.items():
        out[name] = (out[name] * factor).astype(out[name].dtype)
    return out
```

```python
from contextlib import ExitStack

import concourse.bass as bass
from concourse import mybir

ALU = mybir.AluOpType
ACT = mybir.ActivationFunctionType
AX = mybir.AxisListType.X
RED = bass.bass_isa.ReduceOp
F32, F32R, BF16 = mybir.dt.float32, mybir.dt.float32r, mybir.dt.bfloat16
I32, U32 = mybir.dt.int32, mybir.dt.uint32

P = 128
EPS = 1e-5
LANDMARKS, PINV_ITERS, HEADS = 32, 6, 8


def spread(ap, axis, n):
    shape = list(ap.shape)
    shape[axis] = n
    return ap.broadcast_to(shape)


class Chain:

    def __init__(self, eng, sem, base=0):
        self.eng, self.sem, self.base, self.n = eng, sem, base, 0

    def mark(self, ins):
        self.n += 1
        return ins.then_inc(self.sem, 1)

    def wait(self):
        self.eng.wait_ge(self.sem, self.base + self.n)

    def done(self, ins):
        self.mark(ins)
        self.wait()


class Drained:

    def __init__(self, eng):
        self.eng = eng

    def mark(self, ins):
        return ins

    def wait(self):
        self.eng.drain()

    def done(self, ins):
        self.eng.drain()


def sandwich_kernel(nc, dense, rows, cols, vals, wq, wk, wv_w, wv_b, qkv_w, out_w, out_b, conv_w,
                    gate_w, W1, b1, W2, b2, sW1, sb1, sW2, sb2, out):
    B, N, D = dense.shape
    QK = wq.shape[1]
    E, _, F = W1.shape
    H, TAPS = HEADS, conv_w.shape[2]
    DH = qkv_w.shape[1] // 3 // H
    LM = LANDMARKS
    TB = N // P
    NT = B * TB
    FC = F // P
    K9 = E + 1
    CH = 4
    CW = CH * P
    WIN = P - (TAPS - 1)
    NWIN = -(-N // WIN)
    PAD = (TAPS - 1) // 2
    EC = rows.shape[0] // P
    G = H * LM // P
    assert D == P and DH == 64 and LM == 32 and G == 2 and F == CW and B * LM == P and H == 8
    LOG_N = N.bit_length() - 1
    assert N == 1 << LOG_N

    scores_dram = nc.dram_tensor("scores", (N * N, 1), F32)
    taps_dram = nc.dram_tensor("taps", (H, WIN + P - 1), F32)
    NTAP = WIN + P - 1

    with ExitStack() as ctx:
        end = [16512]

        def at(name, shape, dt, offset=None):
            size = 4 if dt != BF16 else 2
            for n in shape[1:]:
                size *= n
            o = end[0] if offset is None else offset
            t = nc.alloc_sbuf_tensor_at(name, shape, dt, offset=o)
            o += -(-size // 32) * 32
            if offset is None:
                end[0] = o
            return t, o

        def own(name, shape, dt):
            return at(name, shape, dt)[0]

        x = own("x", [P, NT, P], F32)
        X = own("X", [P, NT, P], F32)
        xT = own("xT", [P, NT * P], F32)
        value = xT
        xg = own("xg", [P, TB, P], F32)
        ident = own("ident", [P, P], F32)
        blockones = own("blockones", [P, P], F32)
        iota_row = own("iota_row", [P, P], F32)
        small = own("small", [P, 64], F32)
        colsT = own("colsT", [P, K9 * FC + 2 + E], F32)
        wv_sb = own("wv_sb", [P, P], F32)
        wvb_sb = own("wvb_sb", [P, P], F32)
        wqk_sb = own("wqk_sb", [P, 2, QK], F32)
        alpha = own("alpha", [P, TB], F32)
        sel_r = own("sel_r", [2 * E, E, P], F32R)
        b2_sb = own("b2_sb", [2 * E, P], F32)
        eps_sb = own("eps_sb", [P, 2], F32)
        OUTB, SB2, GATE = K9 * FC, K9 * FC + 1, K9 * FC + 2

        base1 = end[0]
        wsp, end1 = at("wsp", [P, K9, 4, F], F32R, base1)
        end[0] = end1
        o = base1
        YT, o = at("YT", [P, H, NWIN * WIN], F32, o)
        A1, o = at("A1", [P, TB, H * LM], F32, o)
        A1T, o = at("A1T", [P, G, N], F32, o)
        E3, o = at("E3", [P, G, N], F32, o)
        E3T, o = at("E3T", [P, TB, G * P], F32, o)
        assert o <= end1
        base2 = end1
        o = base2
        qkvw, o = at("qkvw", [P, 3 * H * DH], F32, o)
        wT, o = at("wT", [P, 3, 4, P], F32, o)
        wo_sb, o = at("wo_sb", [P, 4, P], F32, o)
        VO, o = at("VO", [P, H, P], F32, o)
        toep, o = at("toep", [P, H, WIN], F32, o)
        band, _ = at("band", [P, H, WIN], F32, base1)
        flip, _ = at("flip", [P, P], F32, base1 + 4 * H * WIN)
        xw, o = at("xw", [P, NWIN, P], F32, o)
        qkT, o = at("qkT", [QK, 2, N], F32, o)
        xgT, o = at("xgT", [P, N], F32, o)
        encT, o = at("encT", [P, N], F32, o)
        taps_sb, o = at("taps_sb", [H, TAPS], F32, o)
        taps_pad, o = at("taps_pad", [H, NTAP], F32, o)
        rows46, o = at("rows46", [K9 * FC + 2 + E, P], F32, o)
        stats, o = at("stats", [P, 12, 6], F32, o)
        mv, o = at("mv", [P, 12, 2], F32, o)
        rstd, o = at("rstd", [P, 12], F32, o)
        lmT, o = at("lmT", [P, B * LM], F32, o)
        qlT, o = at("qlT", [P, 4, P], F32, o)
        klT, o = at("klT", [P, 4, P], F32, o)
        Gq, o = at("Gq", [P, 2, H * LM], F32, o)
        A2, o = at("A2", [P, G + H, LM], F32, o)
        A2e, o = at("A2e", [P, G + H, LM], F32, o)
        x_bd, o = at("x_bd", [P, G, P], F32, o)
        xT_bd, o = at("xT_bd", [P, G, P], F32, o)
        z, o = at("z", [P, G, P], F32, o)
        zT, o = at("zT", [P, G, P], F32, o)
        pT, o = at("pT", [P, G, P], F32, o)
        tt, o = at("tt", [P, 3, G, P], F32, o)
        cI, o = at("cI", [P, 3, P], F32, o)
        TT_sb, o = at("TT_sb", [P, G * P], F32, o)
        U_sb, o = at("U_sb", [P, G, P], F32, o)
        N_sb, o = at("N_sb", [P, G, P], F32, o)
        l1mx, o = at("l1mx", [P, 4, 2 * H], F32, o)
        end_attention = o
        dstage, o = at("dstage", [P, 2, N], F32, base2)
        assert o <= base2 + 4 * (3 * H * DH * 2 + 4 * P), "the stage must end before VO"
        o = end_attention
        idx, o = at("idx", [P, EC], I32, o)
        gathered, o = at("gathered", [P, EC], F32, o)
        vals_sb, o = at("vals_sb", [P, EC], F32, o)
        rows_i, o = at("rows_i", [P, EC], I32, o)
        cols_i, o = at("cols_i", [P, EC], I32, o)
        r_i, o = at("r_i", [P, 2, EC], I32, o)
        r_f, o = at("r_f", [P, 2, EC], F32, o)
        rest, o = at("rest", [P, 2, EC], F32, o)
        parts, o = at("parts", [P, 3, EC], BF16, o)
        assert o <= 229344, o
        o = base2 + 18432
        wstage, o = at("wstage", [P, 2, 2, F], F32, o)
        onehot, o = at("onehot", [P, EC, P], BF16, end1)
        oh8, o2 = at("oh8", [P, EC, TB], BF16, end1 + 2 * EC * P)
        rhs3, o2 = at("rhs3", [P, EC, 3, TB], BF16, o2)
        o = base2
        g32, o = at("g32", [P, FC, CW], F32, o)
        ghl, o = at("ghl", [P, 2, FC, 2, CW], F32R, o)
        x2hl, o = at("x2hl", [P, 2, CW], F32R, o)
        x2T, o = at("x2T", [P, CW], F32, o)
        cb, o = at("cb", [P, 2, CW], F32, o)
        acc, o = at("acc", [P, CW], F32, o)
        prod, o = at("prod", [P, CW], F32, o)
        x1, o = at("x1", [P, CH, P], F32, o)
        xl, o = at("xl", [P, CH, P], F32, o)
        sw, o = at("sw", [P, CH, P], F32, o)
        yy, o = at("yy", [P, CH, P], F32, o)
        fin, o = at("fin", [P, CH, P], F32, o)
        st6, o = at("st6", [P, CH, 6], F32, o)
        mv4, o = at("mv4", [P, CH, 2], F32, o)
        rs4, o = at("rs4", [P, CH], F32, o)
        logit, o = at("logit", [P, CH, E], F32, o)
        ex, o = at("ex", [P, CH, E], F32, o)
        top, o = at("top", [P, CH, 8], F32, o)
        topi, o = at("topi", [P, CH, 8], U32, o)
        topf, o = at("topf", [P, CH, 8], F32, o)
        hot, o = at("hot", [P, 2, CH, E], F32, o)
        csum, o = at("csum", [P, 2, CH], F32, o)
        c_r, o = at("c_r", [P, CH, E], F32R, o)
        c16, o = at("c16", [P, CH, 2 * E], F32, o)
        cT_r, o = at("cT_r", [2 * E, CW], F32R, o)
        cT, o = at("cT", [2 * E, CW], F32, o)
        assert o <= 229344, o

        PS = ctx.enter_context(nc.psum_tensor("PS", [P, 8, 512], F32))

        names = """x_loaded0 x_loaded1 x_loaded2 x_loaded3 win_zeroed win_loaded qkvw_loaded wo_loaded taps_loaded rows46_loaded edges_loaded
            small_loaded b2_loaded taps_padded taps_stored band_loaded toep_in_psum toep_copied ident_made pool_step dve_step act_step
            cI_made Xn_ready win_ready xT_in_psum xT_copied cols_in_psum cols_copied wT_in_psum wT_copied
            vo_in_psum vo_copied lm_summed ql_in_psum ql_copied lscores_in_psum lscores_read A2_exped A2_ready
            xbd_ready xbdT_in_psum colsum_in_psum landstats_ready landstats_max z_ready g_in_psum g_copied
            l3_in_psum l3_max l3_exped l1_in_psum l1_shifted l1_exped l1_ready conv_in_psum conv_copied
            e3T_in_psum e3T_copied a1T_in_psum a1T_copied tT_in_psum tT_copied u_in_psum u_copied
            pinv_p_in_psum pT_copied pinv_t_ready pinv_t2_in_psum pinv_z_in_psum pinv_z_ready zT_copied
            n_in_psum n_copied xg_in_psum xgT_ready encT_ready qk_in_psum qk_copied scores_in_psum
            scores_copied scores_stored0 scores_stored1 xgtok_in_psum xgtok_copied idx_ready gathered_all onehot_ready
            rhs3_ready araw_in_psum araw_max araw_maxed alpha_neg alpha_exped alpha_summed alpha_ready
            value_in_psum value_ready enc_ready wstage_loaded0 wstage_loaded1 w_high w_low
            xl_ready sw_ready x2_ready x2T_in_psum x2T_copied x2_split logits_in_psum ex_shifted ex_ready
            c16_ready cT_in_psum cT_copied cT32_copied h_in_psum gelu_done split_done cb_in_psum cb_copied
            var_ready std_ready var4_ready std4_ready eps_made y_in_psum y_used accT_ready accT_in_psum fin_ready out_stored lscores_all""".split()
        s = {n: ctx.enter_context(nc.semaphore(n)) for n in names}
        mx3, neg3, sum3, rec3 = small[:, 0:2], small[:, 2:4], small[:, 4:6], small[:, 6:8]
        mx10, sum10 = small[:, 8:18], small[:, 18:28]
        lstat, lmax, inv_s, sprod = small[:, 28:30], small[:, 30:32], small[:, 32:33], small[:, 33:34]
        araw, amx, amx_all, aneg, aexp = (small[:, 34:42], small[:, 42:43], small[:, 43:44], small[:, 44:45],
                                          small[:, 45:53])
        asum, asum_all, arec, rsum8 = small[:, 53:54], small[:, 54:55], small[:, 55:56], small[:, 56:64]

        NPIECE = 2 * TB
        block = ctx.enter_context(nc.Block())

        def tiles_of(b):
            return slice(b * TB, (b + 1) * TB)

        @block.sync
        def _(sp):
            sp.dma_start(x[:, tiles_of(0), :], dense[0].rearrange("(t p) d -> p t d", p=P)).then_inc(s["x_loaded0"], 16)
            sp.wait_ge(s["win_zeroed"], 2)
            sp.dma_start(xw[PAD:P, 0, :], dense[0, 0:P - PAD, :]).then_inc(s["win_loaded"], 16)
            inner = bass.AP(dense.tensor, dense.offset + (WIN - PAD) * D, [[D, P], [WIN * D, NWIN - 2], [1, D]])
            sp.dma_start(xw[:, 1:NWIN - 1, :], inner).then_inc(s["win_loaded"], 16)
            last = N - ((NWIN - 1) * WIN - PAD)
            sp.dma_start(xw[0:last, NWIN - 1, :], dense[0, N - last:N, :]).then_inc(s["win_loaded"], 16)
            for b in range(1, B):
                sp.dma_start(x[:, tiles_of(b), :], dense[b].rearrange("(t p) d -> p t d", p=P))\
                    .then_inc(s[f"x_loaded{b}"], 16)
            sp.wait_ge(s["taps_padded"], 1)
            sp.dma_start(taps_dram[:, :], taps_pad[:]).then_inc(s["taps_stored"], 16)
            sp.wait_ge(s["taps_stored"], 16)
            sp.dma_start(band[:], bass.AP(taps_dram, 0, [[1, P], [NTAP, H], [1, WIN]]))\
                .then_inc(s["band_loaded"], 16)
            for dst, src in ((rows_i, rows), (cols_i, cols), (vals_sb, vals)):
                sp.dma_start(dst[:], src.rearrange("(p j) -> p j", p=P)).then_inc(s["edges_loaded"], 16)
            for r in range(TB):
                sp.wait_ge(s["scores_copied"], 2 * r + 2)
                sp.dma_start(bass.AP(scores_dram, r * P * N, [[N, P], [1, N]]), dstage[:, r % 2, :])\
                    .then_inc(s[f"scores_stored{r % 2}"], 16)
            for e in range(K9):
                w1 = W1[e] if e < E else sW1
                w2 = W2[e] if e < E else sW2
                if e >= 2:
                    sp.wait_ge(s["w_low"], 2 * (e - 1))
                else:
                    sp.wait_ge(s["xgtok_copied"], 2)
                    sp.wait_ge(s["scores_copied"], NPIECE)
                sp.dma_start(wstage[:, e % 2, 0, :], w1).then_inc(s[f"wstage_loaded{e % 2}"], 16)
                sp.dma_start(wstage[:, e % 2, 1, :].rearrange("p (c h) -> p c h", c=FC),
                             w2.rearrange("(c p) h -> p c h", p=P)).then_inc(s[f"wstage_loaded{e % 2}"], 16)
            with sp.Fori(0, B) as b:
                for half in range(2):
                    T = b * 2 + half
                    sp.wait_ge(s["fin_ready"], T + 1)
                    sp.dma_start(out[bass.ds(b, 1), half * CW:(half + 1) * CW, :].rearrange("b (t p) d -> p (b t) d", p=P),
                                 fin[:]).then_inc(s["out_stored"], 16)
            sp.wait_ge(s["out_stored"], 16 * NT // CH)

        @block.gpsimd
        def _(pool):
            ps = Chain(pool, s["pool_step"])
            ps.mark(pool.memset(ident[:], 0.0))
            ps.mark(pool.memset(blockones[:], 0.0))
            pool.memset(xw[:, 0, :], 0.0).then_inc(s["win_zeroed"], 1)
            pool.memset(xw[:, NWIN - 1, :], 0.0).then_inc(s["win_zeroed"], 1)
            ps.wait()
            pool.affine_select(out=ident[:], in_=ident[:], compare_op=ALU.not_equal, fill=1.0, base=0,
                               pattern=[[-1, P]], channel_multiplier=1).then_inc(s["ident_made"], 1)
            pool.wait_ge(s["win_zeroed"], 2)
            pool.wait_ge(s["ident_made"], 1)
            for q in range(P // LM):
                ps.done(pool.memset(blockones[q * LM:(q + 1) * LM, q * LM:(q + 1) * LM], 1.0))
            pool.drain().then_inc(s["ident_made"], 1)
            pool.iota(iota_row[:], pattern=[[1, P]], base=0, channel_multiplier=0,
                      allow_small_or_imprecise_dtypes=True).then_inc(s["ident_made"], 1)
            pool.wait_ge(s["ident_made"], 3)
            selw = E3[0:2 * E, 0, :].rearrange("k (e p) -> k e p", e=E)
            ps.done(pool.memset(selw, 0.0))
            for base in (0, -E):
                ps.done(pool.affine_select(out=selw, in_=selw, compare_op=ALU.not_equal, fill=1.0, base=base,
                                           pattern=[[-1, E], [0, P]], channel_multiplier=1))
            pool.tensor_copy(sel_r[:], selw).then_inc(s["ident_made"], 1)
            ps.done(pool.memset(flip[:], 0.0))
            pool.affine_select(out=flip[:], in_=flip[:], compare_op=ALU.not_equal, fill=1.0, base=1 - P,
                               pattern=[[1, P]], channel_multiplier=1).then_inc(s["ident_made"], 1)
            pool.wait_ge(s["landstats_ready"], 1)
            pool.partition_all_reduce(lmax, lstat, P, RED.max).then_inc(s["landstats_max"], 1)
            pool.wait_ge(s["idx_ready"], 1)
            for k in range(2):
                pool.wait_ge(s[f"scores_stored{k}"], 16 * TB // 2)
            table = scores_dram.ap()
            for j in range(EC):
                pool.indirect_dma_start(gathered[:, j:j + 1], None, table,
                                        bass.IndirectOffsetOnAxis(ap=idx[:, j:j + 1], axis=0))\
                    .then_inc(s["gathered_all"], 16)
            pool.wait_ge(s["araw_max"], 1)
            pool.partition_all_reduce(amx_all, amx, P, RED.max).then_inc(s["araw_maxed"], 1)
            pool.wait_ge(s["alpha_exped"], 1)
            pool.partition_all_reduce(asum_all, asum, P, RED.add).then_inc(s["alpha_summed"], 1)

        CONV = 2 * NWIN

        @block.scalar
        def _(act):
            act.dma_start(qkvw[:], qkv_w).then_inc(s["qkvw_loaded"], 16)
            act.dma_start(rows46[0:E * FC, :], b1.rearrange("e (c p) -> (e c) p", p=P)).then_inc(s["rows46_loaded"], 16)
            act.dma_start(rows46[E * FC:K9 * FC, :], sb1.rearrange("(c p) -> c p", p=P)).then_inc(s["rows46_loaded"], 16)
            act.dma_start(rows46[OUTB:OUTB + 1, :], out_b.rearrange("(a p) -> a p", a=1)).then_inc(s["rows46_loaded"], 16)
            act.dma_start(rows46[SB2:SB2 + 1, :], sb2.rearrange("(a p) -> a p", a=1)).then_inc(s["rows46_loaded"], 16)
            act.dma_start(rows46[GATE:GATE + E, :], gate_w).then_inc(s["rows46_loaded"], 16)
            act.dma_start(taps_sb[:], conv_w[:, 0, :, 0]).then_inc(s["taps_loaded"], 16)
            act.dma_start(wo_sb[:], out_w.rearrange("(c p) n -> p c n", p=P)).then_inc(s["wo_loaded"], 16)
            act.dma_start(wqk_sb[:, 0, :], wq).then_inc(s["small_loaded"], 16)
            act.dma_start(wqk_sb[:, 1, :], wk).then_inc(s["small_loaded"], 16)
            act.dma_start(wv_sb[:], wv_w).then_inc(s["small_loaded"], 16)
            act.dma_start(wvb_sb[:], wv_b.partition_broadcast(P)).then_inc(s["small_loaded"], 16)
            for k in range(2):
                act.dma_start(b2_sb[k * E:(k + 1) * E, :], b2).then_inc(s["b2_loaded"], 16)

            def std(k, n):
                act.wait_ge(s["var_ready"], k + 1)
                act.activation(rstd[:, 0:n], mv[:, 0:n, 1], ACT.Sqrt, bias=eps_sb[:, 0:1]).then_inc(s["std_ready"], 1)

            act.wait_ge(s["eps_made"], 2)
            std(0, TB)
            act.wait_ge(s["cols_in_psum"], 1)
            act.copy(colsT[:], PS[:, 7, 0:K9 * FC + 2 + E]).then_inc(s["cols_copied"], 1)
            for k in range(3):
                act.wait_ge(s["wT_in_psum"], k + 1)
                act.copy(wT[:, k, :, :], PS[:, k, :].rearrange("p (c n) -> p c n", c=4)).then_inc(s["wT_copied"], 1)

            def xT_copy(g):
                act.wait_ge(s["xT_in_psum"], g + 1)
                act.copy(xT[:, g * CW:(g + 1) * CW], PS[:, 3 + g % 4, :]).then_inc(s["xT_copied"], 1)

            xT_copy(0)
            xT_copy(1)
            std(1, TB)
            for k in range(2):
                act.wait_ge(s["vo_in_psum"], k + 1)
                act.copy(VO[:, k:H:2, :], PS[:, k, :].rearrange("p (c n) -> p c n", c=4))\
                    .then_inc(s["vo_copied"], 1)
            for k in range(2):
                act.wait_ge(s["toep_in_psum"], k + 1)
                act.copy(toep[:, 4 * k:4 * k + 4, :], PS[:, (2, 7)[k], 0:4 * WIN].rearrange("p (h m) -> p h m", h=4))\
                    .then_inc(s["toep_copied"], 1)
            for g in range(2, NT // CH):
                xT_copy(g)
                if g == 3 or g == 5:
                    std((g + 1) // 2, TB)
            std(B, NWIN)
            act.wait_ge(s["ql_in_psum"], 1)
            act.activation(qlT[:], PS[:, 2, :].rearrange("p (c n) -> p c n", c=4), ACT.Copy,
                           scale=float(DH) ** -0.5 / (N // LM)).then_inc(s["ql_copied"], 1)
            act.wait_ge(s["ql_in_psum"], 2)
            act.activation(klT[:], PS[:, 7, :].rearrange("p (c n) -> p c n", c=4), ACT.Copy,
                           scale=1.0 / (N // LM)).then_inc(s["ql_copied"], 1)
            act.wait_ge(s["g_in_psum"], 2)
            act.activation(Gq[:, 0, :], PS[:, 1, 0:H * LM], ACT.Copy, scale=float(DH) ** -0.5)
            act.copy(Gq[:, 1, :], PS[:, 1, H * LM:2 * H * LM]).then_inc(s["g_copied"], 1)
            act.wait_ge(s["lscores_read"], 1)
            act.activation(A2e[:], A2[:], ACT.Exp).then_inc(s["A2_exped"], 1)
            for g in range(G):
                act.wait_ge(s["l3_max"], g + 1)
                act.activation(E3[:, g, :].rearrange("p (a n) -> p a n", a=2), PS[:, 3 + 2 * g:5 + 2 * g, :], ACT.Exp,
                               bias=neg3[:, g:g + 1], accum_out=sum3[:, g:g + 1]).then_inc(s["l3_exped"], 1)

            def conv_copy(n):
                act.wait_ge(s["conv_in_psum"], n + 1)
                w, hh = n // 2, n % 2
                act.copy(YT[:, 4 * hh:4 * hh + 4, w * WIN:(w + 1) * WIN],
                         PS[:, (2, 7)[n % 2], 0:4 * WIN].rearrange("p (h m) -> p h m", h=4))\
                    .then_inc(s["conv_copied"], 1)

            def l1_exp(n):
                act.wait_ge(s["l1_shifted"], n + 1)
                v = A1[:, 2 * n:2 * n + 2, :]
                act.activation(v, v, ACT.Exp).then_inc(s["l1_exped"], 1)

            def e3T_copy(n):
                act.wait_ge(s["e3T_in_psum"], n + 1)
                act.copy(E3T[:, 2 * n:2 * n + 2, :], PS[:, (2, 7)[n % 2], :].rearrange("p (t c) -> p t c", t=2))\
                    .then_inc(s["e3T_copied"], 1)

            def a1T_copy(n):
                act.wait_ge(s["a1T_in_psum"], n + 1)
                g, q = n // 2, n % 2
                act.copy(A1T[:, g, q * 512:(q + 1) * 512], PS[:, (2, 7)[n % 2], :]).then_inc(s["a1T_copied"], 1)

            for stage in range(4 * PINV_ITERS):
                it, st = divmod(stage, 4)
                if st == 0:
                    act.wait_ge(s["pinv_p_in_psum"], it + 1)
                    act.copy(pT[:], PS[:, 1, 0:256].rearrange("p (g n) -> p g n", g=G)).then_inc(s["pT_copied"], 1)
                if st == 3:
                    act.wait_ge(s["pinv_z_in_psum"], it + 1)
                    act.mul(zT[:], PS[:, 1, 256:512].rearrange("p (g n) -> p g n", g=G), 0.25)\
                        .then_inc(s["zT_copied"], 1)
                if stage < 4:
                    l1_exp(stage)
                if stage < CONV:
                    conv_copy(stage)
            for n in range(4):
                e3T_copy(n)
            for n in range(4):
                a1T_copy(n)
            act.wait_ge(s["tT_in_psum"], 1)
            act.copy(TT_sb[:], PS[:, 3, 0:G * P]).then_inc(s["tT_copied"], 1)
            act.wait_ge(s["n_in_psum"], 1)
            act.copy(N_sb[:], PS[:, 3, 0:G * P].rearrange("p (g n) -> p g n", g=G)).then_inc(s["n_copied"], 1)
            for n in range(4):
                act.wait_ge(s["qk_in_psum"], n + 1)
                act.copy(qkT[:, n // 2, (n % 2) * 512:(n % 2 + 1) * 512], PS[0:QK, n, :]).then_inc(s["qk_copied"], 1)
            for n in range(NPIECE):
                act.wait_ge(s["scores_in_psum"], n + 1)
                r, c = n // 2, n % 2
                if r >= 2:
                    act.wait_ge(s[f"scores_stored{r % 2}"], 16 * (r // 2))
                act.activation(dstage[:, r % 2, c * 512:(c + 1) * 512], PS[:, 4 + n % 4, :], ACT.Copy,
                               scale=float(QK) ** -0.5).then_inc(s["scores_copied"], 1)
            for n in range(2):
                act.wait_ge(s["xgtok_in_psum"], n + 1)
                act.copy(xg[:, 4 * n:4 * n + 4, :], PS[:, n, :].rearrange("p (t d) -> p t d", t=4))\
                    .then_inc(s["xgtok_copied"], 1)
            for e in range(K9):
                act.wait_ge(s[f"wstage_loaded{e % 2}"], 32 * (e // 2 + 1))
                act.copy(wsp[:, e, 0:4:2, :], wstage[:, e % 2, :, :]).then_inc(s["w_high"], 1)
            act.wait_ge(s["alpha_neg"], 1)
            act.activation(aexp, araw, ACT.Exp, bias=aneg, accum_out=asum).then_inc(s["alpha_exped"], 1)

            with act.Fori(0, B) as b:
                for half in range(2):
                    T = b * 2 + half
                    act.wait_ge(s["xl_ready"], T + 1)
                    act.activation(sw[:], xl[:], ACT.Sigmoid, scale=-1.0).then_inc(s["act_step"], 1)
                    act.wait_ge(s["act_step"], T + 1)
                    act.activation(sw[:], sw[:], ACT.Square).then_inc(s["sw_ready"], 1)
                    def std4(which):
                        act.wait_ge(s["var4_ready"], T * 3 + which)
                        act.activation(rs4[:], mv4[:, :, 1], ACT.Sqrt, bias=eps_sb[:, int(which == 1):1 + int(which == 1)])\
                            .then_inc(s["std4_ready"], 1)

                    std4(1)
                    std4(2)
                    act.wait_ge(s["x2T_in_psum"], T + 1)
                    act.copy(x2T[:], PS[:, 7, :]).then_inc(s["x2T_copied"], 1)
                    act.wait_ge(s["ex_shifted"], T + 1)
                    act.activation(ex[:], logit[:], ACT.Exp).then_inc(s["ex_ready"], 1)
                    act.wait_ge(s["cT_in_psum"], T + 1)
                    act.copy(cT_r[:], PS[0:2 * E, 6, :]).then_inc(s["cT_copied"], 1)
                    for k in range(K9):
                        w = k - 1 if k else E
                        if k:
                            act.wait_ge(s["cb_in_psum"], T * E + k)
                            act.wait_ge(s["y_used"], T * K9 + k + 1)
                            act.copy(cb[:, k % 2, :], PS[:, 6, :]).then_inc(s["cb_copied"], 1)
                        for f in range(FC):
                            act.wait_ge(s["h_in_psum"], T * (K9 * FC) + k * FC + f + 1)
                            act.wait_ge(s["split_done"], T * (K9 * FC) + k * FC + f + 1)
                            act.activation(g32[:, f, :], PS[:, f, :], ACT.Gelu, bias=colsT[:, w * FC + f:w * FC + f + 1])\
                                .then_inc(s["gelu_done"], 1)
                    std4(3)

        @block.vector
        def _(dve):
            ds = Chain(dve, s["dve_step"])
            dve.sem_inc(s["split_done"], FC)
            dve.sem_inc(s["y_used"], 2)
            for k, eps in enumerate((EPS, EPS / 4)):
                dve.memset(eps_sb[:, k:k + 1], eps).then_inc(s["eps_made"], 1)
            ds.mark(dve.memset(taps_pad[:], 0.0))
            dve.wait_ge(s["taps_loaded"], 16)
            ds.wait()
            dve.tensor_copy(taps_pad[:, WIN - 1:WIN - 1 + TAPS], taps_sb[:, ::-1]).then_inc(s["taps_padded"], 1)

            norms = [0]

            def layernorm(src, dst, n, ready):
                for t in range(n):
                    ds.mark(dve.bn_stats(stats[:, t, :], src(t)))
                ds.wait()
                for t in range(n):
                    i = dve.bn_aggr(mv[:, t, :], stats[:, t, :])
                i.then_inc(s["var_ready"], 1)
                norms[0] += 1
                dve.wait_ge(s["std_ready"], norms[0])
                ds.done(dve.reciprocal(rstd[:, 0:n], rstd[:, 0:n]))
                for t in range(n):
                    dve.tensor_scalar(dst(t), src(t), mv[:, t, 0:1], rstd[:, t:t + 1], ALU.subtract, ALU.mult)\
                        .then_inc(ready, 1)

            def batch_norm(b):
                dve.wait_ge(s[f"x_loaded{b}"], 16)
                layernorm(lambda t: x[:, b * TB + t, :], lambda t: X[:, b * TB + t, :], TB, s["Xn_ready"])

            def landmark_sums(b):
                dve.wait_ge(s["xT_copied"], 2 * (b + 1))
                dve.reduce_sum(lmT[:, b * LM:(b + 1) * LM],
                               xT[:, b * N:(b + 1) * N].rearrange("p (l m) -> p l m", m=N // LM), AX)\
                    .then_inc(s["lm_summed"], 1)

            for b in range(B):
                batch_norm(b)
                if b:
                    landmark_sums(b - 1)
            landmark_sums(B - 1)
            dve.wait_ge(s["win_loaded"], 48)
            layernorm(lambda t: xw[:, t, :], lambda t: xw[:, t, :], NWIN, s["win_ready"])
            dve.wait_ge(s["ident_made"], 4)
            for k, c in enumerate((7.0, 15.0, 13.0)):
                ds.mark(dve.tensor_scalar(cI[:, k, :], ident[:], c, None, ALU.mult))

            dve.wait_ge(s["lscores_in_psum"], 2)
            ls = PS[:, 0, 0:(G + H) * LM].rearrange("p (a j) -> p a j", j=LM)
            ds.done(dve.reduce_max(mx10, ls, AX))
            dve.tensor_tensor(A2[:], ls, spread(mx10.unsqueeze(2), 2, LM), ALU.subtract).then_inc(s["lscores_read"], 1)
            for g in range(G):
                dve.wait_ge(s["l3_in_psum"], 2 * g + 2)
                ds.done(dve.tensor_reduce(mx3[:, g:g + 1], PS[:, 3 + 2 * g:5 + 2 * g, :].rearrange("p a n -> p (a n)"),
                                          AX, ALU.max))
                dve.tensor_scalar(neg3[:, g:g + 1], mx3[:, g:g + 1], -1.0, None, ALU.mult).then_inc(s["l3_max"], 1)
            dve.wait_ge(s["A2_exped"], 1)
            ds.done(dve.reduce_sum(sum10, A2e[:], AX))
            ds.done(dve.reciprocal(mx10, sum10))
            dve.tensor_tensor(A2[:], A2e[:], spread(mx10.unsqueeze(2), 2, LM), ALU.mult).then_inc(s["A2_ready"], 1)
            dve.wait_ge(s["A2_ready"], 1)
            for g in range(G):
                xb = dve.tensor_tensor(x_bd[:, g, :].rearrange("p (q j) -> p q j", j=LM),
                                       spread(A2[:, g:g + 1, :], 1, P // LM),
                                       blockones[:].rearrange("p (q j) -> p q j", j=LM), ALU.mult)
                xb.then_inc(s["xbd_ready"], 1)
            ds.done(dve.reduce_sum(rsum8, A2[:, G:G + H, :], AX))
            ds.mark(dve.reduce_max(lstat[:, 0:1], rsum8, AX))
            dve.wait_ge(s["colsum_in_psum"], 1)
            ds.done(dve.reduce_max(lstat[:, 1:2], PS[:, 0, 256:512], AX))
            dve.engine_nop().then_inc(s["landstats_ready"], 1)
            dve.wait_ge(s["landstats_max"], 1)
            ds.done(dve.tensor_tensor(sprod, lmax[:, 0:1], lmax[:, 1:2], ALU.mult))
            ds.done(dve.reciprocal(inv_s, sprod))
            dve.wait_ge(s["xbdT_in_psum"], 1)
            xTp = PS[:, 0, 0:256].rearrange("p (g n) -> p g n", g=G)
            dve.tensor_scalar(z[:], xTp, inv_s, None, ALU.mult).then_inc(s["z_ready"], 1)
            dve.tensor_copy(xT_bd[:], xTp).then_inc(s["z_ready"], 1)
            dve.tensor_scalar(zT[:], x_bd[:], inv_s, None, ALU.mult).then_inc(s["z_ready"], 1)

            def l1_shift(n):
                dve.wait_ge(s["l1_in_psum"], n + 1)
                v = PS[:, 3 + n, :].rearrange("p (a j) -> p a j", j=LM)
                ds.done(dve.reduce_max(l1mx[:, 2 + n % 2, :], v, AX))
                dve.tensor_tensor(A1[:, 2 * n:2 * n + 2, :].rearrange("p t (h j) -> p (t h) j", j=LM), v,
                                  spread(l1mx[:, 2 + n % 2, :].unsqueeze(2), 2, LM), ALU.subtract)\
                    .then_inc(s["l1_shifted"], 1)

            def l1_norm(n):
                dve.wait_ge(s["l1_exped"], n + 1)
                v = A1[:, 2 * n:2 * n + 2, :].rearrange("p t (h j) -> p (t h) j", j=LM)
                ds.done(dve.reduce_sum(l1mx[:, 0, :], v, AX))
                ds.done(dve.reciprocal(l1mx[:, 1, :], l1mx[:, 0, :]))
                dve.tensor_tensor(v, v, spread(l1mx[:, 1, :].unsqueeze(2), 2, LM), ALU.mult)\
                    .then_inc(s["l1_ready"], 1)
                dve.wait_ge(s["l1_ready"], n + 1)

            for stage in range(4 * PINV_ITERS):
                it, st = divmod(stage, 4)
                if st < 3:
                    if st == 0:
                        dve.wait_ge(s["pinv_p_in_psum"], it + 1)
                        src = PS[:, 0, 0:256]
                    else:
                        dve.wait_ge(s["pinv_t2_in_psum"], 2 * it + st)
                        src = PS[:, 0, (st % 2) * 256:(st % 2) * 256 + 256]
                    dve.scalar_tensor_tensor(tt[:, st, :, :], src.rearrange("p (g n) -> p g n", g=G), -1.0,
                                             spread(cI[:, st:st + 1, :], 1, G), ALU.mult, ALU.add)\
                        .then_inc(s["pinv_t_ready"], 1)
                else:
                    dve.wait_ge(s["pinv_z_in_psum"], it + 1)
                    dve.tensor_scalar(z[:], PS[:, 0, 256:512].rearrange("p (g n) -> p g n", g=G), 0.25, None, ALU.mult)\
                        .then_inc(s["pinv_z_ready"], 1)
                if stage < 4:
                    l1_shift(stage)
                if stage == 0:
                    dve.wait_ge(s["l3_exped"], G)
                    ds.done(dve.reciprocal(rec3, sum3))
                if 1 <= stage < 5:
                    l1_norm(stage - 1)
            dve.wait_ge(s["u_in_psum"], 1)
            for g in range(G):
                dve.tensor_scalar(U_sb[:, g, :], PS[:, 4, g * P:(g + 1) * P], rec3[:, g:g + 1], None, ALU.mult)\
                    .then_inc(s["u_copied"], 1)
            for c in range(2):
                dve.wait_ge(s["xg_in_psum"], c + 1)
                dve.tensor_scalar(xgT[:, c * 512:(c + 1) * 512], PS[:, 5 + c, :], colsT[:, OUTB:OUTB + 1], None, ALU.add)\
                    .then_inc(s["xgT_ready"], 1)
                dve.wait_ge(s["xgT_ready"], c + 1)
                dve.tensor_tensor(encT[:, c * 512:(c + 1) * 512], xgT[:, c * 512:(c + 1) * 512],
                                  xT[:, c * 512:(c + 1) * 512], ALU.add).then_inc(s["encT_ready"], 1)
            dve.wait_ge(s["edges_loaded"], 48)
            ds.done(dve.tensor_scalar(r_i[:, 0, :], rows_i[:], LOG_N, None, ALU.logical_shift_left))
            dve.tensor_tensor(idx[:], r_i[:, 0, :], cols_i[:], ALU.add).then_inc(s["idx_ready"], 1)
            dve.wait_ge(s["idx_ready"], 1)
            ds.mark(dve.tensor_scalar(r_i[:, 0, :], rows_i[:], P - 1, None, ALU.bitwise_and))
            ds.done(dve.tensor_scalar(r_i[:, 1, :], rows_i[:], P.bit_length() - 1, None, ALU.logical_shift_right))
            ds.done(dve.tensor_copy(r_f[:], r_i[:]))
            dve.wait_ge(s["xgtok_copied"], 2)
            for b in range(B):
                dve.tensor_tensor(X[:, tiles_of(b), :], X[:, tiles_of(b), :], xg[:], ALU.add).then_inc(s["enc_ready"], 1)
            for c in range(NT // CH):
                dve.wait_ge(s["value_in_psum"], c + 1)
                dve.tensor_tensor(value[:, c * CW:(c + 1) * CW].rearrange("p (t d) -> p t d", t=CH),
                                  PS[:, 4 + c % 4, :].rearrange("p (t d) -> p t d", t=CH),
                                  spread(wvb_sb[:].unsqueeze(1), 1, CH), ALU.add).then_inc(s["value_ready"], 1)
            for e in range(K9):
                dve.wait_ge(s["w_high"], e + 1)
                for k in range(2):
                    dve.tensor_tensor(wsp[:, e, 2 * k + 1, :], wstage[:, e % 2, k, :], wsp[:, e, 2 * k, :], ALU.subtract)\
                        .then_inc(s["w_low"], 1)
            dve.wait_ge(s["w_low"], 2 * K9)
            for q in range(4):
                a, b_ = q * EC // 4, (q + 1) * EC // 4
                oh = dve.tensor_tensor(onehot[:, a:b_, :], spread(iota_row[:].unsqueeze(1), 1, EC // 4),
                                       spread(r_f[:, 0, a:b_].unsqueeze(2), 2, P), ALU.is_equal)
                oh.then_inc(s["onehot_ready"], 1)
            ds.done(dve.tensor_tensor(oh8[:], spread(iota_row[:, 0:TB].unsqueeze(1), 1, EC),
                                      spread(r_f[:, 1, :].unsqueeze(2), 2, TB), ALU.is_equal))
            dve.wait_ge(s["gathered_all"], 16 * EC)
            ds.done(dve.tensor_tensor(gathered[:], gathered[:], vals_sb[:], ALU.mult))
            ds.done(dve.tensor_copy(parts[:, 0, :], gathered[:]))
            ds.done(dve.tensor_tensor(rest[:, 0, :], gathered[:], parts[:, 0, :], ALU.subtract))
            ds.done(dve.tensor_copy(parts[:, 1, :], rest[:, 0, :]))
            ds.done(dve.tensor_tensor(rest[:, 1, :], rest[:, 0, :], parts[:, 1, :], ALU.subtract))
            ds.done(dve.tensor_copy(parts[:, 2, :], rest[:, 1, :]))
            for k in range(3):
                dve.tensor_tensor(rhs3[:, :, k, :], oh8[:], spread(parts[:, k, :].unsqueeze(2), 2, TB), ALU.mult)\
                    .then_inc(s["rhs3_ready"], 1)
            dve.wait_ge(s["araw_in_psum"], 1)
            ds.done(dve.reduce_sum(araw, PS[:, 0, 0:3 * TB].rearrange("p (k t) -> p t k", k=3), AX))
            dve.reduce_max(amx, araw, AX).then_inc(s["araw_max"], 1)
            dve.wait_ge(s["araw_maxed"], 1)
            dve.tensor_scalar(aneg, amx_all, -1.0, None, ALU.mult).then_inc(s["alpha_neg"], 1)
            dve.wait_ge(s["alpha_summed"], 1)
            ds.done(dve.reciprocal(arec, asum_all))
            ds.done(dve.tensor_scalar(alpha[:], aexp, arec, None, ALU.mult))

            with dve.Fori(0, B) as b:
                for half in range(2):
                    T = b * 2 + half
                    ln = Drained(dve)
                    ch = slice(half * CH, (half + 1) * CH)
                    val = value[:, bass.ds(T * CW, CW)].rearrange("p (t d) -> p t d", t=CH)
                    enc = X[:, bass.ds(T * CH, CH), :]
                    xin = x[:, bass.ds(T * CH, CH), :]
                    dve.tensor_tensor(xl[:], val, spread(alpha[:, ch].unsqueeze(2), 2, P), ALU.mult)\
                        .then_inc(s["xl_ready"], 1)
                    dve.wait_ge(s["xl_ready"], T + 1)
                    ln.mark(dve.tensor_tensor(yy[:], xl[:], enc, ALU.subtract))
                    ln.wait()
                    dve.wait_ge(s["sw_ready"], T + 1)
                    ln.done(dve.tensor_tensor(yy[:], yy[:], sw[:], ALU.mult))
                    ln.done(dve.tensor_tensor(yy[:], yy[:], enc, ALU.add))

                    def normed(src, dst, which):
                        for t in range(CH):
                            i = dve.bn_stats(st6[:, t, :], src[:, t, :])
                        ln.done(i)
                        for t in range(CH):
                            i = dve.bn_aggr(mv4[:, t, :], st6[:, t, :])
                        i.then_inc(s["var4_ready"], 1)
                        dve.wait_ge(s["std4_ready"], T * 3 + which)
                        ln.done(dve.reciprocal(rs4[:], rs4[:]))
                        for t in range(CH):
                            i = dve.tensor_scalar(dst[:, t, :], src[:, t, :], mv4[:, t, 0:1], rs4[:, t:t + 1],
                                                  ALU.subtract, ALU.mult)
                        return i

                    ln.done(normed(yy, yy, 1))
                    ln.done(dve.tensor_tensor(x1[:], yy[:], xin, ALU.add))
                    normed(x1, yy, 2).then_inc(s["x2_ready"], 1)
                    dve.wait_ge(s["x2T_copied"], T + 1)
                    ln.done(dve.tensor_copy(x2hl[:, 0, :], x2T[:]))
                    dve.tensor_tensor(x2hl[:, 1, :], x2T[:], x2hl[:, 0, :], ALU.subtract).then_inc(s["x2_split"], 1)
                    dve.wait_ge(s["logits_in_psum"], T + 1)
                    ln.done(dve.tensor_copy(logit[:], PS[:, 6, 0:CH * E].rearrange("p (t e) -> p t e", t=CH)))
                    for t in range(CH):
                        i = dve.max(top[:, t, :], logit[:, t, :])
                    ln.done(i)
                    for t in range(CH):
                        i = dve.max_index(topi[:, t, :], top[:, t, :], logit[:, t, :])
                    ln.done(i)
                    ln.mark(dve.tensor_copy(topf[:], topi[:]))
                    dve.tensor_tensor(logit[:], logit[:], spread(top[:, :, 0:1], 2, E), ALU.subtract)\
                        .then_inc(s["ex_shifted"], 1)
                    ln.wait()
                    for k in range(2):
                        i = dve.tensor_tensor(hot[:, k, :, :], spread(iota_row[:, 0:E].unsqueeze(1), 1, CH),
                                              spread(topf[:, :, k:k + 1], 2, E), ALU.is_equal)
                    ln.done(i)
                    ln.done(dve.tensor_tensor(hot[:, 0, :, :], hot[:, 0, :, :], hot[:, 1, :, :], ALU.add))
                    dve.wait_ge(s["ex_ready"], T + 1)
                    ln.done(dve.tensor_tensor(hot[:, 1, :, :], hot[:, 0, :, :], ex[:], ALU.mult))
                    ln.done(dve.reduce_sum(csum[:, 0, :], hot[:, 1, :, :], AX))
                    ln.done(dve.reciprocal(csum[:, 1, :], csum[:, 0, :]))
                    ln.done(dve.tensor_tensor(hot[:, 0, :, :], hot[:, 1, :, :],
                                              spread(csum[:, 1, :].unsqueeze(2), 2, E), ALU.mult))
                    ln.done(dve.tensor_copy(c_r[:], hot[:, 0, :, :]))
                    dve.tensor_copy(c16[:, :, 0:E], c_r[:]).then_inc(s["c16_ready"], 1)
                    dve.tensor_tensor(c16[:, :, E:2 * E], hot[:, 0, :, :], c_r[:], ALU.subtract)\
                        .then_inc(s["c16_ready"], 1)
                    dve.wait_ge(s["cT_in_psum"], T + 1)
                    dve.wait_ge(s["cT_copied"], T + 1)
                    dve.tensor_copy(cT[:], PS[0:2 * E, 6, :]).then_inc(s["cT32_copied"], 1)

                    def reduce_expert(k):
                        dve.wait_ge(s["y_in_psum"], T * K9 + k + 1)
                        y = PS[:, 4 + (k + half) % 2, :]
                        if k == 0:
                            dve.tensor_scalar(acc[:], y, colsT[:, SB2:SB2 + 1], None, ALU.add).then_inc(s["y_used"], 1)
                            dve.wait_ge(s["y_used"], T * K9 + 3)
                        else:
                            dve.wait_ge(s["cb_copied"], T * E + k)
                            dve.tensor_tensor(prod[:], y, cb[:, k % 2, :], ALU.mult).then_inc(s["y_used"], 1)
                            dve.wait_ge(s["y_used"], T * K9 + k + 3)
                            dve.tensor_tensor(acc[:], acc[:], prod[:], ALU.add).then_inc(s["accT_ready"], 1)
                            dve.wait_ge(s["accT_ready"], T * E + k)

                    for k in range(K9):
                        for f in range(FC):
                            n = T * (K9 * FC) + k * FC + f
                            if k >= 2 and f == 0:
                                dve.wait_ge(s["y_in_psum"], T * K9 + k - 1)
                            dve.wait_ge(s["gelu_done"], n + 1)
                            dve.tensor_copy(ghl[:, k % 2, f, 0, :], g32[:, f, :]).then_inc(s["w_low"], 1)
                            dve.wait_ge(s["w_low"], n + 1 + 2 * K9)
                            dve.tensor_tensor(ghl[:, k % 2, f, 1, :], g32[:, f, :], ghl[:, k % 2, f, 0, :], ALU.subtract)\
                                .then_inc(s["split_done"], 1)
                        if k:
                            reduce_expert(k - 1)
                    reduce_expert(K9 - 1)
                    dve.wait_ge(s["accT_in_psum"], T + 1)
                    ln.done(dve.tensor_copy(yy[:], PS[:, 7, :].rearrange("p (t d) -> p t d", t=CH)))
                    ln.done(normed(yy, yy, 3))
                    if True:
                        dve.wait_ge(s["out_stored"], T * 16)
                    dve.tensor_tensor(fin[:], yy[:], x1[:], ALU.add).then_inc(s["fin_ready"], 1)
                    dve.wait_ge(s["fin_ready"], T + 1)

        @block.tensor
        def _(pe):
            pe.wait_ge(s["ident_made"], 1)
            pe.wait_ge(s["rows46_loaded"], 80)
            nrow = K9 * FC + 2 + E
            pe.transpose(PS[:, 7, 0:nrow], rows46[:], ident[0:nrow, 0:nrow]).then_inc(s["cols_in_psum"], 1)
            pe.wait_ge(s["qkvw_loaded"], 16)
            for k in range(3):
                for c in range(4):
                    m = pe.transpose(PS[:, k, c * P:(c + 1) * P], qkvw[:, (4 * k + c) * P:(4 * k + c + 1) * P], ident[:])
                m.then_inc(s["wT_in_psum"], 1)

            def xT_group(g):
                pe.wait_ge(s["Xn_ready"], CH * (g + 1))
                if g >= 4:
                    pe.wait_ge(s["xT_copied"], g - 3)
                for t in range(CH):
                    m = pe.transpose(PS[:, 3 + g % 4, t * P:(t + 1) * P], X[:, g * CH + t, :], ident[:])
                m.then_inc(s["xT_in_psum"], 1)

            xT_group(0)
            xT_group(1)
            pe.wait_ge(s["wo_loaded"], 16)
            pe.wait_ge(s["wT_copied"], 3)
            for h in range(H):
                r = slice(DH * (h % 2), DH * (h % 2) + DH)
                m = pe.matmul(PS[:, h % 2, (h // 2) * P:(h // 2 + 1) * P], wT[r, 2, h // 2, :], wo_sb[r, h // 2, :],
                              start=True, stop=True)
                if h >= H - 2:
                    m.then_inc(s["vo_in_psum"], 1)
            pe.wait_ge(s["band_loaded"], 16)
            pe.wait_ge(s["ident_made"], 5)
            pe.wait_ge(s["cols_copied"], 1)
            for k in range(2):
                pe.matmul(PS[:, (2, 7)[k], 0:4 * WIN], flip[:], band[:, 4 * k:4 * k + 4, :], start=True, stop=True)\
                    .then_inc(s["toep_in_psum"], 1)
            for g in range(2, NT // CH):
                xT_group(g)
            pe.wait_ge(s["lm_summed"], B)
            pe.wait_ge(s["toep_copied"], 2)
            for k in range(2):
                for c in range(4):
                    m = pe.matmul(PS[:, (2, 7)[k], c * P:(c + 1) * P], qkvw[:, (4 * k + c) * P:(4 * k + c + 1) * P],
                                  lmT[:], start=True, stop=True)
                m.then_inc(s["ql_in_psum"], 1)
            pe.wait_ge(s["ql_copied"], 2)
            pe.wait_ge(s["vo_copied"], 2)
            for odd in range(2):
                r = slice(DH * odd, DH * odd + DH)
                for h in range(odd, H, 2):
                    q, c = h % 4, h // 2
                    pe.matmul(PS[q * LM:(q + 1) * LM, 0, (h // 4) * LM:(h // 4 + 1) * LM], qlT[r, c, 0:LM],
                              klT[r, c, 0:LM], start=True, stop=True)
                    for b in range(B):
                        m = pe.matmul(PS[b * LM:(b + 1) * LM, 0, (G + h) * LM:(G + h + 1) * LM],
                                      qlT[r, c, b * LM:(b + 1) * LM], klT[r, c, b * LM:(b + 1) * LM],
                                      start=True, stop=True)
                m.then_inc(s["lscores_in_psum"], 1)
                for k, l in enumerate((klT, qlT)):
                    for h in range(odd, H, 2):
                        m = pe.matmul(PS[:, 1, (k * H + h) * LM:(k * H + h + 1) * LM], wT[r, k, h // 2, :],
                                      l[r, h // 2, 0:LM], start=True, stop=True)
                m.then_inc(s["g_in_psum"], 1)
                if not odd:
                    pe.wait_ge(s["g_in_psum"], 1)
            pe.wait_ge(s["g_copied"], 1)
            pe.wait_ge(s["xT_copied"], NT // CH)
            for g in range(G):
                for c in range(2):
                    pe.matmul(PS[:, 3 + 2 * g + c, :], Gq[:, 1, g * P:(g + 1) * P], xT[:, c * 512:(c + 1) * 512],
                              start=True, stop=True).then_inc(s["l3_in_psum"], 1)
            pe.wait_ge(s["xbd_ready"], G)
            for g in range(G):
                m = pe.transpose(PS[:, 0, g * P:(g + 1) * P], x_bd[:, g, :], ident[:])
            m.then_inc(s["xbdT_in_psum"], 1)
            pe.wait_ge(s["ident_made"], 2)
            pe.wait_ge(s["A2_ready"], 1)
            pe.matmul(PS[:, 0, 256:512], blockones[:], A2[:, G:G + H, :].rearrange("p h j -> p (h j)"),
                      start=True, stop=True).then_inc(s["colsum_in_psum"], 1)

            def conv_step(n):
                w, hh = n // 2, n % 2
                if n == 0:
                    pe.wait_ge(s["win_ready"], NWIN)
                    pe.wait_ge(s["toep_copied"], 2)
                if n >= 2:
                    pe.wait_ge(s["conv_copied"], n - 1)
                pe.matmul(PS[:, (2, 7)[n % 2], 0:4 * WIN], xw[:, w, :], toep[:, 4 * hh:4 * hh + 4, :],
                          start=True, stop=True).then_inc(s["conv_in_psum"], 1)

            def l1_step(n):
                pe.wait_ge(s["l3_exped"], n // 2 + 1)
                for t in range(2):
                    tile = 2 * n + t
                    m = pe.matmul(PS[:, 3 + n, t * 256:(t + 1) * 256], xT[:, tile * P:(tile + 1) * P], Gq[:, 0, :],
                                  start=True, stop=True)
                m.then_inc(s["l1_in_psum"], 1)

            pe.wait_ge(s["z_ready"], 3)
            for stage in range(4 * PINV_ITERS):
                it, st = divmod(stage, 4)
                if st == 0:
                    if it:
                        pe.wait_ge(s["pinv_z_ready"], it)
                        pe.wait_ge(s["zT_copied"], it)
                    for g in range(G):
                        pe.matmul(PS[:, 0, g * P:(g + 1) * P], xT_bd[:, g, :], z[:, g, :], start=True, stop=True)
                    for g in range(G):
                        m = pe.matmul(PS[:, 1, g * P:(g + 1) * P], z[:, g, :], xT_bd[:, g, :],
                                      start=True, stop=True)
                    m.then_inc(s["pinv_p_in_psum"], 1)
                elif st < 3:
                    pe.wait_ge(s["pT_copied"], it + 1)
                    pe.wait_ge(s["pinv_t_ready"], 3 * it + st)
                    for g in range(G):
                        m = pe.matmul(PS[:, 0, (st % 2) * 256 + g * P:(st % 2) * 256 + (g + 1) * P], pT[:, g, :],
                                      tt[:, st - 1, g, :], start=True, stop=True)
                    m.then_inc(s["pinv_t2_in_psum"], 1)
                else:
                    pe.wait_ge(s["pinv_t_ready"], 3 * it + 3)
                    for g in range(G):
                        pe.matmul(PS[:, 0, 256 + g * P:256 + (g + 1) * P], zT[:, g, :], tt[:, 2, g, :], start=True, stop=True)
                    for g in range(G):
                        m = pe.matmul(PS[:, 1, 256 + g * P:256 + (g + 1) * P], tt[:, 2, g, :], zT[:, g, :],
                                      start=True, stop=True)
                    m.then_inc(s["pinv_z_in_psum"], 1)
                if stage < 4:
                    l1_step(stage)
                if stage < CONV:
                    conv_step(stage)
            for n in range(4):
                pe.wait_ge(s["conv_copied"], CONV - 1 + n if n < 2 else CONV)
                if n >= 2:
                    pe.wait_ge(s["e3T_copied"], n - 1)
                for t in range(2):
                    for g in range(G):
                        tile = 2 * n + t
                        m = pe.transpose(PS[:, (2, 7)[n % 2], (2 * t + g) * P:(2 * t + g + 1) * P],
                                         E3[:, g, tile * P:(tile + 1) * P], ident[:])
                m.then_inc(s["e3T_in_psum"], 1)
            for n in range(4):
                pe.wait_ge(s["e3T_copied"], min(n + 3, 4))
                if n >= 2:
                    pe.wait_ge(s["a1T_copied"], n - 1)
                pe.wait_ge(s["l1_ready"], 4)
                g, q = n // 2, n % 2
                for t in range(4):
                    m = pe.transpose(PS[:, (2, 7)[n % 2], t * P:(t + 1) * P], A1[:, 4 * q + t, g * P:(g + 1) * P], ident[:])
                m.then_inc(s["a1T_in_psum"], 1)
            pe.wait_ge(s["e3T_copied"], 4)
            for t in range(TB):
                m = pe.matmul(PS[:, 3, 0:G * P], X[:, t, :], E3T[:, t, :], start=(t == 0), stop=(t == TB - 1))
            m.then_inc(s["tT_in_psum"], 1)
            for c in range(2):
                for h in range(H):
                    pe.matmul(PS[:, 5 + c, :], VO[:, h, :], YT[:, h, c * 512:(c + 1) * 512], start=(h == 0), stop=False)
            pe.wait_ge(s["tT_copied"], 1)
            for h in range(H):
                q = h % 4
                m = pe.matmul(PS[q * LM:(q + 1) * LM, 4, (h // 4) * P:(h // 4 + 1) * P], TT_sb[:, h * LM:(h + 1) * LM],
                              VO[:, h, :], start=True, stop=True)
            m.then_inc(s["u_in_psum"], 1)
            pe.wait_ge(s["u_copied"], G)
            pe.wait_ge(s["zT_copied"], PINV_ITERS)
            for g in range(G):
                m = pe.matmul(PS[:, 3, g * P:(g + 1) * P], zT[:, g, :], U_sb[:, g, :], start=True, stop=True)
            m.then_inc(s["n_in_psum"], 1)
            pe.wait_ge(s["n_copied"], 1)
            pe.wait_ge(s["a1T_copied"], 4)
            for c in range(2):
                for g in range(G):
                    m = pe.matmul(PS[:, 5 + c, :], N_sb[:, g, :], A1T[:, g, c * 512:(c + 1) * 512], start=False,
                                  stop=(g == G - 1))
                m.then_inc(s["xg_in_psum"], 1)
            pe.wait_ge(s["small_loaded"], 64)
            for k in range(2):
                for c in range(2):
                    pe.wait_ge(s["encT_ready"], c + 1)
                    pe.matmul(PS[0:QK, 2 * k + c, :], wqk_sb[:, k, :], encT[:, c * 512:(c + 1) * 512],
                              start=True, stop=True).then_inc(s["qk_in_psum"], 1)
            pe.wait_ge(s["qk_copied"], 4)
            for n in range(NPIECE):
                r, c = n // 2, n % 2
                if n >= 4:
                    pe.wait_ge(s["scores_copied"], n - 3)
                pe.matmul(PS[:, 4 + n % 4, :], qkT[:, 0, r * P:(r + 1) * P], qkT[:, 1, c * 512:(c + 1) * 512],
                          start=True, stop=True).then_inc(s["scores_in_psum"], 1)
            for n in range(2):
                for t in range(4):
                    m = pe.transpose(PS[:, n, t * P:(t + 1) * P], xgT[:, (4 * n + t) * P:(4 * n + t + 1) * P], ident[:])
                m.then_inc(s["xgtok_in_psum"], 1)
            for c in range(NT // CH):
                pe.wait_ge(s["scores_copied"], NPIECE)
                if c >= 4:
                    pe.wait_ge(s["value_ready"], c - 3)
                for t in range(CH):
                    tile = c * CH + t
                    m = pe.matmul(PS[:, 4 + c % 4, t * P:(t + 1) * P], xT[:, tile * P:(tile + 1) * P], wv_sb[:],
                                  start=True, stop=True)
                m.then_inc(s["value_in_psum"], 1)
            pe.wait_ge(s["onehot_ready"], 4)
            pe.wait_ge(s["rhs3_ready"], 3)
            pe.wait_ge(s["xgtok_copied"], 2)
            for j in range(EC):
                m = pe.matmul(PS[:, 0, 0:3 * TB], onehot[:, j, :], rhs3[:, j, :, :].rearrange("p k t -> p (k t)"),
                              start=(j == 0), stop=(j == EC - 1))
            m.then_inc(s["araw_in_psum"], 1)
            pe.wait_ge(s["b2_loaded"], 32)
            pe.wait_ge(s["ident_made"], 4)

            with pe.Fori(0, B) as b:
                for half in range(2):
                    T = b * 2 + half
                    pe.wait_ge(s["x2_ready"], T + 1)
                    for t in range(CH):
                        m = pe.transpose(PS[:, 7, t * P:(t + 1) * P], yy[:, t, :], ident[:])
                    m.then_inc(s["x2T_in_psum"], 1)
                    pe.wait_ge(s["x2T_copied"], T + 1)
                    for t in range(CH):
                        m = pe.matmul(PS[:, 6, t * E:(t + 1) * E], x2T[:, t * P:(t + 1) * P], colsT[:, GATE:GATE + E],
                                      start=True, stop=True)
                    m.then_inc(s["logits_in_psum"], 1)
                    pe.wait_ge(s["c16_ready"], 2 * T + 2)
                    for t in range(CH):
                        m = pe.transpose(PS[0:2 * E, 6, t * P:(t + 1) * P], c16[:, t, :], ident[:])
                    m.then_inc(s["cT_in_psum"], 1)
                    pe.wait_ge(s["cT32_copied"], T + 1)
                    pe.wait_ge(s["x2_split"], T + 1)

                    def up(k):
                        w = k - 1 if k else E
                        for f in range(FC):
                            n = T * (K9 * FC) + k * FC + f
                            pe.wait_ge(s["split_done"], n + 1)
                            cols_ = slice(f * P, (f + 1) * P)
                            pe.matmul(PS[:, f, :], wsp[:, w, 0, cols_], x2hl[:, 0, :], start=True, stop=False)
                            pe.matmul(PS[:, f, :], wsp[:, w, 0, cols_], x2hl[:, 1, :], start=False, stop=False)
                            pe.matmul(PS[:, f, :], wsp[:, w, 1, cols_], x2hl[:, 0, :], start=False, stop=True)\
                                .then_inc(s["h_in_psum"], 1)

                    def down(k):
                        w = k - 1 if k else E
                        bank = PS[:, 4 + (k + half) % 2, :]
                        pe.wait_ge(s["y_used"], T * K9 + k + 1)
                        for f in range(FC):
                            pe.wait_ge(s["split_done"], T * (K9 * FC) + k * FC + f + 1 + FC)
                            cols_ = slice(f * P, (f + 1) * P)
                            pe.matmul(bank, wsp[:, w, 2, cols_], ghl[:, k % 2, f, 0, :], start=(f == 0), stop=False)
                            pe.matmul(bank, wsp[:, w, 2, cols_], ghl[:, k % 2, f, 1, :], start=False, stop=False)
                            m = pe.matmul(bank, wsp[:, w, 3, cols_], ghl[:, k % 2, f, 0, :], start=False,
                                          stop=(f == FC - 1 and k > 0))
                        if k == 0:
                            m = pe.matmul(bank, b2_sb[:], cT[:], start=False, stop=True)
                        m.then_inc(s["y_in_psum"], 1)

                    for k in range(K9):
                        if k:
                            if k > 1:
                                pe.wait_ge(s["cb_copied"], T * E + k - 1)
                            pe.matmul(PS[:, 6, :], sel_r[:, k - 1, :], cT_r[:], start=True, stop=True)\
                                .then_inc(s["cb_in_psum"], 1)
                        up(k)
                        if k:
                            down(k - 1)
                    down(K9 - 1)
                    pe.wait_ge(s["accT_ready"], T * E + E)
                    for t in range(CH):
                        m = pe.transpose(PS[:, 7, t * P:(t + 1) * P], acc[:, t * P:(t + 1) * P], ident[:])
                    m.then_inc(s["accT_in_psum"], 1)


_INS = ['L0_attn_dense', 'L0_attn_adj_rows', 'L0_attn_adj_cols', 'L0_attn_adj_vals', 'L0_attn_wq', 'L0_attn_wk',
        'L0_attn_wv_w', 'L0_attn_wv_b', 'L0_attn_qkv_w', 'L0_attn_out_w', 'L0_attn_out_b', 'L0_attn_conv_w',
        'L0_ffn_gate_w', 'L0_ffn_W1', 'L0_ffn_b1', 'L0_ffn_W2', 'L0_ffn_b2', 'L0_ffn_sW1', 'L0_ffn_sb1',
        'L0_ffn_sW2', 'L0_ffn_sb2']


def kernel(**inputs):
    import numpy as _np
    import concourse.bacc as _bacc
    from concourse import mybir as _mybir
    from concourse.bass_utils import run_bass_kernel_spmd as _run

    nc = _bacc.Bacc("TRN2", target_bir_lowering=False, num_devices=1)
    arrays, args = {}, []
    for name in _INS:
        a = _np.ascontiguousarray(inputs[name])
        arrays[f"in_{name}_dram"] = a
        args.append(nc.dram_tensor(f"in_{name}_dram", a.shape, _mybir.dt.from_np(a.dtype), kind="ExternalInput").ap())
    shape = inputs['L0_attn_dense'].shape
    args.append(nc.dram_tensor("out_0_dram", shape, _mybir.dt.float32, kind="ExternalOutput").ap())
    sandwich_kernel(nc, *args)
    r = _run(nc, [arrays], core_ids=[0])
    return r.results[0]["out_0_dram"]
```

```python
from contextlib import ExitStack

import concourse.bass as bass
from concourse import mybir

ALU = mybir.AluOpType
ACT = mybir.ActivationFunctionType
AX = mybir.AxisListType.X
RED = bass.bass_isa.ReduceOp
F32, F32R, BF16 = mybir.dt.float32, mybir.dt.float32r, mybir.dt.bfloat16
I32, U32 = mybir.dt.int32, mybir.dt.uint32

P = 128
EPS = 1e-5
LANDMARKS, PINV_ITERS, HEADS = 32, 6, 8


def spread(ap, axis, n):
    shape = list(ap.shape)
    shape[axis] = n
    return ap.broadcast_to(shape)


class Chain:

    def __init__(self, eng, sem, base=0):
        self.eng, self.sem, self.base, self.n = eng, sem, base, 0

    def mark(self, ins):
        self.n += 1
        return ins.then_inc(self.sem, 1)

    def wait(self):
        self.eng.wait_ge(self.sem, self.base + self.n)

    def done(self, ins):
        self.mark(ins)
        self.wait()


class Drained:

    def __init__(self, eng):
        self.eng = eng

    def mark(self, ins):
        return ins

    def wait(self):
        self.eng.drain()

    def done(self, ins):
        self.eng.drain()


def after(eng, sem, value):
    if not isinstance(value, int) or value > 0:
        eng.wait_ge(sem, value)


def over_chunks(eng, chunks, body):
    body(0, 0, True, False)
    with eng.Fori(0, (chunks - 2) // 2) as i:
        body(i * 2 + 1, 1, False, False)
        body(i * 2 + 2, 0, False, False)
    body(chunks - 1, 1, False, True)


def sandwich_kernel(nc, dense, rows, cols, vals, wq, wk, wv_w, wv_b, qkv_w, out_w, out_b, conv_w,
                    gate_w, W1, b1, W2, b2, sW1, sb1, sW2, sb2, out):
    B, N, D = dense.shape
    QK = wq.shape[1]
    E, _, F = W1.shape
    H, TAPS = HEADS, conv_w.shape[2]
    DH = qkv_w.shape[1] // 3 // H
    LM = LANDMARKS
    TB = N // P
    NT = B * TB
    FC = F // P
    K9 = E + 1
    CH = 4
    CW = CH * P
    WIN = P - (TAPS - 1)
    NWIN = -(-N // WIN)
    PAD = (TAPS - 1) // 2
    EC = rows.shape[0] // P
    G = H * LM // P
    assert D == P and DH == 64 and LM == 32 and G == 2 and F == CW and B * LM == P and H == 8
    LOG_N = N.bit_length() - 1
    assert N == 1 << LOG_N

    scores_dram = nc.dram_tensor("scores", (N * N, 1), F32)
    taps_dram = nc.dram_tensor("taps", (H, WIN + P - 1), F32)
    NTAP = WIN + P - 1

    with ExitStack() as ctx:
        end = [16512]

        def at(name, shape, dt, offset=None):
            size = 4 if dt != BF16 else 2
            for n in shape[1:]:
                size *= n
            o = end[0] if offset is None else offset
            t = nc.alloc_sbuf_tensor_at(name, shape, dt, offset=o)
            o += -(-size // 32) * 32
            if offset is None:
                end[0] = o
            return t, o

        def own(name, shape, dt):
            return at(name, shape, dt)[0]

        x = own("x", [P, NT, P], F32)
        X = own("X", [P, NT, P], F32)
        xT = own("xT", [P, NT * P], F32)
        value = xT
        xg_at = end[0]
        xg = own("xg", [P, TB, P], F32)
        ident = own("ident", [P, P], F32)
        blockones = own("blockones", [P, P], F32)
        iota_row = own("iota_row", [P, P], F32)
        small = own("small", [P, 64], F32)
        colsT = own("colsT", [P, K9 * FC + 2 + 2 * E], F32)
        wv_sb = own("wv_sb", [P, P], F32)
        wvb_sb = own("wvb_sb", [P, P], F32)
        wqk_sb = own("wqk_sb", [P, 2, QK], F32)
        alpha = own("alpha", [P, TB], F32)
        sel_r = own("sel_r", [2 * E, E, P], F32R)
        eps_sb = own("eps_sb", [P, 2], F32)
        OUTB, SB2, GATE, B2 = K9 * FC, K9 * FC + 1, K9 * FC + 2, K9 * FC + 2 + E
        NCOL = B2 + E

        base1 = end[0]
        wsp, end1 = at("wsp", [P, K9, 4, F], F32R, base1)
        end[0] = end1
        o = base1
        YT, o = at("YT", [P, H, NWIN * WIN], F32, o)
        A1, o = at("A1", [P, TB, H * LM], F32, o)
        A1T, o = at("A1T", [P, G, N], F32, o)
        E3, o = at("E3", [P, G, N], F32, o)
        E3T, o = at("E3T", [P, TB, G * P], F32, o)
        assert o <= end1
        base2 = end1
        o = base2
        qkvw, o = at("qkvw", [P, 3 * H * DH], F32, o)
        wT, o = at("wT", [P, 3, 4, P], F32, o)
        wo_sb, o = at("wo_sb", [P, 4, P], F32, o)
        VO, o = at("VO", [P, H, P], F32, o)
        toep, o = at("toep", [P, H, WIN], F32, o)
        band, _ = at("band", [P, H, WIN], F32, base1)
        flip, _ = at("flip", [P, P], F32, base1 + 4 * H * WIN)
        xw, o = at("xw", [P, NWIN, P], F32, o)
        qkT, o = at("qkT", [QK, 2, N], F32, o)
        xgT, o = at("xgT", [P, N], F32, o)
        encT, o = at("encT", [P, N], F32, o)
        taps_sb, o = at("taps_sb", [H, TAPS], F32, o)
        taps_pad, o = at("taps_pad", [H, NTAP], F32, o)
        rows_in, o = at("rows_in", [NCOL, P], F32, o)
        stats, o = at("stats", [P, 12, 6], F32, o)
        mv, o = at("mv", [P, 12, 2], F32, o)
        rstd, o = at("rstd", [P, 12], F32, o)
        lmT, o = at("lmT", [P, B * LM], F32, o)
        qlT, o = at("qlT", [P, 4, P], F32, o)
        klT, o = at("klT", [P, 4, P], F32, o)
        Gq, o = at("Gq", [P, 2, H * LM], F32, o)
        A2, o = at("A2", [P, G + H, LM], F32, o)
        A2e, o = at("A2e", [P, G + H, LM], F32, o)
        x_bd, o = at("x_bd", [P, G, P], F32, o)
        xT_bd, o = at("xT_bd", [P, G, P], F32, o)
        z, o = at("z", [P, G, P], F32, o)
        zT, o = at("zT", [P, G, P], F32, o)
        pT, o = at("pT", [P, G, P], F32, o)
        tt, o = at("tt", [P, 3, G, P], F32, o)
        cI, o = at("cI", [P, 3, P], F32, o)
        TT_sb, o = at("TT_sb", [P, G * P], F32, o)
        U_sb, o = at("U_sb", [P, G, P], F32, o)
        N_sb, o = at("N_sb", [P, G, P], F32, o)
        l1mx, o = at("l1mx", [P, 4, 2 * H], F32, o)
        end_attention = o
        dstage, o = at("dstage", [P, 2, N], F32, base2)
        assert o <= base2 + 4 * (3 * H * DH * 2 + 4 * P), "the stage must end before VO"
        o = end_attention
        idx, o = at("idx", [P, EC], I32, o)
        gathered, o = at("gathered", [P, EC], F32, o)
        vals_sb, o = at("vals_sb", [P, EC], F32, o)
        rows_i, o = at("rows_i", [P, EC], I32, o)
        cols_i, o = at("cols_i", [P, EC], I32, o)
        r_i, o = at("r_i", [P, 2, EC], I32, o)
        r_f, o = at("r_f", [P, 2, EC], F32, o)
        rest, o = at("rest", [P, 2, EC], F32, o)
        parts, o = at("parts", [P, 3, EC], BF16, o)
        assert o <= 229344, o
        o = base2 + 18432
        wstage, o = at("wstage", [P, 2, 2, F], F32, o)
        onehot, o = at("onehot", [P, EC, P], BF16, end1)
        oh8, o2 = at("oh8", [P, EC, TB], BF16, end1 + 2 * EC * P)
        rhs3, o2 = at("rhs3", [P, EC, 3, TB], BF16, o2)
        o = base2
        g32, o = at("g32", [P, FC, CW], F32, o)
        ghl, o = at("ghl", [P, 2, FC, 2, CW], F32R, o)
        x2hl, o = at("x2hl", [P, 2, 2, CW], F32R, o)
        x2T, o = at("x2T", [P, CW], F32, o)
        cb, o = at("cb", [P, 2, CW], F32, o)
        acc, o = at("acc", [P, CW], F32, o)
        prod, _ = at("prod", [P, 2, CW], F32, xg_at)
        x1, o = at("x1", [P, 2, CH, P], F32, o)
        xl, o = at("xl", [P, CH, P], F32, o)
        sw, o = at("sw", [P, CH, P], F32, o)
        yy, o = at("yy", [P, CH, P], F32, o)
        fin, o = at("fin", [P, CH, P], F32, o)
        st6, o = at("st6", [P, CH, 6], F32, o)
        mv4, o = at("mv4", [P, 2 * CH, 2], F32, o)
        newton, o = at("newton", [P, 4, 2 * CH], F32, o)
        guess, o = at("guess", [P, 2 * CH], I32, o)
        logit, o = at("logit", [P, CH, E], F32, o)
        top, o = at("top", [P, CH, 8], F32, o)
        topi, o = at("topi", [P, CH, 8], U32, o)
        topf, o = at("topf", [P, CH, 8], F32, o)
        gap, o = at("gap", [P, CH], F32, o)
        share, o = at("share", [P, 3, CH], F32, o)
        hot, o = at("hot", [P, 2, CH, E], F32, o)
        comb, o = at("comb", [P, CH, E], F32, o)
        c16, o = at("c16", [P, CH, 2 * E], F32R, o)
        cT_r, o = at("cT_r", [2 * E, 2, CW], F32R, o)
        assert o <= 229344, o

        PS = ctx.enter_context(nc.psum_tensor("PS", [P, 8, 512], F32))

        names = """x_loaded0 x_loaded1 x_loaded2 x_loaded3 win_zeroed win_loaded qkvw_loaded wo_loaded taps_loaded rows_in_loaded edges_loaded
            small_loaded taps_padded taps_stored band_loaded toep_in_psum toep_copied ident_made pool_step dve_step act_step
            cI_made Xn_ready win_ready xT_in_psum xT_copied cols_in_psum cols_copied wT_in_psum wT_copied
            vo_in_psum vo_copied lm_summed ql_in_psum ql_copied lscores_in_psum lscores_read A2_exped A2_ready
            xbd_ready xbdT_in_psum colsum_in_psum landstats_ready landstats_max z_ready g_in_psum g_copied
            l3_in_psum l3_max l3_exped l1_in_psum l1_shifted l1_exped l1_ready conv_in_psum conv_copied
            e3T_in_psum e3T_copied a1T_in_psum a1T_copied tT_in_psum tT_copied u_in_psum u_copied
            pinv_p_in_psum pT_copied pinv_t_ready pinv_t2_in_psum pinv_z_in_psum pinv_z_ready zT_copied
            n_in_psum n_copied xg_in_psum xgT_ready encT_ready qk_in_psum qk_copied scores_in_psum
            scores_copied scores_stored0 scores_stored1 xgtok_in_psum xgtok_copied idx_ready gathered_all onehot_ready
            rhs3_ready araw_in_psum araw_max araw_maxed alpha_neg alpha_exped alpha_summed alpha_ready
            value_in_psum value_ready enc_ready wstage_loaded0 wstage_loaded1 w_high w_low
            xl_ready th_done sw_ready mixed mix_normed x1_ready fin_normed x2_ready x2T_in_psum x2T_copied x2_split logits_in_psum gap_ready share_ready
            c16_ready cT_in_psum cT_copied h_in_psum gelu_done0 gelu_done1 gelu_done2 gelu_done3
            high_done0 high_done1 high_done2 high_done3 low_done0 low_done1 low_done2 low_done3 cb_in_psum cb_copied
            y_in_psum y_used prod_added acc_ready accT_in_psum fin_ready out_stored var_ready std_ready eps_made""".split()
        s = {n: ctx.enter_context(nc.semaphore(n)) for n in names}
        half_sb = eps_sb[:, 1:2]

        def step(T, k):
            return T * K9 + k

        HIGH_BY_ACT = 2
        LOW_BY_POOL = 2
        mx3, neg3, sum3, rec3 = small[:, 0:2], small[:, 2:4], small[:, 4:6], small[:, 6:8]
        mx10, sum10 = small[:, 8:18], small[:, 18:28]
        lstat, lmax, inv_s, sprod = small[:, 28:30], small[:, 30:32], small[:, 32:33], small[:, 33:34]
        araw, amx, amx_all, aneg, aexp = (small[:, 34:42], small[:, 42:43], small[:, 43:44], small[:, 44:45],
                                          small[:, 45:53])
        asum, asum_all, arec, rsum8 = small[:, 53:54], small[:, 54:55], small[:, 55:56], small[:, 56:64]

        NPIECE = 2 * TB
        block = ctx.enter_context(nc.Block())

        def tiles_of(b):
            return slice(b * TB, (b + 1) * TB)

        @block.sync
        def _(sp):
            sp.dma_start(x[:, tiles_of(0), :], dense[0].rearrange("(t p) d -> p t d", p=P)).then_inc(s["x_loaded0"], 16)
            sp.wait_ge(s["win_zeroed"], 2)
            sp.dma_start(xw[PAD:P, 0, :], dense[0, 0:P - PAD, :]).then_inc(s["win_loaded"], 16)
            inner = bass.AP(dense.tensor, dense.offset + (WIN - PAD) * D, [[D, P], [WIN * D, NWIN - 2], [1, D]])
            sp.dma_start(xw[:, 1:NWIN - 1, :], inner).then_inc(s["win_loaded"], 16)
            last = N - ((NWIN - 1) * WIN - PAD)
            sp.dma_start(xw[0:last, NWIN - 1, :], dense[0, N - last:N, :]).then_inc(s["win_loaded"], 16)
            for b in range(1, B):
                sp.dma_start(x[:, tiles_of(b), :], dense[b].rearrange("(t p) d -> p t d", p=P))\
                    .then_inc(s[f"x_loaded{b}"], 16)
            sp.wait_ge(s["taps_padded"], 1)
            sp.dma_start(taps_dram[:, :], taps_pad[:]).then_inc(s["taps_stored"], 16)
            sp.wait_ge(s["taps_stored"], 16)
            sp.dma_start(band[:], bass.AP(taps_dram, 0, [[1, P], [NTAP, H], [1, WIN]]))\
                .then_inc(s["band_loaded"], 16)
            for dst, src in ((rows_i, rows), (cols_i, cols), (vals_sb, vals)):
                sp.dma_start(dst[:], src.rearrange("(p j) -> p j", p=P)).then_inc(s["edges_loaded"], 16)
            for r in range(TB):
                sp.wait_ge(s["scores_copied"], 2 * r + 2)
                sp.dma_start(bass.AP(scores_dram, r * P * N, [[N, P], [1, N]]), dstage[:, r % 2, :])\
                    .then_inc(s[f"scores_stored{r % 2}"], 16)
            for e in range(K9):
                w1 = W1[e] if e < E else sW1
                w2 = W2[e] if e < E else sW2
                if e >= 2:
                    sp.wait_ge(s["w_low"], 2 * (e - 1))
                else:
                    sp.wait_ge(s["xgtok_copied"], 2)
                    sp.wait_ge(s["scores_copied"], NPIECE)
                sp.dma_start(wstage[:, e % 2, 0, :], w1).then_inc(s[f"wstage_loaded{e % 2}"], 16)
                sp.dma_start(wstage[:, e % 2, 1, :].rearrange("p (c h) -> p c h", c=FC),
                             w2.rearrange("(c p) h -> p c h", p=P)).then_inc(s[f"wstage_loaded{e % 2}"], 16)
            with sp.Fori(0, B) as b:
                for half in range(2):
                    T = b * 2 + half
                    sp.wait_ge(s["fin_ready"], T + 1)
                    sp.dma_start(out[bass.ds(b, 1), half * CW:(half + 1) * CW, :].rearrange("b (t p) d -> p (b t) d", p=P),
                                 fin[:]).then_inc(s["out_stored"], 16)
            sp.wait_ge(s["out_stored"], 16 * NT // CH)

        @block.gpsimd
        def _(pool):
            ps = Chain(pool, s["pool_step"])
            ps.mark(pool.memset(ident[:], 0.0))
            ps.mark(pool.memset(blockones[:], 0.0))
            pool.memset(xw[:, 0, :], 0.0).then_inc(s["win_zeroed"], 1)
            pool.memset(xw[:, NWIN - 1, :], 0.0).then_inc(s["win_zeroed"], 1)
            ps.wait()
            pool.affine_select(out=ident[:], in_=ident[:], compare_op=ALU.not_equal, fill=1.0, base=0,
                               pattern=[[-1, P]], channel_multiplier=1).then_inc(s["ident_made"], 1)
            pool.wait_ge(s["win_zeroed"], 2)
            pool.wait_ge(s["ident_made"], 1)
            for q in range(P // LM):
                ps.done(pool.memset(blockones[q * LM:(q + 1) * LM, q * LM:(q + 1) * LM], 1.0))
            pool.drain().then_inc(s["ident_made"], 1)
            pool.iota(iota_row[:], pattern=[[1, P]], base=0, channel_multiplier=0,
                      allow_small_or_imprecise_dtypes=True).then_inc(s["ident_made"], 1)
            pool.wait_ge(s["ident_made"], 3)
            selw = E3[0:2 * E, 0, :].rearrange("k (e p) -> k e p", e=E)
            ps.done(pool.memset(selw, 0.0))
            for base in (0, -E):
                ps.done(pool.affine_select(out=selw, in_=selw, compare_op=ALU.not_equal, fill=1.0, base=base,
                                           pattern=[[-1, E], [0, P]], channel_multiplier=1))
            pool.tensor_copy(sel_r[:], selw).then_inc(s["ident_made"], 1)
            ps.done(pool.memset(flip[:], 0.0))
            pool.affine_select(out=flip[:], in_=flip[:], compare_op=ALU.not_equal, fill=1.0, base=1 - P,
                               pattern=[[1, P]], channel_multiplier=1).then_inc(s["ident_made"], 1)
            pool.wait_ge(s["landstats_ready"], 1)
            pool.partition_all_reduce(lmax, lstat, P, RED.max).then_inc(s["landstats_max"], 1)
            pool.wait_ge(s["idx_ready"], 1)
            for k in range(2):
                pool.wait_ge(s[f"scores_stored{k}"], 16 * TB // 2)
            table = scores_dram.ap()
            for j in range(EC):
                pool.indirect_dma_start(gathered[:, j:j + 1], None, table,
                                        bass.IndirectOffsetOnAxis(ap=idx[:, j:j + 1], axis=0))\
                    .then_inc(s["gathered_all"], 16)
            pool.wait_ge(s["araw_max"], 1)
            pool.partition_all_reduce(amx_all, amx, P, RED.max).then_inc(s["araw_maxed"], 1)
            pool.wait_ge(s["alpha_exped"], 1)
            pool.partition_all_reduce(asum_all, asum, P, RED.add).then_inc(s["alpha_summed"], 1)

            def weigh(T, slot):
                val = value[:, bass.ds(T * CW, CW)].rearrange("p (t d) -> p t d", t=CH)
                pool.tensor_tensor(xl[:], val, spread(alpha[:, slot * CH:(slot + 1) * CH].unsqueeze(2), 2, P), ALU.mult)\
                    .then_inc(s["xl_ready"], 1)

            def mix(T):
                enc = X[:, bass.ds(T * CH, CH), :]
                pool.drain()
                pool.tensor_tensor(yy[:], xl[:], enc, ALU.subtract)
                pool.drain()
                pool.wait_ge(s["sw_ready"], T + 1)
                pool.tensor_tensor(yy[:], yy[:], sw[:], ALU.mult)
                pool.drain()
                pool.tensor_tensor(yy[:], yy[:], enc, ALU.add).then_inc(s["mixed"], 1)

            def residual(T, slot):
                pool.drain()
                pool.tensor_tensor(x1[:, slot, :, :], yy[:], x[:, bass.ds(T * CH, CH), :], ALU.add)\
                    .then_inc(s["x1_ready"], 1)

            def last_residual(T, slot):
                pool.wait_ge(s["fin_normed"], T + 1)
                pool.tensor_tensor(fin[:], fin[:], x1[:, slot, :, :], ALU.add).then_inc(s["fin_ready"], 1)

            def expert_steps(T, slot, first, last):
                for k in range(K9):
                    m = step(T, k)
                    if k == 4 and not last:
                        pool.wait_ge(s["mix_normed"], T + 2)
                    for f in range(LOW_BY_POOL):
                        pool.wait_ge(s[f"high_done{f}"], m + 1)
                        pool.tensor_tensor(ghl[:, (slot + k) % 2, f, 1, :], g32[:, f, :], ghl[:, (slot + k) % 2, f, 0, :],
                                           ALU.subtract).then_inc(s[f"low_done{f}"], 1)
                    if k >= 2:
                        add_expert(T, k - 1)
                    if k == 4 and not first:
                        last_residual(T - 1, 1 - slot)
                    if not last:
                        if k == 0:
                            weigh(T + 1, 1 - slot)
                        if k == 1:
                            mix(T + 1)
                        if k == 4:
                            residual(T + 1, 1 - slot)
                add_expert(T, K9 - 1)

            def add_expert(T, k):
                pool.wait_ge(s["y_used"], step(T, k) + 1)
                after(pool, s["prod_added"], T * E + k - 1)
                pool.tensor_tensor(acc[:], acc[:], prod[:, k % 2, :], ALU.add).then_inc(s["prod_added"], 1)

            pool.wait_ge(s["alpha_ready"], 1)
            pool.wait_ge(s["value_ready"], NT // CH)
            pool.wait_ge(s["enc_ready"], B)
            weigh(0, 0)
            mix(0)
            pool.wait_ge(s["mix_normed"], 1)
            residual(0, 0)
            over_chunks(pool, NT // CH, expert_steps)
            last_residual(NT // CH - 1, 1)

        CONV = 2 * NWIN

        @block.scalar
        def _(act):
            act.dma_start(qkvw[:], qkv_w).then_inc(s["qkvw_loaded"], 16)
            act.dma_start(rows_in[0:E * FC, :], b1.rearrange("e (c p) -> (e c) p", p=P)).then_inc(s["rows_in_loaded"], 16)
            act.dma_start(rows_in[E * FC:K9 * FC, :], sb1.rearrange("(c p) -> c p", p=P)).then_inc(s["rows_in_loaded"], 16)
            act.dma_start(rows_in[OUTB:OUTB + 1, :], out_b.rearrange("(a p) -> a p", a=1)).then_inc(s["rows_in_loaded"], 16)
            act.dma_start(rows_in[SB2:SB2 + 1, :], sb2.rearrange("(a p) -> a p", a=1)).then_inc(s["rows_in_loaded"], 16)
            act.dma_start(rows_in[GATE:GATE + E, :], gate_w).then_inc(s["rows_in_loaded"], 16)
            act.dma_start(rows_in[B2:B2 + E, :], b2).then_inc(s["rows_in_loaded"], 16)
            act.dma_start(taps_sb[:], conv_w[:, 0, :, 0]).then_inc(s["taps_loaded"], 16)
            act.dma_start(wo_sb[:], out_w.rearrange("(c p) n -> p c n", p=P)).then_inc(s["wo_loaded"], 16)
            act.dma_start(wqk_sb[:, 0, :], wq).then_inc(s["small_loaded"], 16)
            act.dma_start(wqk_sb[:, 1, :], wk).then_inc(s["small_loaded"], 16)
            act.dma_start(wv_sb[:], wv_w).then_inc(s["small_loaded"], 16)
            act.dma_start(wvb_sb[:], wv_b.partition_broadcast(P)).then_inc(s["small_loaded"], 16)

            def std(k, n):
                act.wait_ge(s["var_ready"], k + 1)
                act.activation(rstd[:, 0:n], mv[:, 0:n, 1], ACT.Sqrt, bias=eps_sb[:, 0:1]).then_inc(s["std_ready"], 1)

            act.wait_ge(s["eps_made"], 2)
            std(0, TB)
            act.wait_ge(s["cols_in_psum"], 1)
            act.copy(colsT[:], PS[:, 7, 0:NCOL]).then_inc(s["cols_copied"], 1)
            for k in range(3):
                act.wait_ge(s["wT_in_psum"], k + 1)
                act.copy(wT[:, k, :, :], PS[:, k, :].rearrange("p (c n) -> p c n", c=4)).then_inc(s["wT_copied"], 1)

            def xT_copy(g):
                act.wait_ge(s["xT_in_psum"], g + 1)
                act.copy(xT[:, g * CW:(g + 1) * CW], PS[:, 3 + g % 4, :]).then_inc(s["xT_copied"], 1)

            xT_copy(0)
            xT_copy(1)
            std(1, TB)
            for k in range(2):
                act.wait_ge(s["vo_in_psum"], k + 1)
                act.copy(VO[:, k:H:2, :], PS[:, k, :].rearrange("p (c n) -> p c n", c=4))\
                    .then_inc(s["vo_copied"], 1)
            for k in range(2):
                act.wait_ge(s["toep_in_psum"], k + 1)
                act.copy(toep[:, 4 * k:4 * k + 4, :], PS[:, (2, 7)[k], 0:4 * WIN].rearrange("p (h m) -> p h m", h=4))\
                    .then_inc(s["toep_copied"], 1)
            for g in range(2, NT // CH):
                xT_copy(g)
                if g == 3 or g == 5:
                    std((g + 1) // 2, TB)
            std(B, NWIN)
            act.wait_ge(s["ql_in_psum"], 1)
            act.activation(qlT[:], PS[:, 2, :].rearrange("p (c n) -> p c n", c=4), ACT.Copy,
                           scale=float(DH) ** -0.5 / (N // LM)).then_inc(s["ql_copied"], 1)
            act.wait_ge(s["ql_in_psum"], 2)
            act.activation(klT[:], PS[:, 7, :].rearrange("p (c n) -> p c n", c=4), ACT.Copy,
                           scale=1.0 / (N // LM)).then_inc(s["ql_copied"], 1)
            act.wait_ge(s["g_in_psum"], 2)
            act.activation(Gq[:, 0, :], PS[:, 1, 0:H * LM], ACT.Copy, scale=float(DH) ** -0.5)
            act.copy(Gq[:, 1, :], PS[:, 1, H * LM:2 * H * LM]).then_inc(s["g_copied"], 1)
            act.wait_ge(s["lscores_read"], 1)
            act.activation(A2e[:], A2[:], ACT.Exp).then_inc(s["A2_exped"], 1)
            for g in range(G):
                act.wait_ge(s["l3_max"], g + 1)
                act.activation(E3[:, g, :].rearrange("p (a n) -> p a n", a=2), PS[:, 3 + 2 * g:5 + 2 * g, :], ACT.Exp,
                               bias=neg3[:, g:g + 1], accum_out=sum3[:, g:g + 1]).then_inc(s["l3_exped"], 1)

            def conv_copy(n):
                act.wait_ge(s["conv_in_psum"], n + 1)
                w, hh = n // 2, n % 2
                act.copy(YT[:, 4 * hh:4 * hh + 4, w * WIN:(w + 1) * WIN],
                         PS[:, (2, 7)[n % 2], 0:4 * WIN].rearrange("p (h m) -> p h m", h=4))\
                    .then_inc(s["conv_copied"], 1)

            def l1_exp(n):
                act.wait_ge(s["l1_shifted"], n + 1)
                v = A1[:, 2 * n:2 * n + 2, :]
                act.activation(v, v, ACT.Exp).then_inc(s["l1_exped"], 1)

            def e3T_copy(n):
                act.wait_ge(s["e3T_in_psum"], n + 1)
                act.copy(E3T[:, 2 * n:2 * n + 2, :], PS[:, (2, 7)[n % 2], :].rearrange("p (t c) -> p t c", t=2))\
                    .then_inc(s["e3T_copied"], 1)

            def a1T_copy(n):
                act.wait_ge(s["a1T_in_psum"], n + 1)
                g, q = n // 2, n % 2
                act.copy(A1T[:, g, q * 512:(q + 1) * 512], PS[:, (2, 7)[n % 2], :]).then_inc(s["a1T_copied"], 1)

            for stage in range(4 * PINV_ITERS):
                it, st = divmod(stage, 4)
                if st == 0:
                    act.wait_ge(s["pinv_p_in_psum"], it + 1)
                    act.copy(pT[:], PS[:, 1, 0:256].rearrange("p (g n) -> p g n", g=G)).then_inc(s["pT_copied"], 1)
                if st == 3:
                    act.wait_ge(s["pinv_z_in_psum"], it + 1)
                    act.mul(zT[:], PS[:, 1, 256:512].rearrange("p (g n) -> p g n", g=G), 0.25)\
                        .then_inc(s["zT_copied"], 1)
                if stage < 4:
                    l1_exp(stage)
                if stage < CONV:
                    conv_copy(stage)
            for n in range(4):
                e3T_copy(n)
            for n in range(4):
                a1T_copy(n)
            act.wait_ge(s["tT_in_psum"], 1)
            act.copy(TT_sb[:], PS[:, 3, 0:G * P]).then_inc(s["tT_copied"], 1)
            act.wait_ge(s["n_in_psum"], 1)
            act.copy(N_sb[:], PS[:, 3, 0:G * P].rearrange("p (g n) -> p g n", g=G)).then_inc(s["n_copied"], 1)
            for n in range(4):
                act.wait_ge(s["qk_in_psum"], n + 1)
                act.copy(qkT[:, n // 2, (n % 2) * 512:(n % 2 + 1) * 512], PS[0:QK, n, :]).then_inc(s["qk_copied"], 1)
            for n in range(NPIECE):
                act.wait_ge(s["scores_in_psum"], n + 1)
                r, c = n // 2, n % 2
                if r >= 2:
                    act.wait_ge(s[f"scores_stored{r % 2}"], 16 * (r // 2))
                act.activation(dstage[:, r % 2, c * 512:(c + 1) * 512], PS[:, 4 + n % 4, :], ACT.Copy,
                               scale=float(QK) ** -0.5).then_inc(s["scores_copied"], 1)
            for n in range(2):
                act.wait_ge(s["xgtok_in_psum"], n + 1)
                act.copy(xg[:, 4 * n:4 * n + 4, :], PS[:, n, :].rearrange("p (t d) -> p t d", t=4))\
                    .then_inc(s["xgtok_copied"], 1)
            for e in range(K9):
                act.wait_ge(s[f"wstage_loaded{e % 2}"], 32 * (e // 2 + 1))
                act.copy(wsp[:, e, 0:4:2, :], wstage[:, e % 2, :, :]).then_inc(s["w_high"], 1)
            act.wait_ge(s["alpha_neg"], 1)
            act.activation(aexp, araw, ACT.Exp, bias=aneg, accum_out=asum).then_inc(s["alpha_exped"], 1)

            def gate(T):
                act.wait_ge(s["xl_ready"], T + 1)
                act.activation(sw[:], xl[:], ACT.Tanh, scale=0.5).then_inc(s["th_done"], 1)
                act.wait_ge(s["th_done"], T + 1)
                act.activation(sw[:], sw[:], ACT.Square, scale=-0.5, bias=half_sb).then_inc(s["sw_ready"], 1)

            def x2T_copy(T):
                act.wait_ge(s["x2T_in_psum"], T + 1)
                act.copy(x2T[:], PS[:, 7, :]).then_inc(s["x2T_copied"], 1)

            def shares(T):
                act.wait_ge(s["gap_ready"], T + 1)
                act.activation(share[:, 0, :], gap[:], ACT.Tanh, scale=0.5).then_inc(s["share_ready"], 1)

            def cT_copy(T, slot):
                act.wait_ge(s["cT_in_psum"], T + 1)
                act.copy(cT_r[:, slot, :], PS[0:2 * E, 7, :]).then_inc(s["cT_copied"], 1)

            def expert_steps(T, slot, first, last):
                for k in range(K9):
                    m = step(T, k)
                    w = k - 1 if k else E
                    if k == 2:
                        cb_copy(T, 1)
                    for f in range(FC):
                        act.wait_ge(s["h_in_psum"], m * FC + f + 1)
                        after(act, s[f"low_done{f}"], m)
                        bias = colsT[:, w * FC + f:w * FC + f + 1]
                        if f < HIGH_BY_ACT:
                            act.activation(g32[:, f, :], PS[:, f, :], ACT.Gelu, bias=bias)
                            after(act, s["y_in_psum"], m - 1)
                            act.activation(ghl[:, (slot + k) % 2, f, 0, :], PS[:, f, :], ACT.Gelu, bias=bias)\
                                .then_inc(s[f"high_done{f}"], 1)
                        else:
                            act.activation(g32[:, f, :], PS[:, f, :], ACT.Gelu, bias=bias)\
                                .then_inc(s[f"gelu_done{f}"], 1)
                    if k >= 2:
                        cb_copy(T, k)
                    if k == 0:
                        shares(T)
                    if k == 1:
                        cT_copy(T, slot)
                    if not last:
                        if k == 1:
                            gate(T + 1)
                        if k == 7:
                            x2T_copy(T + 1)

            def cb_copy(T, k):
                act.wait_ge(s["cb_in_psum"], T * E + k)
                after(act, s["y_used"], step(T, k - 2) + 1 if k > 2 else step(T, 0))
                act.copy(cb[:, k % 2, :], PS[:, 6, :]).then_inc(s["cb_copied"], 1)

            gate(0)
            x2T_copy(0)
            over_chunks(act, NT // CH, expert_steps)

        @block.vector
        def _(dve):
            ds = Chain(dve, s["dve_step"])
            for k, eps in enumerate((EPS, 0.5)):
                dve.memset(eps_sb[:, k:k + 1], eps).then_inc(s["eps_made"], 1)
            ds.mark(dve.memset(taps_pad[:], 0.0))
            dve.wait_ge(s["taps_loaded"], 16)
            ds.wait()
            dve.tensor_copy(taps_pad[:, WIN - 1:WIN - 1 + TAPS], taps_sb[:, ::-1]).then_inc(s["taps_padded"], 1)

            norms = [0]

            def layernorm(src, dst, n, ready):
                for t in range(n):
                    ds.mark(dve.bn_stats(stats[:, t, :], src(t)))
                ds.wait()
                for t in range(n):
                    i = dve.bn_aggr(mv[:, t, :], stats[:, t, :])
                i.then_inc(s["var_ready"], 1)
                norms[0] += 1
                dve.wait_ge(s["std_ready"], norms[0])
                ds.done(dve.reciprocal(rstd[:, 0:n], rstd[:, 0:n]))
                for t in range(n):
                    dve.tensor_scalar(dst(t), src(t), mv[:, t, 0:1], rstd[:, t:t + 1], ALU.subtract, ALU.mult)\
                        .then_inc(ready, 1)

            def batch_norm(b):
                dve.wait_ge(s[f"x_loaded{b}"], 16)
                layernorm(lambda t: x[:, b * TB + t, :], lambda t: X[:, b * TB + t, :], TB, s["Xn_ready"])

            def landmark_sums(b):
                dve.wait_ge(s["xT_copied"], 2 * (b + 1))
                dve.reduce_sum(lmT[:, b * LM:(b + 1) * LM],
                               xT[:, b * N:(b + 1) * N].rearrange("p (l m) -> p l m", m=N // LM), AX)\
                    .then_inc(s["lm_summed"], 1)

            for b in range(B):
                batch_norm(b)
                if b:
                    landmark_sums(b - 1)
            landmark_sums(B - 1)
            dve.wait_ge(s["win_loaded"], 48)
            layernorm(lambda t: xw[:, t, :], lambda t: xw[:, t, :], NWIN, s["win_ready"])
            dve.wait_ge(s["ident_made"], 4)
            for k, c in enumerate((7.0, 15.0, 13.0)):
                ds.mark(dve.tensor_scalar(cI[:, k, :], ident[:], c, None, ALU.mult))

            dve.wait_ge(s["lscores_in_psum"], 2)
            ls = PS[:, 0, 0:(G + H) * LM].rearrange("p (a j) -> p a j", j=LM)
            ds.done(dve.reduce_max(mx10, ls, AX))
            dve.tensor_tensor(A2[:], ls, spread(mx10.unsqueeze(2), 2, LM), ALU.subtract).then_inc(s["lscores_read"], 1)
            for g in range(G):
                dve.wait_ge(s["l3_in_psum"], 2 * g + 2)
                ds.done(dve.tensor_reduce(mx3[:, g:g + 1], PS[:, 3 + 2 * g:5 + 2 * g, :].rearrange("p a n -> p (a n)"),
                                          AX, ALU.max))
                dve.tensor_scalar(neg3[:, g:g + 1], mx3[:, g:g + 1], -1.0, None, ALU.mult).then_inc(s["l3_max"], 1)
            dve.wait_ge(s["A2_exped"], 1)
            ds.done(dve.reduce_sum(sum10, A2e[:], AX))
            ds.done(dve.reciprocal(mx10, sum10))
            dve.tensor_tensor(A2[:], A2e[:], spread(mx10.unsqueeze(2), 2, LM), ALU.mult).then_inc(s["A2_ready"], 1)
            dve.wait_ge(s["A2_ready"], 1)
            for g in range(G):
                xb = dve.tensor_tensor(x_bd[:, g, :].rearrange("p (q j) -> p q j", j=LM),
                                       spread(A2[:, g:g + 1, :], 1, P // LM),
                                       blockones[:].rearrange("p (q j) -> p q j", j=LM), ALU.mult)
                xb.then_inc(s["xbd_ready"], 1)
            ds.done(dve.reduce_sum(rsum8, A2[:, G:G + H, :], AX))
            ds.mark(dve.reduce_max(lstat[:, 0:1], rsum8, AX))
            dve.wait_ge(s["colsum_in_psum"], 1)
            ds.done(dve.reduce_max(lstat[:, 1:2], PS[:, 0, 256:512], AX))
            dve.engine_nop().then_inc(s["landstats_ready"], 1)
            dve.wait_ge(s["landstats_max"], 1)
            ds.done(dve.tensor_tensor(sprod, lmax[:, 0:1], lmax[:, 1:2], ALU.mult))
            ds.done(dve.reciprocal(inv_s, sprod))
            dve.wait_ge(s["xbdT_in_psum"], 1)
            xTp = PS[:, 0, 0:256].rearrange("p (g n) -> p g n", g=G)
            dve.tensor_scalar(z[:], xTp, inv_s, None, ALU.mult).then_inc(s["z_ready"], 1)
            dve.tensor_copy(xT_bd[:], xTp).then_inc(s["z_ready"], 1)
            dve.tensor_scalar(zT[:], x_bd[:], inv_s, None, ALU.mult).then_inc(s["z_ready"], 1)

            def l1_shift(n):
                dve.wait_ge(s["l1_in_psum"], n + 1)
                v = PS[:, 3 + n, :].rearrange("p (a j) -> p a j", j=LM)
                ds.done(dve.reduce_max(l1mx[:, 2 + n % 2, :], v, AX))
                dve.tensor_tensor(A1[:, 2 * n:2 * n + 2, :].rearrange("p t (h j) -> p (t h) j", j=LM), v,
                                  spread(l1mx[:, 2 + n % 2, :].unsqueeze(2), 2, LM), ALU.subtract)\
                    .then_inc(s["l1_shifted"], 1)

            def l1_norm(n):
                dve.wait_ge(s["l1_exped"], n + 1)
                v = A1[:, 2 * n:2 * n + 2, :].rearrange("p t (h j) -> p (t h) j", j=LM)
                ds.done(dve.reduce_sum(l1mx[:, 0, :], v, AX))
                ds.done(dve.reciprocal(l1mx[:, 1, :], l1mx[:, 0, :]))
                dve.tensor_tensor(v, v, spread(l1mx[:, 1, :].unsqueeze(2), 2, LM), ALU.mult)\
                    .then_inc(s["l1_ready"], 1)
                dve.wait_ge(s["l1_ready"], n + 1)

            for stage in range(4 * PINV_ITERS):
                it, st = divmod(stage, 4)
                if st < 3:
                    if st == 0:
                        dve.wait_ge(s["pinv_p_in_psum"], it + 1)
                        src = PS[:, 0, 0:256]
                    else:
                        dve.wait_ge(s["pinv_t2_in_psum"], 2 * it + st)
                        src = PS[:, 0, (st % 2) * 256:(st % 2) * 256 + 256]
                    dve.scalar_tensor_tensor(tt[:, st, :, :], src.rearrange("p (g n) -> p g n", g=G), -1.0,
                                             spread(cI[:, st:st + 1, :], 1, G), ALU.mult, ALU.add)\
                        .then_inc(s["pinv_t_ready"], 1)
                else:
                    dve.wait_ge(s["pinv_z_in_psum"], it + 1)
                    dve.tensor_scalar(z[:], PS[:, 0, 256:512].rearrange("p (g n) -> p g n", g=G), 0.25, None, ALU.mult)\
                        .then_inc(s["pinv_z_ready"], 1)
                if stage < 4:
                    l1_shift(stage)
                if stage == 0:
                    dve.wait_ge(s["l3_exped"], G)
                    ds.done(dve.reciprocal(rec3, sum3))
                if 1 <= stage < 5:
                    l1_norm(stage - 1)
            dve.wait_ge(s["u_in_psum"], 1)
            for g in range(G):
                dve.tensor_scalar(U_sb[:, g, :], PS[:, 4, g * P:(g + 1) * P], rec3[:, g:g + 1], None, ALU.mult)\
                    .then_inc(s["u_copied"], 1)
            for c in range(2):
                dve.wait_ge(s["xg_in_psum"], c + 1)
                dve.tensor_scalar(xgT[:, c * 512:(c + 1) * 512], PS[:, 5 + c, :], colsT[:, OUTB:OUTB + 1], None, ALU.add)\
                    .then_inc(s["xgT_ready"], 1)
                dve.wait_ge(s["xgT_ready"], c + 1)
                dve.tensor_tensor(encT[:, c * 512:(c + 1) * 512], xgT[:, c * 512:(c + 1) * 512],
                                  xT[:, c * 512:(c + 1) * 512], ALU.add).then_inc(s["encT_ready"], 1)
            dve.wait_ge(s["edges_loaded"], 48)
            ds.done(dve.tensor_scalar(r_i[:, 0, :], rows_i[:], LOG_N, None, ALU.logical_shift_left))
            dve.tensor_tensor(idx[:], r_i[:, 0, :], cols_i[:], ALU.add).then_inc(s["idx_ready"], 1)
            dve.wait_ge(s["idx_ready"], 1)
            ds.mark(dve.tensor_scalar(r_i[:, 0, :], rows_i[:], P - 1, None, ALU.bitwise_and))
            ds.done(dve.tensor_scalar(r_i[:, 1, :], rows_i[:], P.bit_length() - 1, None, ALU.logical_shift_right))
            ds.done(dve.tensor_copy(r_f[:], r_i[:]))
            dve.wait_ge(s["xgtok_copied"], 2)
            for b in range(B):
                dve.tensor_tensor(X[:, tiles_of(b), :], X[:, tiles_of(b), :], xg[:], ALU.add).then_inc(s["enc_ready"], 1)
            for c in range(NT // CH):
                dve.wait_ge(s["value_in_psum"], c + 1)
                dve.tensor_tensor(value[:, c * CW:(c + 1) * CW].rearrange("p (t d) -> p t d", t=CH),
                                  PS[:, 4 + c % 4, :].rearrange("p (t d) -> p t d", t=CH),
                                  spread(wvb_sb[:].unsqueeze(1), 1, CH), ALU.add).then_inc(s["value_ready"], 1)
            for e in range(K9):
                dve.wait_ge(s["w_high"], e + 1)
                for k in range(2):
                    dve.tensor_tensor(wsp[:, e, 2 * k + 1, :], wstage[:, e % 2, k, :], wsp[:, e, 2 * k, :], ALU.subtract)\
                        .then_inc(s["w_low"], 1)
            dve.wait_ge(s["w_low"], 2 * K9)
            for q in range(4):
                a, b_ = q * EC // 4, (q + 1) * EC // 4
                oh = dve.tensor_tensor(onehot[:, a:b_, :], spread(iota_row[:].unsqueeze(1), 1, EC // 4),
                                       spread(r_f[:, 0, a:b_].unsqueeze(2), 2, P), ALU.is_equal)
                oh.then_inc(s["onehot_ready"], 1)
            ds.done(dve.tensor_tensor(oh8[:], spread(iota_row[:, 0:TB].unsqueeze(1), 1, EC),
                                      spread(r_f[:, 1, :].unsqueeze(2), 2, TB), ALU.is_equal))
            dve.wait_ge(s["gathered_all"], 16 * EC)
            ds.done(dve.tensor_tensor(gathered[:], gathered[:], vals_sb[:], ALU.mult))
            ds.done(dve.tensor_copy(parts[:, 0, :], gathered[:]))
            ds.done(dve.tensor_tensor(rest[:, 0, :], gathered[:], parts[:, 0, :], ALU.subtract))
            ds.done(dve.tensor_copy(parts[:, 1, :], rest[:, 0, :]))
            ds.done(dve.tensor_tensor(rest[:, 1, :], rest[:, 0, :], parts[:, 1, :], ALU.subtract))
            ds.done(dve.tensor_copy(parts[:, 2, :], rest[:, 1, :]))
            for k in range(3):
                dve.tensor_tensor(rhs3[:, :, k, :], oh8[:], spread(parts[:, k, :].unsqueeze(2), 2, TB), ALU.mult)\
                    .then_inc(s["rhs3_ready"], 1)
            dve.wait_ge(s["araw_in_psum"], 1)
            ds.done(dve.reduce_sum(araw, PS[:, 0, 0:3 * TB].rearrange("p (k t) -> p t k", k=3), AX))
            dve.reduce_max(amx, araw, AX).then_inc(s["araw_max"], 1)
            dve.wait_ge(s["araw_maxed"], 1)
            dve.tensor_scalar(aneg, amx_all, -1.0, None, ALU.mult).then_inc(s["alpha_neg"], 1)
            dve.wait_ge(s["alpha_summed"], 1)
            ds.done(dve.reciprocal(arec, asum_all))
            dve.tensor_scalar(alpha[:], aexp, arec, None, ALU.mult).then_inc(s["alpha_ready"], 1)

            ln = Drained(dve)

            def moments(src, half):
                for t in range(CH):
                    i = dve.bn_stats(st6[:, t, :], src[:, t, :])
                ln.done(i)
                for t in range(CH):
                    i = dve.bn_aggr(mv4[:, half * CH + t, :], st6[:, t, :])
                ln.done(i)

            def rsqrt(eps0, eps1=None):
                halves = [h for h, e in enumerate((eps0, eps1)) if e is not None]
                cut = slice(halves[0] * CH, (halves[-1] + 1) * CH)
                v, r, t, u = (newton[:, i, cut] for i in range(4))
                for h in halves:
                    c = slice(h * CH, (h + 1) * CH)
                    i = dve.tensor_scalar(newton[:, 0, c], mv4[:, c, 1], (eps0, eps1)[h], None, ALU.add)
                ln.done(i)
                ln.done(dve.tensor_scalar(guess[:, cut], v.bitcast(I32), 1, None, ALU.logical_shift_right))
                ln.done(dve.tensor_scalar(r.bitcast(I32), guess[:, cut], -1.0, float(0x5F3759DF), ALU.mult, ALU.add))

            def newton_steps(cut, n):
                v, r, t, u = (newton[:, i, cut] for i in range(4))
                for _ in range(n):
                    ln.done(dve.tensor_tensor(t, r, r, ALU.mult))
                    ln.done(dve.scalar_tensor_tensor(u, t, -0.5, v, ALU.mult, ALU.mult))
                    ln.done(dve.scalar_tensor_tensor(r, u, 1.5, r, ALU.add, ALU.mult))

            OTHER = slice(CH, 2 * CH)

            def normed(src, dst, half):
                for t in range(CH):
                    a = half * CH + t
                    i = dve.tensor_scalar(dst[:, t, :], src[:, t, :], mv4[:, a, 0:1], newton[:, 1, a:a + 1],
                                          ALU.subtract, ALU.mult)
                return i

            ffn_result = PS[:, 7, :].rearrange("p (t d) -> p t d", t=CH)

            def result_moments(T):
                dve.wait_ge(s["accT_in_psum"], T + 1)
                moments(ffn_result, 0)

            def result_normed(T):
                after(dve, s["out_stored"], T * 16)
                normed(ffn_result, fin, 0).then_inc(s["fin_normed"], 1)

            def mix_moments(T):
                dve.wait_ge(s["mixed"], T + 1)
                moments(yy, 1)

            def mix_normed():
                normed(yy, yy, 1).then_inc(s["mix_normed"], 1)

            def x1_moments(T, slot):
                dve.wait_ge(s["x1_ready"], T + 1)
                moments(x1[:, slot, :, :], 1)
                rsqrt(None, EPS)
                newton_steps(OTHER, 1)

            def x1_normed(slot):
                newton_steps(OTHER, 2)
                normed(x1[:, slot, :, :], yy, 1).then_inc(s["x2_ready"], 1)

            def x2_split(T, slot):
                dve.wait_ge(s["x2T_copied"], T + 1)
                ln.done(dve.tensor_copy(x2hl[:, slot, 0, :], x2T[:]))
                dve.tensor_tensor(x2hl[:, slot, 1, :], x2T[:], x2hl[:, slot, 0, :], ALU.subtract)\
                    .then_inc(s["x2_split"], 1)

            def route(T):
                dve.wait_ge(s["logits_in_psum"], T + 1)
                ln.done(dve.tensor_copy(logit[:], PS[:, 7, 0:CH * E].rearrange("p (t e) -> p t e", t=CH)))
                for t in range(CH):
                    i = dve.max(top[:, t, :], logit[:, t, :])
                ln.done(i)
                dve.tensor_tensor(gap[:], top[:, :, 1], top[:, :, 0], ALU.subtract).then_inc(s["gap_ready"], 1)
                for t in range(CH):
                    i = dve.max_index(topi[:, t, :], top[:, t, :], logit[:, t, :])
                ln.done(i)
                ln.done(dve.tensor_copy(topf[:], topi[:]))
                ln.done(dve.tensor_tensor(hot[:],
                                          spread(spread(iota_row[:, 0:E].unsqueeze(1).unsqueeze(1), 1, 2), 2, CH),
                                          spread(topf[:, :, 0:2].rearrange("p t k -> p k t").unsqueeze(3), 3, E),
                                          ALU.is_equal))

            def combine(T):
                dve.wait_ge(s["share_ready"], T + 1)
                for k in range(2):
                    i = dve.tensor_scalar(share[:, 1 + k, :], share[:, 0, :], (-0.5, 0.5)[k], 0.5, ALU.mult, ALU.add)
                ln.done(i)
                ln.done(dve.tensor_tensor(hot[:], hot[:], spread(share[:, 1:3, :].unsqueeze(3), 3, E), ALU.mult))
                ln.done(dve.tensor_tensor(comb[:], hot[:, 0, :, :], hot[:, 1, :, :], ALU.add))
                ln.done(dve.tensor_copy(c16[:, :, 0:E], comb[:]))
                dve.tensor_tensor(c16[:, :, E:2 * E], comb[:], c16[:, :, 0:E], ALU.subtract).then_inc(s["c16_ready"], 1)

            def split(T, slot, k):
                m = step(T, k)
                g = (slot + k) % 2
                for f in range(HIGH_BY_ACT, FC):
                    dve.wait_ge(s[f"gelu_done{f}"], m + 1)
                    if f == HIGH_BY_ACT:
                        after(dve, s["y_in_psum"], m - 1)
                    i = dve.tensor_copy(ghl[:, g, f, 0, :], g32[:, f, :])
                ln.done(i)
                for f in range(LOW_BY_POOL, FC):
                    if f < HIGH_BY_ACT:
                        dve.wait_ge(s[f"high_done{f}"], m + 1)
                    dve.tensor_tensor(ghl[:, g, f, 1, :], g32[:, f, :], ghl[:, g, f, 0, :], ALU.subtract)\
                        .then_inc(s[f"low_done{f}"], 1)

            def reduce_expert(T, slot, k):
                m = step(T, k)
                dve.wait_ge(s["y_in_psum"], m + 1)
                y = PS[:, 4 + (slot + k) % 2, :]
                if k == 0:
                    after(dve, s["accT_in_psum"], T)
                    dve.tensor_scalar(acc[:], y, colsT[:, SB2:SB2 + 1], None, ALU.add).then_inc(s["y_used"], 1)
                else:
                    dve.wait_ge(s["cb_copied"], T * E + k)
                    after(dve, s["prod_added"], T * E + k - 2)
                    dve.scalar_tensor_tensor(prod[:, k % 2, :], y, colsT[:, B2 + k - 1:B2 + k], cb[:, k % 2, :],
                                             ALU.add, ALU.mult).then_inc(s["y_used"], 1)

            def expert_steps(T, slot, first, last):
                for k in range(K9):
                    split(T, slot, k)
                    if k:
                        reduce_expert(T, slot, k - 1)
                    if k == 0:
                        combine(T)
                    if k == 2:
                        if not first:
                            result_moments(T - 1)
                        if not last:
                            mix_moments(T + 1)
                        rsqrt(None if first else EPS, None if last else EPS / 4)
                        newton_steps(slice(CH if first else 0, CH if last else 2 * CH), 1)
                    if k == 3:
                        newton_steps(slice(CH if first else 0, CH if last else 2 * CH), 2)
                        if not first:
                            result_normed(T - 1)
                        if not last:
                            mix_normed()
                    if not last:
                        if k == 5:
                            x1_moments(T + 1, 1 - slot)
                        if k == 6:
                            x1_normed(1 - slot)
                        if k == 7:
                            x2_split(T + 1, 1 - slot)
                        if k == 8:
                            route(T + 1)
                reduce_expert(T, slot, K9 - 1)

            mix_moments(0)
            rsqrt(None, EPS / 4)
            newton_steps(OTHER, 3)
            mix_normed()
            x1_moments(0, 0)
            x1_normed(0)
            x2_split(0, 0)
            route(0)
            over_chunks(dve, NT // CH, expert_steps)
            result_moments(NT // CH - 1)
            rsqrt(EPS)
            newton_steps(slice(0, CH), 3)
            result_normed(NT // CH - 1)

        @block.tensor
        def _(pe):
            pe.wait_ge(s["ident_made"], 1)
            pe.wait_ge(s["rows_in_loaded"], 96)
            pe.transpose(PS[:, 7, 0:NCOL], rows_in[:], ident[0:NCOL, 0:NCOL]).then_inc(s["cols_in_psum"], 1)
            pe.wait_ge(s["qkvw_loaded"], 16)
            for k in range(3):
                for c in range(4):
                    m = pe.transpose(PS[:, k, c * P:(c + 1) * P], qkvw[:, (4 * k + c) * P:(4 * k + c + 1) * P], ident[:])
                m.then_inc(s["wT_in_psum"], 1)

            def xT_group(g):
                pe.wait_ge(s["Xn_ready"], CH * (g + 1))
                if g >= 4:
                    pe.wait_ge(s["xT_copied"], g - 3)
                for t in range(CH):
                    m = pe.transpose(PS[:, 3 + g % 4, t * P:(t + 1) * P], X[:, g * CH + t, :], ident[:])
                m.then_inc(s["xT_in_psum"], 1)

            xT_group(0)
            xT_group(1)
            pe.wait_ge(s["wo_loaded"], 16)
            pe.wait_ge(s["wT_copied"], 3)
            for h in range(H):
                r = slice(DH * (h % 2), DH * (h % 2) + DH)
                m = pe.matmul(PS[:, h % 2, (h // 2) * P:(h // 2 + 1) * P], wT[r, 2, h // 2, :], wo_sb[r, h // 2, :],
                              start=True, stop=True)
                if h >= H - 2:
                    m.then_inc(s["vo_in_psum"], 1)
            pe.wait_ge(s["band_loaded"], 16)
            pe.wait_ge(s["ident_made"], 5)
            pe.wait_ge(s["cols_copied"], 1)
            for k in range(2):
                pe.matmul(PS[:, (2, 7)[k], 0:4 * WIN], flip[:], band[:, 4 * k:4 * k + 4, :], start=True, stop=True)\
                    .then_inc(s["toep_in_psum"], 1)
            for g in range(2, NT // CH):
                xT_group(g)
            pe.wait_ge(s["lm_summed"], B)
            pe.wait_ge(s["toep_copied"], 2)
            for k in range(2):
                for c in range(4):
                    m = pe.matmul(PS[:, (2, 7)[k], c * P:(c + 1) * P], qkvw[:, (4 * k + c) * P:(4 * k + c + 1) * P],
                                  lmT[:], start=True, stop=True)
                m.then_inc(s["ql_in_psum"], 1)
            pe.wait_ge(s["ql_copied"], 2)
            pe.wait_ge(s["vo_copied"], 2)
            for odd in range(2):
                r = slice(DH * odd, DH * odd + DH)
                for h in range(odd, H, 2):
                    q, c = h % 4, h // 2
                    pe.matmul(PS[q * LM:(q + 1) * LM, 0, (h // 4) * LM:(h // 4 + 1) * LM], qlT[r, c, 0:LM],
                              klT[r, c, 0:LM], start=True, stop=True)
                    for b in range(B):
                        m = pe.matmul(PS[b * LM:(b + 1) * LM, 0, (G + h) * LM:(G + h + 1) * LM],
                                      qlT[r, c, b * LM:(b + 1) * LM], klT[r, c, b * LM:(b + 1) * LM],
                                      start=True, stop=True)
                m.then_inc(s["lscores_in_psum"], 1)
                for k, l in enumerate((klT, qlT)):
                    for h in range(odd, H, 2):
                        m = pe.matmul(PS[:, 1, (k * H + h) * LM:(k * H + h + 1) * LM], wT[r, k, h // 2, :],
                                      l[r, h // 2, 0:LM], start=True, stop=True)
                m.then_inc(s["g_in_psum"], 1)
                if not odd:
                    pe.wait_ge(s["g_in_psum"], 1)
            pe.wait_ge(s["g_copied"], 1)
            pe.wait_ge(s["xT_copied"], NT // CH)
            for g in range(G):
                for c in range(2):
                    pe.matmul(PS[:, 3 + 2 * g + c, :], Gq[:, 1, g * P:(g + 1) * P], xT[:, c * 512:(c + 1) * 512],
                              start=True, stop=True).then_inc(s["l3_in_psum"], 1)
            pe.wait_ge(s["xbd_ready"], G)
            for g in range(G):
                m = pe.transpose(PS[:, 0, g * P:(g + 1) * P], x_bd[:, g, :], ident[:])
            m.then_inc(s["xbdT_in_psum"], 1)
            pe.wait_ge(s["ident_made"], 2)
            pe.wait_ge(s["A2_ready"], 1)
            pe.matmul(PS[:, 0, 256:512], blockones[:], A2[:, G:G + H, :].rearrange("p h j -> p (h j)"),
                      start=True, stop=True).then_inc(s["colsum_in_psum"], 1)

            def conv_step(n):
                w, hh = n // 2, n % 2
                if n == 0:
                    pe.wait_ge(s["win_ready"], NWIN)
                    pe.wait_ge(s["toep_copied"], 2)
                if n >= 2:
                    pe.wait_ge(s["conv_copied"], n - 1)
                pe.matmul(PS[:, (2, 7)[n % 2], 0:4 * WIN], xw[:, w, :], toep[:, 4 * hh:4 * hh + 4, :],
                          start=True, stop=True).then_inc(s["conv_in_psum"], 1)

            def l1_step(n):
                pe.wait_ge(s["l3_exped"], n // 2 + 1)
                for t in range(2):
                    tile = 2 * n + t
                    m = pe.matmul(PS[:, 3 + n, t * 256:(t + 1) * 256], xT[:, tile * P:(tile + 1) * P], Gq[:, 0, :],
                                  start=True, stop=True)
                m.then_inc(s["l1_in_psum"], 1)

            pe.wait_ge(s["z_ready"], 3)
            for stage in range(4 * PINV_ITERS):
                it, st = divmod(stage, 4)
                if st == 0:
                    if it:
                        pe.wait_ge(s["pinv_z_ready"], it)
                        pe.wait_ge(s["zT_copied"], it)
                    for g in range(G):
                        pe.matmul(PS[:, 0, g * P:(g + 1) * P], xT_bd[:, g, :], z[:, g, :], start=True, stop=True)
                    for g in range(G):
                        m = pe.matmul(PS[:, 1, g * P:(g + 1) * P], z[:, g, :], xT_bd[:, g, :],
                                      start=True, stop=True)
                    m.then_inc(s["pinv_p_in_psum"], 1)
                elif st < 3:
                    pe.wait_ge(s["pT_copied"], it + 1)
                    pe.wait_ge(s["pinv_t_ready"], 3 * it + st)
                    for g in range(G):
                        m = pe.matmul(PS[:, 0, (st % 2) * 256 + g * P:(st % 2) * 256 + (g + 1) * P], pT[:, g, :],
                                      tt[:, st - 1, g, :], start=True, stop=True)
                    m.then_inc(s["pinv_t2_in_psum"], 1)
                else:
                    pe.wait_ge(s["pinv_t_ready"], 3 * it + 3)
                    for g in range(G):
                        pe.matmul(PS[:, 0, 256 + g * P:256 + (g + 1) * P], zT[:, g, :], tt[:, 2, g, :], start=True, stop=True)
                    for g in range(G):
                        m = pe.matmul(PS[:, 1, 256 + g * P:256 + (g + 1) * P], tt[:, 2, g, :], zT[:, g, :],
                                      start=True, stop=True)
                    m.then_inc(s["pinv_z_in_psum"], 1)
                if stage < 4:
                    l1_step(stage)
                if stage < CONV:
                    conv_step(stage)
            for n in range(4):
                pe.wait_ge(s["conv_copied"], CONV - 1 + n if n < 2 else CONV)
                if n >= 2:
                    pe.wait_ge(s["e3T_copied"], n - 1)
                for t in range(2):
                    for g in range(G):
                        tile = 2 * n + t
                        m = pe.transpose(PS[:, (2, 7)[n % 2], (2 * t + g) * P:(2 * t + g + 1) * P],
                                         E3[:, g, tile * P:(tile + 1) * P], ident[:])
                m.then_inc(s["e3T_in_psum"], 1)
            for n in range(4):
                pe.wait_ge(s["e3T_copied"], min(n + 3, 4))
                if n >= 2:
                    pe.wait_ge(s["a1T_copied"], n - 1)
                pe.wait_ge(s["l1_ready"], 4)
                g, q = n // 2, n % 2
                for t in range(4):
                    m = pe.transpose(PS[:, (2, 7)[n % 2], t * P:(t + 1) * P], A1[:, 4 * q + t, g * P:(g + 1) * P], ident[:])
                m.then_inc(s["a1T_in_psum"], 1)
            pe.wait_ge(s["e3T_copied"], 4)
            for t in range(TB):
                m = pe.matmul(PS[:, 3, 0:G * P], X[:, t, :], E3T[:, t, :], start=(t == 0), stop=(t == TB - 1))
            m.then_inc(s["tT_in_psum"], 1)
            for c in range(2):
                for h in range(H):
                    pe.matmul(PS[:, 5 + c, :], VO[:, h, :], YT[:, h, c * 512:(c + 1) * 512], start=(h == 0), stop=False)
            pe.wait_ge(s["tT_copied"], 1)
            for h in range(H):
                q = h % 4
                m = pe.matmul(PS[q * LM:(q + 1) * LM, 4, (h // 4) * P:(h // 4 + 1) * P], TT_sb[:, h * LM:(h + 1) * LM],
                              VO[:, h, :], start=True, stop=True)
            m.then_inc(s["u_in_psum"], 1)
            pe.wait_ge(s["u_copied"], G)
            pe.wait_ge(s["zT_copied"], PINV_ITERS)
            for g in range(G):
                m = pe.matmul(PS[:, 3, g * P:(g + 1) * P], zT[:, g, :], U_sb[:, g, :], start=True, stop=True)
            m.then_inc(s["n_in_psum"], 1)
            pe.wait_ge(s["n_copied"], 1)
            pe.wait_ge(s["a1T_copied"], 4)
            for c in range(2):
                for g in range(G):
                    m = pe.matmul(PS[:, 5 + c, :], N_sb[:, g, :], A1T[:, g, c * 512:(c + 1) * 512], start=False,
                                  stop=(g == G - 1))
                m.then_inc(s["xg_in_psum"], 1)
            pe.wait_ge(s["small_loaded"], 64)
            for k in range(2):
                for c in range(2):
                    pe.wait_ge(s["encT_ready"], c + 1)
                    pe.matmul(PS[0:QK, 2 * k + c, :], wqk_sb[:, k, :], encT[:, c * 512:(c + 1) * 512],
                              start=True, stop=True).then_inc(s["qk_in_psum"], 1)
            pe.wait_ge(s["qk_copied"], 4)
            for n in range(NPIECE):
                r, c = n // 2, n % 2
                if n >= 4:
                    pe.wait_ge(s["scores_copied"], n - 3)
                pe.matmul(PS[:, 4 + n % 4, :], qkT[:, 0, r * P:(r + 1) * P], qkT[:, 1, c * 512:(c + 1) * 512],
                          start=True, stop=True).then_inc(s["scores_in_psum"], 1)
            for n in range(2):
                for t in range(4):
                    m = pe.transpose(PS[:, n, t * P:(t + 1) * P], xgT[:, (4 * n + t) * P:(4 * n + t + 1) * P], ident[:])
                m.then_inc(s["xgtok_in_psum"], 1)
            for c in range(NT // CH):
                pe.wait_ge(s["scores_copied"], NPIECE)
                if c >= 4:
                    pe.wait_ge(s["value_ready"], c - 3)
                for t in range(CH):
                    tile = c * CH + t
                    m = pe.matmul(PS[:, 4 + c % 4, t * P:(t + 1) * P], xT[:, tile * P:(tile + 1) * P], wv_sb[:],
                                  start=True, stop=True)
                m.then_inc(s["value_in_psum"], 1)
            pe.wait_ge(s["onehot_ready"], 4)
            pe.wait_ge(s["rhs3_ready"], 3)
            pe.wait_ge(s["xgtok_copied"], 2)
            for j in range(EC):
                m = pe.matmul(PS[:, 0, 0:3 * TB], onehot[:, j, :], rhs3[:, j, :, :].rearrange("p k t -> p (k t)"),
                              start=(j == 0), stop=(j == EC - 1))
            m.then_inc(s["araw_in_psum"], 1)
            pe.wait_ge(s["ident_made"], 4)

            def x2_transposes(T):
                pe.wait_ge(s["x2_ready"], T + 1)
                after(pe, s["fin_ready"], T - 1)
                for t in range(CH):
                    m = pe.transpose(PS[:, 7, t * P:(t + 1) * P], yy[:, t, :], ident[:])
                m.then_inc(s["x2T_in_psum"], 1)

            def logits(T):
                pe.wait_ge(s["x2T_copied"], T + 1)
                for t in range(CH):
                    m = pe.matmul(PS[:, 7, t * E:(t + 1) * E], x2T[:, t * P:(t + 1) * P], colsT[:, GATE:GATE + E],
                                  start=True, stop=True)
                m.then_inc(s["logits_in_psum"], 1)

            def c_transposes(T):
                pe.wait_ge(s["c16_ready"], T + 1)
                for t in range(CH):
                    m = pe.transpose(PS[0:2 * E, 7, t * P:(t + 1) * P], c16[:, t, :].bitcast(F32), ident[:])
                m.then_inc(s["cT_in_psum"], 1)

            def up(T, slot, k):
                w = k - 1 if k else E
                m = step(T, k)
                for f in range(FC):
                    after(pe, s[f"high_done{f}" if f < HIGH_BY_ACT else f"gelu_done{f}"], m)
                    cols_ = slice(f * P, (f + 1) * P)
                    pe.matmul(PS[:, f, :], wsp[:, w, 0, cols_], x2hl[:, slot, 0, :], start=True, stop=False)
                    pe.matmul(PS[:, f, :], wsp[:, w, 0, cols_], x2hl[:, slot, 1, :], start=False, stop=False)
                    pe.matmul(PS[:, f, :], wsp[:, w, 1, cols_], x2hl[:, slot, 0, :], start=False, stop=True)\
                        .then_inc(s["h_in_psum"], 1)

            def down(T, slot, k):
                w = k - 1 if k else E
                m = step(T, k)
                g = (slot + k) % 2
                bank = PS[:, 4 + g, :]
                after(pe, s["y_used"], m - 1)
                for f in range(FC):
                    pe.wait_ge(s[f"low_done{f}"], m + 1)
                    cols_ = slice(f * P, (f + 1) * P)
                    pe.matmul(bank, wsp[:, w, 2, cols_], ghl[:, g, f, 0, :], start=(f == 0), stop=False)
                    pe.matmul(bank, wsp[:, w, 2, cols_], ghl[:, g, f, 1, :], start=False, stop=False)
                    i = pe.matmul(bank, wsp[:, w, 3, cols_], ghl[:, g, f, 0, :], start=False, stop=(f == FC - 1))
                i.then_inc(s["y_in_psum"], 1)

            def acc_transposes(T):
                pe.wait_ge(s["prod_added"], T * E + E)
                for t in range(CH):
                    m = pe.transpose(PS[:, 7, t * P:(t + 1) * P], acc[:, t * P:(t + 1) * P], ident[:])
                m.then_inc(s["accT_in_psum"], 1)

            def expert_steps(T, slot, first, last):
                pe.wait_ge(s["x2_split"], T + 1)
                for k in range(K9):
                    up(T, slot, k)
                    if k == 2:
                        spread_weights(T, slot, 1)
                    if k >= 2:
                        spread_weights(T, slot, k)
                    if not last:
                        if k == 7:
                            x2_transposes(T + 1)
                        if k == 8:
                            logits(T + 1)
                    if k:
                        down(T, slot, k - 1)
                    if k == 1:
                        c_transposes(T)
                    if k == 2 and not first:
                        acc_transposes(T - 1)
                down(T, slot, K9 - 1)

            def spread_weights(T, slot, k):
                pe.wait_ge(s["cT_copied"], T + 1)
                after(pe, s["cb_copied"], T * E + k - 1)
                pe.matmul(PS[:, 6, :], sel_r[:, k - 1, :], cT_r[:, slot, :], start=True, stop=True)\
                    .then_inc(s["cb_in_psum"], 1)

            x2_transposes(0)
            logits(0)
            over_chunks(pe, NT // CH, expert_steps)
            acc_transposes(NT // CH - 1)


_INS = ['L0_attn_dense', 'L0_attn_adj_rows', 'L0_attn_adj_cols', 'L0_attn_adj_vals', 'L0_attn_wq', 'L0_attn_wk',
        'L0_attn_wv_w', 'L0_attn_wv_b', 'L0_attn_qkv_w', 'L0_attn_out_w', 'L0_attn_out_b', 'L0_attn_conv_w',
        'L0_ffn_gate_w', 'L0_ffn_W1', 'L0_ffn_b1', 'L0_ffn_W2', 'L0_ffn_b2', 'L0_ffn_sW1', 'L0_ffn_sb1',
        'L0_ffn_sW2', 'L0_ffn_sb2']


def kernel(**inputs):
    import numpy as _np
    import concourse.bacc as _bacc
    from concourse import mybir as _mybir
    from concourse.bass_utils import run_bass_kernel_spmd as _run

    nc = _bacc.Bacc("TRN2", target_bir_lowering=False, num_devices=1)
    arrays, args = {}, []
    for name in _INS:
        a = _np.ascontiguousarray(inputs[name])
        arrays[f"in_{name}_dram"] = a
        args.append(nc.dram_tensor(f"in_{name}_dram", a.shape, _mybir.dt.from_np(a.dtype), kind="ExternalInput").ap())
    shape = inputs['L0_attn_dense'].shape
    args.append(nc.dram_tensor("out_0_dram", shape, _mybir.dt.float32, kind="ExternalOutput").ap())
    sandwich_kernel(nc, *args)
    r = _run(nc, [arrays], core_ids=[0])
    return r.results[0]["out_0_dram"]
```

```python
from contextlib import ExitStack

import concourse.bass as bass
from concourse import mybir

ALU = mybir.AluOpType
ACT = mybir.ActivationFunctionType
AX = mybir.AxisListType.X
RED = bass.bass_isa.ReduceOp
F32, F32R, BF16, F16 = mybir.dt.float32, mybir.dt.float32r, mybir.dt.bfloat16, mybir.dt.float16
I32, U32 = mybir.dt.int32, mybir.dt.uint32

P = 128
EPS = 1e-5
LANDMARKS, PINV_ITERS, HEADS = 32, 6, 8


def spread(ap, axis, n):
    shape = list(ap.shape)
    shape[axis] = n
    return ap.broadcast_to(shape)


class Chain:

    def __init__(self, eng, sem, base=0):
        self.eng, self.sem, self.base, self.n = eng, sem, base, 0

    def mark(self, ins):
        self.n += 1
        return ins.then_inc(self.sem, 1)

    def wait(self):
        self.eng.wait_ge(self.sem, self.base + self.n)

    def done(self, ins):
        self.mark(ins)
        self.wait()


class Drained:

    def __init__(self, eng):
        self.eng = eng

    def mark(self, ins):
        return ins

    def wait(self):
        self.eng.drain()

    def done(self, ins):
        self.eng.drain()


def after(eng, sem, value):
    if not isinstance(value, int) or value > 0:
        eng.wait_ge(sem, value)


def over_chunks(eng, chunks, body):
    body(0, 0, True, False)
    with eng.Fori(0, (chunks - 2) // 2) as i:
        body(i * 2 + 1, 1, False, False)
        body(i * 2 + 2, 0, False, False)
    body(chunks - 1, 1, False, True)


def sandwich_kernel(nc, dense, rows, cols, vals, wq, wk, wv_w, wv_b, qkv_w, out_w, out_b, conv_w,
                    gate_w, W1, b1, W2, b2, sW1, sb1, sW2, sb2, out):
    B, N, D = dense.shape
    QK = wq.shape[1]
    E, _, F = W1.shape
    H, TAPS = HEADS, conv_w.shape[2]
    DH = qkv_w.shape[1] // 3 // H
    LM = LANDMARKS
    TB = N // P
    NT = B * TB
    FC = F // P
    K9 = E + 1
    CH = 4
    CW = CH * P
    WIN = P - (TAPS - 1)
    NWIN = -(-N // WIN)
    PAD = (TAPS - 1) // 2
    EC = rows.shape[0] // P
    KE = EC // 4
    GE = 4
    NG = KE // GE
    G = H * LM // P
    assert D == P and DH == 64 and LM == 32 and G == 2 and F == CW and B * LM == P and H == 8
    LOG_N = N.bit_length() - 1
    assert N == 1 << LOG_N

    scores_dram = nc.dram_tensor("scores", (N * N, 1), F32)
    taps_dram = nc.dram_tensor("taps", (H, WIN + P - 1), F32)
    NTAP = WIN + P - 1

    with ExitStack() as ctx:
        end = [16512]

        def at(name, shape, dt, offset=None):
            size = 4 if dt not in (BF16, F16) else 2
            for n in shape[1:]:
                size *= n
            o = end[0] if offset is None else offset
            t = nc.alloc_sbuf_tensor_at(name, shape, dt, offset=o)
            o += -(-size // 32) * 32
            if offset is None:
                end[0] = o
            return t, o

        def own(name, shape, dt):
            return at(name, shape, dt)[0]

        x = own("x", [P, NT, P], F32)
        X = own("X", [P, NT, P], F32)
        xT = own("xT", [P, NT * P], F32)
        value = xT
        xg_at = end[0]
        xg = own("xg", [P, TB, P], F32)
        ident = own("ident", [P, P], F32)
        blockones = own("blockones", [P, P], F32)
        iota_row = own("iota_row", [P, P], F32)
        small = own("small", [P, 64], F32)
        colsT = own("colsT", [P, K9 * FC + 2 + 2 * E], F32)
        wv_sb = own("wv_sb", [P, P], F32)
        wvb_sb = own("wvb_sb", [P, P], F32)
        wqk_sb = own("wqk_sb", [P, 2, P], F32)
        alpha = own("alpha", [P, TB], F32)
        sel_r = own("sel_r", [2 * E, E, P], F32R)
        eps_sb = own("eps_sb", [P, 2], F32)
        iota_col = own("iota_col", [P, TB], F32)
        ident_r = own("ident_r", [KE, KE], F32R)
        OUTB, SB2, GATE, B2 = K9 * FC, K9 * FC + 1, K9 * FC + 2, K9 * FC + 2 + E
        NCOL = B2 + E

        base1 = end[0]
        wsp, end1 = at("wsp", [P, K9, 4, F], F32R, base1)
        wraw, _ = at("wraw", [P, K9, 4, F], F32, base1)
        end[0] = end1
        o = base1
        YT, o = at("YT", [P, H, NWIN * WIN], F32, o)
        A1, o = at("A1", [P, TB, H * LM], F32, o)
        A1T, o = at("A1T", [P, G, N], F32, o)
        E3, o = at("E3", [P, G, N], F32, o)
        E3T, o = at("E3T", [P, TB, G * P], F32, o)
        assert o <= end1
        base2 = end1
        o = base2
        qkvw, o = at("qkvw", [P, 3 * H * DH], F32, o)
        wT, o = at("wT", [P, 3, 4, P], F32, o)
        wo_sb, o = at("wo_sb", [P, 4, P], F32, o)
        VO, o = at("VO", [P, H, P], F32, o)
        toep, o = at("toep", [P, H, WIN], F32, o)
        band, _ = at("band", [P, H, WIN], F32, base1)
        flip, _ = at("flip", [P, P], F32, base1 + 4 * H * WIN)
        xw, o = at("xw", [P, NWIN, P], F32, o)
        qkT, o = at("qkT", [P, 2, N], F32, o)
        xgT, o = at("xgT", [P, N], F32, o)
        encT, o = at("encT", [P, N], F32, o)
        taps_sb, o = at("taps_sb", [H, TAPS], F32, o)
        taps_pad, o = at("taps_pad", [H, NTAP], F32, o)
        rows_in, o = at("rows_in", [NCOL, P], F32, o)
        stats, o = at("stats", [P, 12, 6], F32, o)
        mv, o = at("mv", [P, 12, 2], F32, o)
        rstd, o = at("rstd", [P, 12], F32, o)
        lmT, o = at("lmT", [P, B * LM], F32, o)
        qlT, o = at("qlT", [P, 4, P], F32, o)
        klT, o = at("klT", [P, 4, P], F32, o)
        Gq, o = at("Gq", [P, 2, H * LM], F32, o)
        A2, o = at("A2", [P, G + H, LM], F32, o)
        A2e, o = at("A2e", [P, G + H, LM], F32, o)
        x_bd, o = at("x_bd", [P, G, P], F32, o)
        xT_bd, o = at("xT_bd", [P, G, P], F32, o)
        z, o = at("z", [P, G, P], F32, o)
        zT, o = at("zT", [P, G, P], F32, o)
        pT, o = at("pT", [P, G, P], F32, o)
        tt, o = at("tt", [P, 3, G, P], F32, o)
        cI, o = at("cI", [P, 3, P], F32, o)
        TT_sb, o = at("TT_sb", [P, G * P], F32, o)
        U_sb, o = at("U_sb", [P, G, P], F32, o)
        N_sb, o = at("N_sb", [P, G, P], F32, o)
        l1mx, o = at("l1mx", [P, 4, 2 * H], F32, o)
        end_attention = o
        dstage, o = at("dstage", [P, 2, N], F32, base2)
        assert o <= base2 + 4 * (3 * H * DH * 2 + 4 * P), "the stage must end before VO"
        o = end_attention
        idx, o = at("idx", [P, EC], I32, o)
        gathered, o = at("gathered", [P, EC], F32, o)
        vals_sb, o = at("vals_sb", [P, EC], F32, o)
        rows_i, o = at("rows_i", [P, EC], I32, o)
        cols_i, o = at("cols_i", [P, EC], I32, o)
        r_i, o = at("r_i", [P, 2, EC], I32, o)
        r_f, o = at("r_f", [P, 2, EC], F32, o)
        ek_i, o = at("ek_i", [KE, 2, P], I32, o)
        ek_r, o = at("ek_r", [KE, 2, P], F32R, o)
        ekrow_i, o = at("ekrow_i", [KE, 2, P], I32, o)
        ekrow, o = at("ekrow", [KE, 3, P], F32, o)
        assert o <= 229344, o
        o = base1
        oht, o = at("oht", [P, 2, 2, TB, GE * P], BF16, o)
        qkp, o = at("qkp", [P, 3, TB, 2, QK], BF16, o)
        bc16, o = at("bc16", [P, NG, 2, GE * P], F16, o)
        qkrest, o = at("qkrest", [P, 2, 2, 2, QK], F32, o)
        qkprod, o = at("qkprod", [P, GE, QK], F32, o)
        assert o <= base1 + E * 4 * F * 4, "the shared expert's weights lie behind"
        o = base2 + 2 * EC * (P + 4 * TB)
        rest, o = at("rest", [P, 2, EC], F32, o)
        parts, o = at("parts", [P, 3, EC], BF16, o)
        assert o <= end_attention
        onehot, o = at("onehot", [P, EC, P], BF16, end1)
        oh8, o2 = at("oh8", [P, EC, TB], BF16, end1 + 2 * EC * P)
        rhs3, o2 = at("rhs3", [P, EC, 3, TB], BF16, o2)
        o = base2
        g32, o = at("g32", [P, FC, CW], F32, o)
        ghl, o = at("ghl", [P, 2, FC, 2, CW], F32R, o)
        x2hl, o = at("x2hl", [P, 2, 2, CW], F32R, o)
        x2T, o = at("x2T", [P, CW], F32, o)
        cb, o = at("cb", [P, 2, CW], F32, o)
        acc, o = at("acc", [P, 2, CW], F32, o)
        prod, _ = at("prod", [P, 2, CW], F32, xg_at)
        x1, o = at("x1", [P, 2, CH, P], F32, o)
        xl, o = at("xl", [P, CH, P], F32, o)
        sw, o = at("sw", [P, CH, P], F32, o)
        yy, o = at("yy", [P, CH, P], F32, o)
        fin, o = at("fin", [P, CH, P], F32, o)
        st6, o = at("st6", [P, CH, 6], F32, o)
        mv4, o = at("mv4", [P, 2 * CH, 2], F32, o)
        newton, o = at("newton", [P, 4, 2 * CH], F32, o)
        shift, o = at("shift", [P, CH], F32, o)
        guess, o = at("guess", [P, 2 * CH], I32, o)
        logit, o = at("logit", [P, CH, E], F32, o)
        top, o = at("top", [P, CH, 8], F32, o)
        topi, o = at("topi", [P, CH, 8], U32, o)
        topf, o = at("topf", [P, CH, 8], F32, o)
        gap, o = at("gap", [P, CH], F32, o)
        share, o = at("share", [P, 3, CH], F32, o)
        hot, o = at("hot", [P, 2, CH, E], F32, o)
        comb, o = at("comb", [P, CH, E], F32, o)
        c16, o = at("c16", [P, CH, 2 * E], F32R, o)
        cT_r, o = at("cT_r", [2 * E, 2, CW], F32R, o)
        assert o <= 229344, o

        PS = ctx.enter_context(nc.psum_tensor("PS", [P, 8, 512], F32))

        names = """x_loaded0 x_loaded1 x_loaded2 x_loaded3 win_zeroed win_loaded qkvw_loaded wo_loaded taps_loaded rows_in_loaded edges_loaded
            small_loaded taps_padded taps_stored band_loaded toep_in_psum toep_copied ident_made pool_step dve_step
            Xn_ready win_ready xT_in_psum xT_copied cols_in_psum cols_copied wT_in_psum wT_copied
            vo_in_psum vo_copied lm_summed ql_in_psum ql_copied lscores_in_psum lscores_read A2_exped A2_ready
            xbd_ready xbdT_in_psum colsum_in_psum landstats_ready landstats_max z_ready g_in_psum g_copied
            l3_in_psum l3_max l3_exped l1_in_psum l1_shifted l1_exped l1_ready conv_in_psum conv_copied
            e3T_in_psum e3T_copied a1T_in_psum a1T_copied tT_in_psum tT_copied u_in_psum u_copied
            pinv_p_in_psum pT_copied pinv_t_ready pinv_t2_in_psum pinv_z_in_psum pinv_z_ready zT_copied
            n_in_psum n_copied xg_in_psum xgT_ready encT_ready qk_in_psum qk_copied scores_in_psum
            scores_copied scores_stored0 scores_stored1 xgtok_in_psum xgtok_copied idx_ready gathered0 gathered1 onehot_ready
            rhs3_ready araw_in_psum araw_max araw_maxed alpha_neg alpha_exped alpha_summed alpha_ready wqk_padded ek_ready ekT_in_psum ekT_copied qkt_in_psum qkp_split qkp_ready bc_in_psum bc_copied oht_ready pairs_in_psum q_picked dots_done picks_over result_stats
            value_in_psum value_ready enc_ready wstage_loaded0 wstage_loaded1 w_high w_low
            xl_ready th_done sw_ready mixed mix_normed x1_ready fin_normed x2_ready x2T_in_psum x2T_copied x2_split logits_in_psum gap_ready share_ready
            c16_ready cT_in_psum cT_copied h_in_psum gelu_done2 gelu_done3
            high_done0 high_done1 low_done0 low_done1 low_done2 low_done3 cb_in_psum cb_copied
            y_in_psum y_used prod_added accT_in_psum fin_ready out_stored var_ready std_ready eps_made""".split()
        s = {n: ctx.enter_context(nc.semaphore(n)) for n in names}
        half_sb = eps_sb[:, 1:2]
        W_EARLY = 5

        def step(T, k):
            return T * K9 + k

        HIGH_BY_ACT = 2

        def low_by_pool(k):
            return 1 if k in (5,) else 2
        mx3, neg3, sum3, rec3 = small[:, 0:2], small[:, 2:4], small[:, 4:6], small[:, 6:8]
        mx10, sum10 = small[:, 8:18], small[:, 18:28]
        lstat, lmax, inv_s, sprod = small[:, 28:30], small[:, 30:32], small[:, 32:33], small[:, 33:34]
        araw, amx, amx_all, aneg, aexp = (small[:, 34:42], small[:, 42:43], small[:, 43:44], small[:, 44:45],
                                          small[:, 45:53])
        asum, asum_all, arec, rsum8 = small[:, 53:54], small[:, 54:55], small[:, 55:56], small[:, 56:64]

        EC0 = EC * 7 // 8
        NPIECE = 2 * TB
        block = ctx.enter_context(nc.Block())

        CONV, CONV_EARLY = 2 * NWIN, 4
        STAGES = 4 * PINV_ITERS
        beside = {name: [range(0)] * STAGES for name in ("l3", "l1", "conv", "e3T", "a1T", "tT", "vo")}
        for g in range(G):
            beside["l3"][g] = range(g, g + 1)
        for n in range(4):
            beside["l1"][4 + n] = range(n, n + 1)
        done = CONV_EARLY
        for stage in range(1, STAGES):
            n = min(1 if beside["l1"][stage] else 2, CONV - done)
            beside["conv"][stage] = range(done, done + n)
            done += n
        for k in range(2):
            beside["e3T"][14 + k] = beside["a1T"][16 + k] = range(2 * k, 2 * k + 2)
        for k in range(4):
            beside["tT"][17 + k] = range(2 * k, 2 * k + 2)
        for stage in range(10, STAGES):
            beside["vo"][stage] = [k for k in range(2 * H) if 10 + k * (STAGES - 10) // (2 * H) == stage]

        def tiles_of(b):
            return slice(b * TB, (b + 1) * TB)

        @block.sync
        def _(sp):
            sp.dma_start(x[:, tiles_of(0), :], dense[0].rearrange("(t p) d -> p t d", p=P)).then_inc(s["x_loaded0"], 16)
            sp.dma_start(x[:, tiles_of(1), :], dense[1].rearrange("(t p) d -> p t d", p=P)).then_inc(s["x_loaded1"], 16)
            sp.dma_start(qkvw[:], qkv_w).then_inc(s["qkvw_loaded"], 16)
            for b in range(2, B):
                sp.dma_start(x[:, tiles_of(b), :], dense[b].rearrange("(t p) d -> p t d", p=P))\
                    .then_inc(s[f"x_loaded{b}"], 16)
            sp.dma_start(wo_sb[:], out_w.rearrange("(c p) n -> p c n", p=P)).then_inc(s["wo_loaded"], 16)
            sp.dma_start(taps_sb[:], conv_w[:, 0, :, 0]).then_inc(s["taps_loaded"], 16)
            sp.dma_start(rows_in[0:E * FC, :], b1.rearrange("e (c p) -> (e c) p", p=P)).then_inc(s["rows_in_loaded"], 16)
            sp.dma_start(rows_in[E * FC:K9 * FC, :], sb1.rearrange("(c p) -> c p", p=P)).then_inc(s["rows_in_loaded"], 16)
            sp.dma_start(rows_in[OUTB:OUTB + 1, :], out_b.rearrange("(a p) -> a p", a=1)).then_inc(s["rows_in_loaded"], 16)
            sp.dma_start(rows_in[SB2:SB2 + 1, :], sb2.rearrange("(a p) -> a p", a=1)).then_inc(s["rows_in_loaded"], 16)
            sp.dma_start(rows_in[GATE:GATE + E, :], gate_w).then_inc(s["rows_in_loaded"], 16)
            sp.dma_start(rows_in[B2:B2 + E, :], b2).then_inc(s["rows_in_loaded"], 16)
            sp.wait_ge(s["win_zeroed"], 2)
            sp.dma_start(xw[PAD:P, 0, :], dense[0, 0:P - PAD, :]).then_inc(s["win_loaded"], 16)
            inner = bass.AP(dense.tensor, dense.offset + (WIN - PAD) * D, [[D, P], [WIN * D, NWIN - 2], [1, D]])
            sp.dma_start(xw[:, 1:NWIN - 1, :], inner).then_inc(s["win_loaded"], 16)
            last = N - ((NWIN - 1) * WIN - PAD)
            sp.dma_start(xw[0:last, NWIN - 1, :], dense[0, N - last:N, :]).then_inc(s["win_loaded"], 16)
            sp.wait_ge(s["taps_padded"], 1)
            sp.dma_start(taps_dram[:, :], taps_pad[:]).then_inc(s["taps_stored"], 16)
            sp.wait_ge(s["taps_stored"], 16)
            sp.dma_start(band[:], bass.AP(taps_dram, 0, [[1, P], [NTAP, H], [1, WIN]]))\
                .then_inc(s["band_loaded"], 16)
            sp.dma_start(wqk_sb[:, 0, 0:QK], wq).then_inc(s["small_loaded"], 16)
            sp.dma_start(wqk_sb[:, 1, 0:QK], wk).then_inc(s["small_loaded"], 16)
            sp.dma_start(wv_sb[:], wv_w).then_inc(s["small_loaded"], 16)
            sp.dma_start(wvb_sb[:], wv_b.partition_broadcast(P)).then_inc(s["small_loaded"], 16)
            for dst, src in ((rows_i, rows), (cols_i, cols), (vals_sb, vals)):
                sp.dma_start(dst[:, KE:EC], src[KE * P:EC * P].rearrange("(p j) -> p j", p=P))\
                    .then_inc(s["edges_loaded"], 16)
            for dst, src in ((ek_i[:, 0, :], rows), (ek_i[:, 1, :], cols), (ekrow[:, 2, :], vals)):
                sp.dma_start(dst, src[0:KE * P].rearrange("(k p) -> k p", p=P)).then_inc(s["edges_loaded"], 16)
            for r in range(TB):
                sp.wait_ge(s["scores_copied"], 2 * r + 2)
                sp.dma_start(bass.AP(scores_dram, r * P * N, [[N, P], [1, N]]), dstage[:, r % 2, :])\
                    .then_inc(s[f"scores_stored{r % 2}"], 16)
            for n in range(K9):
                w1 = W1[n - 1] if n else sW1
                w2 = W2[n - 1] if n else sW2
                if n == 0:
                    sp.wait_ge(s["xgtok_copied"], 2)
                if n == 1:
                    sp.wait_ge(s["picks_over"], 1)
                if n >= 2:
                    sp.wait_ge(s[f"wstage_loaded{n % 2}"], 32 * (n // 2))
                raw = wraw[:, n - 1 if n else E, :, :]
                sp.dma_start(raw[:, 1, :], w1).then_inc(s[f"wstage_loaded{n % 2}"], 16)
                sp.dma_start(raw[:, 3, :].rearrange("p (c h) -> p c h", c=FC),
                             w2.rearrange("(c p) h -> p c h", p=P)).then_inc(s[f"wstage_loaded{n % 2}"], 16)
            with sp.Fori(0, B) as b:
                for half in range(2):
                    T = b * 2 + half
                    sp.wait_ge(s["fin_ready"], T + 1)
                    sp.dma_start(out[bass.ds(b, 1), half * CW:(half + 1) * CW, :].rearrange("b (t p) d -> p (b t) d", p=P),
                                 fin[:]).then_inc(s["out_stored"], 16)
            sp.wait_ge(s["out_stored"], 16 * NT // CH)

        @block.gpsimd
        def _(pool):
            ps = Chain(pool, s["pool_step"])
            ps.mark(pool.memset(ident[:], 0.0))
            ps.mark(pool.memset(blockones[:], 0.0))
            pool.memset(xw[:, 0, :], 0.0).then_inc(s["win_zeroed"], 1)
            pool.memset(xw[:, NWIN - 1, :], 0.0).then_inc(s["win_zeroed"], 1)
            ps.wait()
            pool.affine_select(out=ident[:], in_=ident[:], compare_op=ALU.not_equal, fill=1.0, base=0,
                               pattern=[[-1, P]], channel_multiplier=1).then_inc(s["ident_made"], 1)
            pool.wait_ge(s["win_zeroed"], 2)
            pool.wait_ge(s["ident_made"], 1)
            for q in range(P // LM):
                ps.done(pool.memset(blockones[q * LM:(q + 1) * LM, q * LM:(q + 1) * LM], 1.0))
            pool.drain().then_inc(s["ident_made"], 1)
            pool.iota(iota_row[:], pattern=[[1, P]], base=0, channel_multiplier=0,
                      allow_small_or_imprecise_dtypes=True).then_inc(s["ident_made"], 1)
            ps.done(pool.iota(iota_col[:], pattern=[[P, TB]], base=0, channel_multiplier=1,
                              allow_small_or_imprecise_dtypes=True))
            pool.wait_ge(s["ident_made"], 3)
            selw = E3[0:2 * E, 0, :].rearrange("k (e p) -> k e p", e=E)
            ps.done(pool.memset(selw, 0.0))
            for base in (0, -E):
                ps.done(pool.affine_select(out=selw, in_=selw, compare_op=ALU.not_equal, fill=1.0, base=base,
                                           pattern=[[-1, E], [0, P]], channel_multiplier=1))
            pool.tensor_copy(sel_r[:], selw).then_inc(s["ident_made"], 1)
            ps.done(pool.memset(flip[:], 0.0))
            pool.affine_select(out=flip[:], in_=flip[:], compare_op=ALU.not_equal, fill=1.0, base=1 - P,
                               pattern=[[1, P]], channel_multiplier=1).then_inc(s["ident_made"], 1)
            pool.wait_ge(s["landstats_ready"], 1)
            pool.partition_all_reduce(lmax, lstat, P, RED.max).then_inc(s["landstats_max"], 1)
            pool.wait_ge(s["idx_ready"], 1)
            for k in range(2):
                pool.wait_ge(s[f"scores_stored{k}"], 16 * TB // 2)
            table = scores_dram.ap()
            for j in range(KE, EC):
                pool.indirect_dma_start(gathered[:, j:j + 1], None, table,
                                        bass.IndirectOffsetOnAxis(ap=idx[:, j:j + 1], axis=0))\
                    .then_inc(s["gathered0" if j < EC0 else "gathered1"], 16)
            pool.wait_ge(s["araw_max"], 1)
            pool.partition_all_reduce(amx_all, amx, P, RED.max).then_inc(s["araw_maxed"], 1)
            pool.wait_ge(s["alpha_exped"], 1)
            pool.partition_all_reduce(asum_all, asum, P, RED.add).then_inc(s["alpha_summed"], 1)

            def weigh(T, slot):
                val = value[:, bass.ds(T * CW, CW)].rearrange("p (t d) -> p t d", t=CH)
                pool.tensor_tensor(xl[:], val, spread(alpha[:, slot * CH:(slot + 1) * CH].unsqueeze(2), 2, P), ALU.mult)\
                    .then_inc(s["xl_ready"], 1)

            def mix(T):
                enc = X[:, bass.ds(T * CH, CH), :]
                pool.drain()
                pool.tensor_tensor(yy[:], xl[:], enc, ALU.subtract)
                pool.drain()
                pool.wait_ge(s["sw_ready"], T + 1)
                pool.tensor_tensor(yy[:], yy[:], sw[:], ALU.mult)
                pool.drain()
                pool.tensor_tensor(yy[:], yy[:], enc, ALU.add).then_inc(s["mixed"], 1)

            def residual(T, slot):
                pool.drain()
                pool.tensor_tensor(x1[:, slot, :, :], yy[:], x[:, bass.ds(T * CH, CH), :], ALU.add)\
                    .then_inc(s["x1_ready"], 1)

            def last_residual(T, slot):
                pool.wait_ge(s["fin_normed"], T + 1)
                pool.tensor_tensor(fin[:], fin[:], x1[:, slot, :, :], ALU.add).then_inc(s["fin_ready"], 1)

            def expert_steps(T, slot, first, last):
                for k in range(K9):
                    m = step(T, k)
                    if k == 4 and not last:
                        pool.wait_ge(s["mix_normed"], T + 2)
                    for f in range(low_by_pool(k)):
                        pool.wait_ge(s[f"high_done{f}"], m + 1)
                        pool.tensor_tensor(ghl[:, (slot + k) % 2, f, 1, :], g32[:, f, :], ghl[:, (slot + k) % 2, f, 0, :],
                                           ALU.subtract).then_inc(s[f"low_done{f}"], 1)
                    if k >= 2:
                        add_expert(T, slot, k - 1)
                    if k == 0 and not first:
                        add_expert(T - 1, 1 - slot, K9 - 1)
                    if k == 4 and not first:
                        last_residual(T - 1, 1 - slot)
                    if not last:
                        if k == 0:
                            weigh(T + 1, 1 - slot)
                        if k == 1:
                            mix(T + 1)
                        if k == 4:
                            residual(T + 1, 1 - slot)

            def add_expert(T, slot, k):
                pool.wait_ge(s["y_used"], step(T, k) + 1)
                after(pool, s["prod_added"], T * E + k - 1)
                pool.tensor_tensor(acc[:, slot, :], acc[:, slot, :], prod[:, k % 2, :], ALU.add).then_inc(s["prod_added"], 1)

            pool.wait_ge(s["x1_ready"], 1)
            over_chunks(pool, NT // CH, expert_steps)
            add_expert(NT // CH - 1, 1, K9 - 1)
            last_residual(NT // CH - 1, 1)

        @block.scalar
        def _(act):
            def std(k, n):
                act.wait_ge(s["var_ready"], k + 1)
                act.activation(rstd[:, 0:n], mv[:, 0:n, 1], ACT.Sqrt, bias=eps_sb[:, 0:1]).then_inc(s["std_ready"], 1)

            act.wait_ge(s["eps_made"], 2)
            std(0, TB)

            def xT_copy(g):
                act.wait_ge(s["xT_in_psum"], g + 1)
                act.copy(xT[:, g * CW:(g + 1) * CW], PS[:, 3 + g % 4, :]).then_inc(s["xT_copied"], 1)

            xT_copy(0)
            xT_copy(1)
            std(1, TB)
            for k in range(3):
                act.wait_ge(s["wT_in_psum"], k + 1)
                act.copy(wT[:, k, :, :], PS[:, k, :].rearrange("p (c n) -> p c n", c=4)).then_inc(s["wT_copied"], 1)
            for k in range(2):
                act.wait_ge(s["vo_in_psum"], k + 1)
                act.copy(VO[:, k:H:2, :], PS[:, k, :].rearrange("p (c n) -> p c n", c=4))\
                    .then_inc(s["vo_copied"], 1)
            for g in range(2, NT // CH):
                xT_copy(g)
                if g == 3 or g == 5:
                    std((g + 1) // 2, TB)
                if g == 5:
                    for k in range(2):
                        act.wait_ge(s["toep_in_psum"], k + 1)
                        act.copy(toep[:, 4 * k:4 * k + 4, :], PS[:, (2, 7)[k], 0:4 * WIN].rearrange("p (h m) -> p h m", h=4))\
                            .then_inc(s["toep_copied"], 1)
            act.wait_ge(s["cols_in_psum"], 1)
            act.copy(colsT[:], PS[:, 7, 0:NCOL]).then_inc(s["cols_copied"], 1)
            act.wait_ge(s["ql_in_psum"], 1)
            act.activation(qlT[:], PS[:, 2, :].rearrange("p (c n) -> p c n", c=4), ACT.Copy,
                           scale=float(DH) ** -0.5 / (N // LM)).then_inc(s["ql_copied"], 1)
            act.wait_ge(s["ql_in_psum"], 2)
            act.activation(klT[:], PS[:, 7, :].rearrange("p (c n) -> p c n", c=4), ACT.Copy,
                           scale=1.0 / (N // LM)).then_inc(s["ql_copied"], 1)
            std(B, NWIN)
            act.wait_ge(s["lscores_read"], 1)
            act.activation(A2e[:], A2[:], ACT.Exp).then_inc(s["A2_exped"], 1)
            act.wait_ge(s["g_in_psum"], 2)
            act.activation(Gq[:, 0, :], PS[:, 1, 0:H * LM], ACT.Copy, scale=float(DH) ** -0.5)
            act.copy(Gq[:, 1, :], PS[:, 1, H * LM:2 * H * LM]).then_inc(s["g_copied"], 1)

            def conv_copy(n):
                act.wait_ge(s["conv_in_psum"], n + 1)
                w, hh = n // 2, n % 2
                act.copy(YT[:, 4 * hh:4 * hh + 4, w * WIN:(w + 1) * WIN],
                         PS[:, (2, 7)[n % 2], 0:4 * WIN].rearrange("p (h m) -> p h m", h=4))\
                    .then_inc(s["conv_copied"], 1)

            for n in range(CONV_EARLY):
                conv_copy(n)

            def l3_exp(g):
                act.wait_ge(s["l3_max"], g + 1)
                act.activation(E3[:, g, :].rearrange("p (a n) -> p a n", a=2), PS[:, 3 + 2 * g:5 + 2 * g, :], ACT.Exp,
                               bias=neg3[:, g:g + 1], accum_out=sum3[:, g:g + 1]).then_inc(s["l3_exped"], 1)

            def l1_exp(n):
                act.wait_ge(s["l1_shifted"], n + 1)
                v = A1[:, 2 * n:2 * n + 2, :]
                act.activation(v, v, ACT.Exp).then_inc(s["l1_exped"], 1)

            def e3T_copy(n):
                act.wait_ge(s["e3T_in_psum"], n + 1)
                act.copy(E3T[:, 2 * n:2 * n + 2, :], PS[:, (2, 7)[n % 2], :].rearrange("p (t c) -> p t c", t=2))\
                    .then_inc(s["e3T_copied"], 1)

            def a1T_copy(n):
                act.wait_ge(s["a1T_in_psum"], n + 1)
                g, q = n // 2, n % 2
                act.copy(A1T[:, g, q * 512:(q + 1) * 512], PS[:, (2, 7)[n % 2], :]).then_inc(s["a1T_copied"], 1)

            for stage in range(STAGES):
                it, st = divmod(stage, 4)
                if st == 0:
                    act.wait_ge(s["pinv_p_in_psum"], it + 1)
                    act.copy(pT[:], PS[:, 1, 0:256].rearrange("p (g n) -> p g n", g=G)).then_inc(s["pT_copied"], 1)
                if st == 3:
                    act.wait_ge(s["pinv_z_in_psum"], it + 1)
                    act.mul(zT[:], PS[:, 1, 256:512].rearrange("p (g n) -> p g n", g=G), 0.25)\
                        .then_inc(s["zT_copied"], 1)
                if stage:
                    for n in beside["l3"][stage - 1]:
                        l3_exp(n)
                    for n in beside["l1"][stage - 1]:
                        l1_exp(n)
                for n in beside["conv"][stage]:
                    conv_copy(n)
                for n in beside["e3T"][stage]:
                    e3T_copy(n)
                for n in beside["a1T"][stage]:
                    a1T_copy(n)
            act.wait_ge(s["tT_in_psum"], 1)
            act.copy(TT_sb[:], PS[:, 3, 0:G * P]).then_inc(s["tT_copied"], 1)
            act.wait_ge(s["n_in_psum"], 1)
            act.copy(N_sb[:], PS[:, 3, 0:G * P].rearrange("p (g n) -> p g n", g=G)).then_inc(s["n_copied"], 1)
            for n in range(4):
                act.wait_ge(s["qk_in_psum"], n + 1)
                act.copy(qkT[:, n // 2, (n % 2) * 512:(n % 2 + 1) * 512], PS[:, n, :]).then_inc(s["qk_copied"], 1)
            for n in range(NPIECE):
                act.wait_ge(s["scores_in_psum"], n + 1)
                r, c = n // 2, n % 2
                if r >= 2:
                    act.wait_ge(s[f"scores_stored{r % 2}"], 16 * (r // 2))
                act.activation(dstage[:, r % 2, c * 512:(c + 1) * 512], PS[:, 4 + n % 4, :], ACT.Copy,
                               scale=float(QK) ** -0.5).then_inc(s["scores_copied"], 1)
            for n in range(2):
                act.wait_ge(s["xgtok_in_psum"], n + 1)
                act.copy(xg[:, 4 * n:4 * n + 4, :], PS[:, n, :].rearrange("p (t d) -> p t d", t=4))\
                    .then_inc(s["xgtok_copied"], 1)
            for n in range(2 * NG):
                act.wait_ge(s["bc_in_psum"], n + 1)
                act.copy(bc16[:, n // 2, :, (n % 2) * 2 * P:(n % 2 + 1) * 2 * P].rearrange("p a (c e) -> p c a e", c=2),
                         PS[:, 2 + n % 2, :].rearrange("p (c a e) -> p c a e", c=2, a=2)).then_inc(s["bc_copied"], 1)
            def w_high(n):
                act.wait_ge(s[f"wstage_loaded{n % 2}"], 32 * (n // 2 + 1))
                w = n - 1 if n else E
                act.copy(wsp[:, w, 0:4:2, :], wraw[:, w, 1:4:2, :]).then_inc(s["w_high"], 1)

            w_high(0)
            for g in range(NG):
                act.wait_ge(s["pairs_in_psum"], g + 1)
                act.activation(qkrest[:, g % 2].rearrange("p t a d -> p (t a d)"), PS[:, 4 + 2 * (g % 2), 0:GE * QK],
                               ACT.Copy, scale=float(QK) ** -0.5).then_inc(s["q_picked"], 1)
            for n in range(1, W_EARLY):
                w_high(n)
            act.wait_ge(s["alpha_neg"], 1)
            act.activation(aexp, araw, ACT.Exp, bias=aneg, accum_out=asum).then_inc(s["alpha_exped"], 1)

            def gate(T):
                act.wait_ge(s["xl_ready"], T + 1)
                act.activation(sw[:], xl[:], ACT.Tanh, scale=0.5).then_inc(s["th_done"], 1)
                act.wait_ge(s["th_done"], T + 1)
                act.activation(sw[:], sw[:], ACT.Square, scale=-0.5, bias=half_sb).then_inc(s["sw_ready"], 1)

            def x2T_copy(T):
                act.wait_ge(s["x2T_in_psum"], T + 1)
                act.copy(x2T[:], PS[:, 7, :]).then_inc(s["x2T_copied"], 1)

            def shares(T):
                act.wait_ge(s["gap_ready"], T + 1)
                act.activation(share[:, 0, :], gap[:], ACT.Tanh, scale=0.5).then_inc(s["share_ready"], 1)

            def cT_copy(T, slot):
                act.wait_ge(s["cT_in_psum"], T + 1)
                act.copy(cT_r[:, slot, :], PS[0:2 * E, 6, :]).then_inc(s["cT_copied"], 1)

            def expert_steps(T, slot, first, last):
                for k in range(K9):
                    m = step(T, k)
                    w = k - 1 if k else E
                    if first and 1 <= k <= K9 - W_EARLY:
                        w_high(W_EARLY - 1 + k)
                    if k == 2:
                        cb_copy(T, 1)
                    for f in range(FC):
                        act.wait_ge(s["h_in_psum"], m * FC + f + 1)
                        after(act, s[f"low_done{f}"], m)
                        bias = colsT[:, w * FC + f:w * FC + f + 1]
                        if f < HIGH_BY_ACT:
                            act.activation(g32[:, f, :], PS[:, f, :], ACT.Gelu, bias=bias)
                            after(act, s["y_in_psum"], m - 1)
                            act.activation(ghl[:, (slot + k) % 2, f, 0, :], PS[:, f, :], ACT.Gelu, bias=bias)\
                                .then_inc(s[f"high_done{f}"], 1)
                        else:
                            act.activation(g32[:, f, :], PS[:, f, :], ACT.Gelu, bias=bias)\
                                .then_inc(s[f"gelu_done{f}"], 1)
                    if k >= 2:
                        cb_copy(T, k)
                    if k == 0:
                        shares(T)
                    if k == 1:
                        cT_copy(T, slot)
                    if k == 4 and not first:
                        result_norm(T - 1)
                    if not last:
                        if k == 1:
                            gate(T + 1)
                        if k == 7:
                            x2T_copy(T + 1)

            def result_norm(T):
                act.wait_ge(s["result_stats"], T + 1)
                after(act, s["out_stored"], T * 16)
                for t in range(CH):
                    i = act.activation(fin[:, t, :], PS[:, 7, t * P:(t + 1) * P], ACT.Identity,
                                       bias=shift[:, t:t + 1], scale=newton[:, 1, t:t + 1])
                i.then_inc(s["fin_normed"], 1)

            def cb_copy(T, k):
                act.wait_ge(s["cb_in_psum"], T * E + k)
                after(act, s["y_used"], step(T, k - 2) + 1 if k > 2 else step(T, 0))
                act.copy(cb[:, k % 2, :], PS[:, 6, :]).then_inc(s["cb_copied"], 1)

            gate(0)
            x2T_copy(0)
            over_chunks(act, NT // CH, expert_steps)
            result_norm(NT // CH - 1)

        @block.vector
        def _(dve):
            ds = Chain(dve, s["dve_step"])
            for k, eps in enumerate((EPS, 0.5)):
                dve.memset(eps_sb[:, k:k + 1], eps).then_inc(s["eps_made"], 1)
            ds.mark(dve.memset(taps_pad[:], 0.0))
            dve.memset(wqk_sb[:, :, QK:P], 0.0).then_inc(s["wqk_padded"], 1)

            def pad_taps():
                dve.wait_ge(s["taps_loaded"], 16)
                dve.tensor_copy(taps_pad[:, WIN - 1:WIN - 1 + TAPS], taps_sb[:, ::-1]).then_inc(s["taps_padded"], 1)

            norms = [0]

            def layernorm(src, dst, n, ready):
                for t in range(n):
                    ds.mark(dve.bn_stats(stats[:, t, :], src(t)))
                ds.wait()
                for t in range(n):
                    i = dve.bn_aggr(mv[:, t, :], stats[:, t, :])
                i.then_inc(s["var_ready"], 1)
                norms[0] += 1
                dve.wait_ge(s["std_ready"], norms[0])
                ds.done(dve.reciprocal(rstd[:, 0:n], rstd[:, 0:n]))
                for t in range(n):
                    dve.tensor_scalar(dst(t), src(t), mv[:, t, 0:1], rstd[:, t:t + 1], ALU.subtract, ALU.mult)\
                        .then_inc(ready, 1)

            def batch_norm(b):
                dve.wait_ge(s[f"x_loaded{b}"], 16)
                layernorm(lambda t: x[:, b * TB + t, :], lambda t: X[:, b * TB + t, :], TB, s["Xn_ready"])

            def landmark_sums(b):
                dve.wait_ge(s["xT_copied"], 2 * (b + 1))
                dve.reduce_sum(lmT[:, b * LM:(b + 1) * LM],
                               xT[:, b * N:(b + 1) * N].rearrange("p (l m) -> p l m", m=N // LM), AX)\
                    .then_inc(s["lm_summed"], 1)

            for b in range(B):
                batch_norm(b)
                if b:
                    landmark_sums(b - 1)
                else:
                    pad_taps()
            landmark_sums(B - 1)
            dve.wait_ge(s["win_loaded"], 48)
            layernorm(lambda t: xw[:, t, :], lambda t: xw[:, t, :], NWIN, s["win_ready"])
            dve.wait_ge(s["ident_made"], 4)
            for k, c in enumerate((7.0, 15.0, 13.0)):
                ds.mark(dve.tensor_scalar(cI[:, k, :], ident[:], c, None, ALU.mult))

            dve.wait_ge(s["lscores_in_psum"], 2)
            ls = PS[:, 0, 0:(G + H) * LM].rearrange("p (a j) -> p a j", j=LM)
            ds.done(dve.reduce_max(mx10, ls, AX))
            dve.tensor_tensor(A2[:], ls, spread(mx10.unsqueeze(2), 2, LM), ALU.subtract).then_inc(s["lscores_read"], 1)
            dve.wait_ge(s["A2_exped"], 1)
            ds.done(dve.reduce_sum(sum10, A2e[:], AX))
            ds.done(dve.reciprocal(mx10, sum10))
            dve.tensor_tensor(A2[:], A2e[:], spread(mx10.unsqueeze(2), 2, LM), ALU.mult).then_inc(s["A2_ready"], 1)
            dve.wait_ge(s["A2_ready"], 1)
            for g in range(G):
                xb = dve.tensor_tensor(x_bd[:, g, :].rearrange("p (q j) -> p q j", j=LM),
                                       spread(A2[:, g:g + 1, :], 1, P // LM),
                                       blockones[:].rearrange("p (q j) -> p q j", j=LM), ALU.mult)
                xb.then_inc(s["xbd_ready"], 1)
            ds.done(dve.reduce_sum(rsum8, A2[:, G:G + H, :], AX))
            ds.mark(dve.reduce_max(lstat[:, 0:1], rsum8, AX))
            dve.wait_ge(s["colsum_in_psum"], 1)
            ds.done(dve.reduce_max(lstat[:, 1:2], PS[:, 0, 256:512], AX))
            dve.engine_nop().then_inc(s["landstats_ready"], 1)
            dve.wait_ge(s["landstats_max"], 1)
            ds.done(dve.tensor_tensor(sprod, lmax[:, 0:1], lmax[:, 1:2], ALU.mult))
            ds.done(dve.reciprocal(inv_s, sprod))
            dve.wait_ge(s["xbdT_in_psum"], 1)
            xTp = PS[:, 0, 0:256].rearrange("p (g n) -> p g n", g=G)
            dve.tensor_scalar(z[:], xTp, inv_s, None, ALU.mult).then_inc(s["z_ready"], 1)
            dve.tensor_copy(xT_bd[:], xTp).then_inc(s["z_ready"], 1)
            dve.tensor_scalar(zT[:], x_bd[:], inv_s, None, ALU.mult).then_inc(s["z_ready"], 1)

            def l3_maximum(g):
                dve.wait_ge(s["l3_in_psum"], 2 * g + 2)
                ds.done(dve.tensor_reduce(mx3[:, g:g + 1], PS[:, 3 + 2 * g:5 + 2 * g, :].rearrange("p a n -> p (a n)"),
                                          AX, ALU.max))
                dve.tensor_scalar(neg3[:, g:g + 1], mx3[:, g:g + 1], -1.0, None, ALU.mult).then_inc(s["l3_max"], 1)

            def l1_shift(n):
                dve.wait_ge(s["l1_in_psum"], n + 1)
                v = PS[:, 3 + n, :].rearrange("p (a j) -> p a j", j=LM)
                ds.done(dve.reduce_max(l1mx[:, 2 + n % 2, :], v, AX))
                dve.tensor_tensor(A1[:, 2 * n:2 * n + 2, :].rearrange("p t (h j) -> p (t h) j", j=LM), v,
                                  spread(l1mx[:, 2 + n % 2, :].unsqueeze(2), 2, LM), ALU.subtract)\
                    .then_inc(s["l1_shifted"], 1)

            def l1_norm(n):
                dve.wait_ge(s["l1_exped"], n + 1)
                v = A1[:, 2 * n:2 * n + 2, :].rearrange("p t (h j) -> p (t h) j", j=LM)
                ds.done(dve.reduce_sum(l1mx[:, 0, :], v, AX))
                ds.done(dve.reciprocal(l1mx[:, 1, :], l1mx[:, 0, :]))
                dve.tensor_tensor(v, v, spread(l1mx[:, 1, :].unsqueeze(2), 2, LM), ALU.mult)\
                    .then_inc(s["l1_ready"], 1)
                dve.wait_ge(s["l1_ready"], n + 1)

            for stage in range(STAGES):
                it, st = divmod(stage, 4)
                if st < 3:
                    if st == 0:
                        dve.wait_ge(s["pinv_p_in_psum"], it + 1)
                        src = PS[:, 0, 0:256]
                    else:
                        dve.wait_ge(s["pinv_t2_in_psum"], 2 * it + st)
                        src = PS[:, 0, (st % 2) * 256:(st % 2) * 256 + 256]
                    dve.scalar_tensor_tensor(tt[:, st, :, :], src.rearrange("p (g n) -> p g n", g=G), -1.0,
                                             spread(cI[:, st:st + 1, :], 1, G), ALU.mult, ALU.add)\
                        .then_inc(s["pinv_t_ready"], 1)
                else:
                    dve.wait_ge(s["pinv_z_in_psum"], it + 1)
                    dve.tensor_scalar(z[:], PS[:, 0, 256:512].rearrange("p (g n) -> p g n", g=G), 0.25, None, ALU.mult)\
                        .then_inc(s["pinv_z_ready"], 1)
                for n in beside["l3"][stage]:
                    l3_maximum(n)
                for n in beside["l1"][stage]:
                    l1_shift(n)
                if stage >= 2:
                    for n in beside["l1"][stage - 2]:
                        l1_norm(n)
                if stage == 4:
                    dve.wait_ge(s["l3_exped"], G)
                    ds.done(dve.reciprocal(rec3, sum3))
            dve.wait_ge(s["u_in_psum"], 1)
            for g in range(G):
                dve.tensor_scalar(U_sb[:, g, :], PS[:, 4, g * P:(g + 1) * P], rec3[:, g:g + 1], None, ALU.mult)\
                    .then_inc(s["u_copied"], 1)
            for c in range(2):
                dve.wait_ge(s["xg_in_psum"], c + 1)
                dve.tensor_scalar(xgT[:, c * 512:(c + 1) * 512], PS[:, 5 + c, :], colsT[:, OUTB:OUTB + 1], None, ALU.add)\
                    .then_inc(s["xgT_ready"], 1)
                dve.wait_ge(s["xgT_ready"], c + 1)
                dve.tensor_tensor(encT[:, c * 512:(c + 1) * 512], xgT[:, c * 512:(c + 1) * 512],
                                  xT[:, c * 512:(c + 1) * 512], ALU.add).then_inc(s["encT_ready"], 1)
            dve.wait_ge(s["edges_loaded"], 96)
            e = slice(KE, EC)
            ds.done(dve.tensor_scalar(r_i[:, 0, e], rows_i[:, e], LOG_N, None, ALU.logical_shift_left))
            dve.tensor_tensor(idx[:, e], r_i[:, 0, e], cols_i[:, e], ALU.add).then_inc(s["idx_ready"], 1)
            dve.wait_ge(s["idx_ready"], 1)
            for dst, src in ((r_i[:, :, e], rows_i[:, e]), (ekrow_i, ek_i[:, 0, :])):
                ds.mark(dve.tensor_scalar(dst[:, 0, :], src, P - 1, None, ALU.bitwise_and))
                ds.done(dve.tensor_scalar(dst[:, 1, :], src, P.bit_length() - 1, None, ALU.logical_shift_right))
            ds.mark(dve.tensor_copy(r_f[:, :, e], r_i[:, :, e]))
            ds.mark(dve.tensor_copy(ident_r[:], ident[0:KE, 0:KE]))
            ds.mark(dve.tensor_copy(ek_r[:], ek_i[:]))
            ds.done(dve.tensor_copy(ekrow[:, 0:2, :], ekrow_i[:]))
            dve.engine_nop().then_inc(s["ek_ready"], 1)
            for n in range(TB // 2):
                dve.wait_ge(s["qkt_in_psum"], n + 1)
                if n:
                    dve.wait_ge(s["qkp_ready"], n)
                src = PS[:, n, 0:4 * QK].rearrange("p (t a d) -> p t a d", t=2, a=2)
                dst = qkp[:, :, 2 * n:2 * n + 2, :, :]
                ds.done(dve.tensor_copy(dst[:, 0], src))
                dve.tensor_tensor(qkrest[:, 0], src, dst[:, 0], ALU.subtract).then_inc(s["qkp_split"], 1)
                dve.wait_ge(s["qkp_split"], n + 1)
                ds.done(dve.tensor_copy(dst[:, 1], qkrest[:, 0]))
                ds.done(dve.tensor_tensor(qkrest[:, 1], qkrest[:, 0], dst[:, 1], ALU.subtract))
                dve.tensor_copy(dst[:, 2], qkrest[:, 1]).then_inc(s["qkp_ready"], 1)
            dve.wait_ge(s["ekT_in_psum"], 1)
            ds.mark(dve.tensor_copy(r_f[:, :, 0:KE], PS[:, 0, 4 * QK:4 * QK + 2 * KE].rearrange("p (a k) -> p a k", a=2)))
            ds.done(dve.tensor_copy(vals_sb[:, 0:KE], PS[:, 0, 4 * QK + 2 * KE:4 * QK + 3 * KE]))
            dve.engine_nop().then_inc(s["ekT_copied"], 1)
            dve.wait_ge(s["xgtok_copied"], 2)
            for b in range(B):
                dve.tensor_tensor(X[:, tiles_of(b), :], X[:, tiles_of(b), :], xg[:], ALU.add).then_inc(s["enc_ready"], 1)
            for c in range(NT // CH):
                dve.wait_ge(s["value_in_psum"], c + 1)
                dve.tensor_tensor(value[:, c * CW:(c + 1) * CW].rearrange("p (t d) -> p t d", t=CH),
                                  PS[:, 4 + c % 4, :].rearrange("p (t d) -> p t d", t=CH),
                                  spread(wvb_sb[:].unsqueeze(1), 1, CH), ALU.add).then_inc(s["value_ready"], 1)
            ln = Drained(dve)

            def pick(g, slot):
                for kind in range(2):
                    for t in range(TB):
                        i = dve.tensor_scalar(oht[:, slot, kind, t:t + 1, :], bc16[:, bass.ds(g, 1), kind, :],
                                              iota_col[:, t:t + 1], None, ALU.is_equal)
                i.then_inc(s["oht_ready"], 1)

            def dots(g, slot):
                dve.wait_ge(s["q_picked"], g + 1)
                ln.done(dve.tensor_tensor(qkprod[:], qkrest[:, slot].rearrange("p t a d -> p (t a) d"),
                                          PS[:, 5 + 2 * slot, 0:GE * QK].rearrange("p (c d) -> p c d", c=GE), ALU.mult)
                        .then_inc(s["dots_done"], 1))
                dve.reduce_sum(gathered[:, bass.ds(g * GE, GE)], qkprod[:], AX)
                dve.drain()

            QUARTER = EC // 4

            def row_onehots(q):
                j = bass.ds(q * QUARTER, QUARTER)
                dve.tensor_tensor(onehot[:, j, :], spread(iota_row[:].unsqueeze(1), 1, QUARTER),
                                  spread(r_f[:, 0, j].unsqueeze(2), 2, P), ALU.is_equal).then_inc(s["onehot_ready"], 1)

            dve.wait_ge(s["bc_copied"], 4)
            pick(0, 0)
            pick(1, 1)
            dve.wait_ge(s["bc_copied"], 2 * NG)
            for k in range(2):
                dve.wait_ge(s[f"scores_stored{k}"], 16 * TB // 2)
            with dve.Fori(0, NG // 2 - 1) as it:
                for slot in range(2):
                    dots(it * 2 + slot, slot)
                    pick(it * 2 + slot + 2, slot)
                row_onehots(it)
            dots(NG - 2, 0)
            dots(NG - 1, 1)
            dve.engine_nop().then_inc(s["picks_over"], 1)
            row_onehots(NG // 2 - 1)
            def w_low(n):
                dve.wait_ge(s["w_high"], n + 1)
                w = n - 1 if n else E
                for k in range(2):
                    dve.tensor_tensor(wsp[:, w, 2 * k + 1, :], wraw[:, w, 2 * k + 1, :], wsp[:, w, 2 * k, :],
                                      ALU.subtract).then_inc(s["w_low"], 1)

            w_low(0)
            ds.done(dve.tensor_tensor(oh8[:], spread(iota_row[:, 0:TB].unsqueeze(1), 1, EC),
                                      spread(r_f[:, 1, :].unsqueeze(2), 2, TB), ALU.is_equal))
            for half, (a, b_) in enumerate(((0, EC0), (EC0, EC))):
                if half:
                    for n in range(1, W_EARLY):
                        w_low(n)
                dve.wait_ge(s[f"gathered{half}"], 16 * (b_ - max(a, KE)))
                e = slice(a, b_)
                ds.done(dve.tensor_tensor(gathered[:, e], gathered[:, e], vals_sb[:, e], ALU.mult))
                ds.done(dve.tensor_copy(parts[:, 0, e], gathered[:, e]))
                ds.done(dve.tensor_tensor(rest[:, 0, e], gathered[:, e], parts[:, 0, e], ALU.subtract))
                ds.done(dve.tensor_copy(parts[:, 1, e], rest[:, 0, e]))
                ds.done(dve.tensor_tensor(rest[:, 1, e], rest[:, 0, e], parts[:, 1, e], ALU.subtract))
                ds.done(dve.tensor_copy(parts[:, 2, e], rest[:, 1, e]))
                for k in range(3):
                    dve.tensor_tensor(rhs3[:, e, k, :], oh8[:, e, :], spread(parts[:, k, e].unsqueeze(2), 2, TB), ALU.mult)\
                        .then_inc(s["rhs3_ready"], 1)
            dve.wait_ge(s["araw_in_psum"], 1)
            ds.done(dve.reduce_sum(araw, PS[:, 0, 0:3 * TB].rearrange("p (k t) -> p t k", k=3), AX))
            dve.reduce_max(amx, araw, AX).then_inc(s["araw_max"], 1)
            dve.wait_ge(s["araw_maxed"], 1)
            dve.tensor_scalar(aneg, amx_all, -1.0, None, ALU.mult).then_inc(s["alpha_neg"], 1)
            dve.wait_ge(s["alpha_summed"], 1)
            ds.done(dve.reciprocal(arec, asum_all))
            dve.tensor_scalar(alpha[:], aexp, arec, None, ALU.mult).then_inc(s["alpha_ready"], 1)

            def moments(src, half):
                for t in range(CH):
                    i = dve.bn_stats(st6[:, t, :], src[:, t, :])
                ln.done(i)
                for t in range(CH):
                    i = dve.bn_aggr(mv4[:, half * CH + t, :], st6[:, t, :])
                ln.done(i)

            def rsqrt(eps0, eps1=None):
                halves = [h for h, e in enumerate((eps0, eps1)) if e is not None]
                cut = slice(halves[0] * CH, (halves[-1] + 1) * CH)
                v, r, t, u = (newton[:, i, cut] for i in range(4))
                for h in halves:
                    c = slice(h * CH, (h + 1) * CH)
                    i = dve.tensor_scalar(newton[:, 0, c], mv4[:, c, 1], (eps0, eps1)[h], None, ALU.add)
                ln.done(i)
                ln.done(dve.tensor_scalar(guess[:, cut], v.bitcast(I32), 1, None, ALU.logical_shift_right))
                ln.done(dve.tensor_scalar(r.bitcast(I32), guess[:, cut], -1.0, float(0x5F3759DF), ALU.mult, ALU.add))

            def newton_steps(cut, n):
                v, r, t, u = (newton[:, i, cut] for i in range(4))
                for _ in range(n):
                    ln.done(dve.tensor_tensor(t, r, r, ALU.mult))
                    ln.done(dve.scalar_tensor_tensor(u, t, -0.5, v, ALU.mult, ALU.mult))
                    ln.done(dve.scalar_tensor_tensor(r, u, 1.5, r, ALU.add, ALU.mult))

            OTHER = slice(CH, 2 * CH)

            def normed(src, dst, half):
                for t in range(CH):
                    a = half * CH + t
                    i = dve.tensor_scalar(dst[:, t, :], src[:, t, :], mv4[:, a, 0:1], newton[:, 1, a:a + 1],
                                          ALU.subtract, ALU.mult)
                return i

            ffn_result = PS[:, 7, :].rearrange("p (t d) -> p t d", t=CH)

            def result_moments(T):
                dve.wait_ge(s["accT_in_psum"], T + 1)
                moments(ffn_result, 0)

            def result_stats():
                dve.scalar_tensor_tensor(shift[:], mv4[:, 0:CH, 0], -1.0, newton[:, 1, 0:CH], ALU.mult, ALU.mult)\
                    .then_inc(s["result_stats"], 1)

            def mix_moments(T):
                dve.wait_ge(s["mixed"], T + 1)
                moments(yy, 1)

            def mix_normed():
                normed(yy, yy, 1).then_inc(s["mix_normed"], 1)

            def x1_moments(T, slot):
                dve.wait_ge(s["x1_ready"], T + 1)
                moments(x1[:, slot, :, :], 1)
                rsqrt(None, EPS)
                newton_steps(OTHER, 2)

            def x1_normed(slot):
                newton_steps(OTHER, 1)
                normed(x1[:, slot, :, :], yy, 1).then_inc(s["x2_ready"], 1)

            def x2_split(T, slot):
                dve.wait_ge(s["x2T_copied"], T + 1)
                ln.done(dve.tensor_copy(x2hl[:, slot, 0, :], x2T[:]))
                dve.tensor_tensor(x2hl[:, slot, 1, :], x2T[:], x2hl[:, slot, 0, :], ALU.subtract)\
                    .then_inc(s["x2_split"], 1)

            def route(T):
                dve.wait_ge(s["logits_in_psum"], T + 1)
                ln.done(dve.tensor_copy(logit[:], PS[:, 7, 0:CH * E].rearrange("p (t e) -> p t e", t=CH)))
                for t in range(CH):
                    i = dve.max(top[:, t, :], logit[:, t, :])
                ln.done(i)
                dve.tensor_tensor(gap[:], top[:, :, 1], top[:, :, 0], ALU.subtract).then_inc(s["gap_ready"], 1)
                for t in range(CH):
                    i = dve.max_index(topi[:, t, :], top[:, t, :], logit[:, t, :])
                ln.done(i)
                ln.done(dve.tensor_copy(topf[:], topi[:]))
                ln.done(dve.tensor_tensor(hot[:],
                                          spread(spread(iota_row[:, 0:E].unsqueeze(1).unsqueeze(1), 1, 2), 2, CH),
                                          spread(topf[:, :, 0:2].rearrange("p t k -> p k t").unsqueeze(3), 3, E),
                                          ALU.is_equal))

            def combine(T):
                dve.wait_ge(s["share_ready"], T + 1)
                for k in range(2):
                    i = dve.tensor_scalar(share[:, 1 + k, :], share[:, 0, :], (-0.5, 0.5)[k], 0.5, ALU.mult, ALU.add)
                ln.done(i)
                ln.done(dve.tensor_tensor(hot[:], hot[:], spread(share[:, 1:3, :].unsqueeze(3), 3, E), ALU.mult))
                ln.done(dve.tensor_tensor(comb[:], hot[:, 0, :, :], hot[:, 1, :, :], ALU.add))
                ln.done(dve.tensor_copy(c16[:, :, 0:E], comb[:]))
                dve.tensor_tensor(c16[:, :, E:2 * E], comb[:], c16[:, :, 0:E], ALU.subtract).then_inc(s["c16_ready"], 1)

            def split(T, slot, k):
                m = step(T, k)
                g = (slot + k) % 2
                for f in range(HIGH_BY_ACT, FC):
                    dve.wait_ge(s[f"gelu_done{f}"], m + 1)
                    if f == HIGH_BY_ACT:
                        after(dve, s["y_in_psum"], m - 1)
                    i = dve.tensor_copy(ghl[:, g, f, 0, :], g32[:, f, :])
                ln.done(i)
                for f in range(low_by_pool(k), FC):
                    if f < HIGH_BY_ACT:
                        dve.wait_ge(s[f"high_done{f}"], m + 1)
                    dve.tensor_tensor(ghl[:, g, f, 1, :], g32[:, f, :], ghl[:, g, f, 0, :], ALU.subtract)\
                        .then_inc(s[f"low_done{f}"], 1)

            def reduce_expert(T, slot, k):
                m = step(T, k)
                dve.wait_ge(s["y_in_psum"], m + 1)
                y = PS[:, 4 + (slot + k) % 2, :]
                if k == 0:
                    after(dve, s["accT_in_psum"], T - 1)
                    dve.tensor_scalar(acc[:, slot, :], y, colsT[:, SB2:SB2 + 1], None, ALU.add).then_inc(s["y_used"], 1)
                else:
                    dve.wait_ge(s["cb_copied"], T * E + k)
                    after(dve, s["prod_added"], T * E + k - 2)
                    dve.scalar_tensor_tensor(prod[:, k % 2, :], y, colsT[:, B2 + k - 1:B2 + k], cb[:, k % 2, :],
                                             ALU.add, ALU.mult).then_inc(s["y_used"], 1)

            def expert_steps(T, slot, first, last):
                for k in range(K9):
                    if first and 1 <= k <= K9 - W_EARLY:
                        w_low(W_EARLY - 1 + k)
                    split(T, slot, k)
                    if k:
                        reduce_expert(T, slot, k - 1)
                    elif not first:
                        reduce_expert(T - 1, 1 - slot, K9 - 1)
                    if k == 0:
                        combine(T)
                    if k == 1 and not first:
                        result_moments(T - 1)
                    if k == 2:
                        if not last:
                            mix_moments(T + 1)
                        rsqrt(None if first else EPS, None if last else EPS / 4)
                        newton_steps(slice(CH if first else 0, CH if last else 2 * CH), 1)
                    if k == 3:
                        newton_steps(slice(CH if first else 0, CH if last else 2 * CH), 2)
                        if not last:
                            mix_normed()
                        if not first:
                            result_stats()
                    if not last:
                        if k == 5:
                            x1_moments(T + 1, 1 - slot)
                        if k == 6:
                            x1_normed(1 - slot)
                        if k == 7:
                            x2_split(T + 1, 1 - slot)
                        if k == 8:
                            route(T + 1)

            dve.wait_ge(s["alpha_ready"], 1)
            dve.tensor_tensor(xl[:], value[:, 0:CW].rearrange("p (t d) -> p t d", t=CH),
                              spread(alpha[:, 0:CH].unsqueeze(2), 2, P), ALU.mult).then_inc(s["xl_ready"], 1)
            dve.wait_ge(s["xl_ready"], 1)
            ln.done(dve.tensor_tensor(yy[:], xl[:], X[:, 0:CH, :], ALU.subtract))
            dve.wait_ge(s["sw_ready"], 1)
            ln.done(dve.tensor_tensor(yy[:], yy[:], sw[:], ALU.mult))
            dve.tensor_tensor(yy[:], yy[:], X[:, 0:CH, :], ALU.add).then_inc(s["mixed"], 1)
            mix_moments(0)
            rsqrt(None, EPS / 4)
            newton_steps(OTHER, 3)
            mix_normed()
            dve.wait_ge(s["mix_normed"], 1)
            dve.tensor_tensor(x1[:, 0, :, :], yy[:], x[:, 0:CH, :], ALU.add).then_inc(s["x1_ready"], 1)
            x1_moments(0, 0)
            x1_normed(0)
            x2_split(0, 0)
            route(0)
            over_chunks(dve, NT // CH, expert_steps)
            reduce_expert(NT // CH - 1, 1, K9 - 1)
            result_moments(NT // CH - 1)
            rsqrt(EPS)
            newton_steps(slice(0, CH), 3)
            result_stats()

        @block.tensor
        def _(pe):
            pe.wait_ge(s["ident_made"], 1)
            def xT_group(g):
                pe.wait_ge(s["Xn_ready"], CH * (g + 1))
                if g >= 4:
                    pe.wait_ge(s["xT_copied"], g - 3)
                for t in range(CH):
                    m = pe.transpose(PS[:, 3 + g % 4, t * P:(t + 1) * P], X[:, g * CH + t, :], ident[:])
                m.then_inc(s["xT_in_psum"], 1)

            xT_group(0)
            xT_group(1)
            pe.wait_ge(s["qkvw_loaded"], 16)
            for k in range(3):
                for c in range(4):
                    m = pe.transpose(PS[:, k, c * P:(c + 1) * P], qkvw[:, (4 * k + c) * P:(4 * k + c + 1) * P], ident[:])
                m.then_inc(s["wT_in_psum"], 1)
            pe.wait_ge(s["wo_loaded"], 16)
            pe.wait_ge(s["wT_copied"], 3)
            for h in range(H):
                r = slice(DH * (h % 2), DH * (h % 2) + DH)
                m = pe.matmul(PS[:, h % 2, (h // 2) * P:(h // 2 + 1) * P], wT[r, 2, h // 2, :], wo_sb[r, h // 2, :],
                              start=True, stop=True)
                if h >= H - 2:
                    m.then_inc(s["vo_in_psum"], 1)
            for g in range(2, NT // CH):
                xT_group(g)
                if g == 5:
                    pe.wait_ge(s["band_loaded"], 16)
                    pe.wait_ge(s["ident_made"], 5)
                    for k in range(2):
                        pe.matmul(PS[:, (2, 7)[k], 0:4 * WIN], flip[:], band[:, 4 * k:4 * k + 4, :], start=True, stop=True)\
                            .then_inc(s["toep_in_psum"], 1)
            pe.wait_ge(s["toep_copied"], 2)
            pe.wait_ge(s["rows_in_loaded"], 96)
            pe.transpose(PS[:, 7, 0:NCOL], rows_in[:], ident[0:NCOL, 0:NCOL]).then_inc(s["cols_in_psum"], 1)
            pe.wait_ge(s["lm_summed"], B)
            pe.wait_ge(s["cols_copied"], 1)
            for k in range(2):
                for c in range(4):
                    m = pe.matmul(PS[:, (2, 7)[k], c * P:(c + 1) * P], qkvw[:, (4 * k + c) * P:(4 * k + c + 1) * P],
                                  lmT[:], start=True, stop=True)
                m.then_inc(s["ql_in_psum"], 1)
            pe.wait_ge(s["ql_copied"], 2)
            pe.wait_ge(s["vo_copied"], 2)
            for odd in range(2):
                r = slice(DH * odd, DH * odd + DH)
                for h in range(odd, H, 2):
                    q, c = h % 4, h // 2
                    pe.matmul(PS[q * LM:(q + 1) * LM, 0, (h // 4) * LM:(h // 4 + 1) * LM], qlT[r, c, 0:LM],
                              klT[r, c, 0:LM], start=True, stop=True)
                    for b in range(B):
                        m = pe.matmul(PS[b * LM:(b + 1) * LM, 0, (G + h) * LM:(G + h + 1) * LM],
                                      qlT[r, c, b * LM:(b + 1) * LM], klT[r, c, b * LM:(b + 1) * LM],
                                      start=True, stop=True)
                m.then_inc(s["lscores_in_psum"], 1)
                if not odd:
                    pe.wait_ge(s["lscores_in_psum"], 1)
            for odd in range(2):
                r = slice(DH * odd, DH * odd + DH)
                for k, l in enumerate((klT, qlT)):
                    for h in range(odd, H, 2):
                        m = pe.matmul(PS[:, 1, (k * H + h) * LM:(k * H + h + 1) * LM], wT[r, k, h // 2, :],
                                      l[r, h // 2, 0:LM], start=True, stop=True)
                m.then_inc(s["g_in_psum"], 1)
                if not odd:
                    pe.wait_ge(s["g_in_psum"], 1)
            pe.wait_ge(s["xbd_ready"], G)
            for g in range(G):
                m = pe.transpose(PS[:, 0, g * P:(g + 1) * P], x_bd[:, g, :], ident[:])
            m.then_inc(s["xbdT_in_psum"], 1)
            pe.wait_ge(s["ident_made"], 2)
            pe.wait_ge(s["A2_ready"], 1)
            pe.matmul(PS[:, 0, 256:512], blockones[:], A2[:, G:G + H, :].rearrange("p h j -> p (h j)"),
                      start=True, stop=True).then_inc(s["colsum_in_psum"], 1)
            def l3_step(g):
                for c in range(2):
                    pe.matmul(PS[:, 3 + 2 * g + c, :], Gq[:, 1, g * P:(g + 1) * P], xT[:, c * 512:(c + 1) * 512],
                              start=True, stop=True).then_inc(s["l3_in_psum"], 1)

            def conv_step(n):
                w, hh = n // 2, n % 2
                if n == 0:
                    pe.wait_ge(s["win_ready"], NWIN)
                    pe.wait_ge(s["toep_copied"], 2)
                if n >= 2:
                    pe.wait_ge(s["conv_copied"], n - 1)
                pe.matmul(PS[:, (2, 7)[n % 2], 0:4 * WIN], xw[:, w, :], toep[:, 4 * hh:4 * hh + 4, :],
                          start=True, stop=True).then_inc(s["conv_in_psum"], 1)

            def l1_step(n):
                pe.wait_ge(s["l3_exped"], n // 2 + 1)
                for t in range(2):
                    tile = 2 * n + t
                    m = pe.matmul(PS[:, 3 + n, t * 256:(t + 1) * 256], xT[:, tile * P:(tile + 1) * P], Gq[:, 0, :],
                                  start=True, stop=True)
                m.then_inc(s["l1_in_psum"], 1)

            def e3T_step(n):
                pe.wait_ge(s["conv_copied"], CONV - 1 + n if n < 2 else CONV)
                if n >= 2:
                    pe.wait_ge(s["e3T_copied"], n - 1)
                for t in range(2):
                    for g in range(G):
                        tile = 2 * n + t
                        m = pe.transpose(PS[:, (2, 7)[n % 2], (2 * t + g) * P:(2 * t + g + 1) * P],
                                         E3[:, g, tile * P:(tile + 1) * P], ident[:])
                m.then_inc(s["e3T_in_psum"], 1)

            def a1T_step(n):
                pe.wait_ge(s["e3T_copied"], min(n + 3, 4))
                if n >= 2:
                    pe.wait_ge(s["a1T_copied"], n - 1)
                pe.wait_ge(s["l1_ready"], 4)
                g, q = n // 2, n % 2
                for t in range(4):
                    m = pe.transpose(PS[:, (2, 7)[n % 2], t * P:(t + 1) * P], A1[:, 4 * q + t, g * P:(g + 1) * P], ident[:])
                m.then_inc(s["a1T_in_psum"], 1)

            def tT_step(n):
                if n == 0:
                    pe.wait_ge(s["e3T_copied"], 4)
                m = pe.matmul(PS[:, 3, 0:G * P], X[:, n, :], E3T[:, n, :], start=(n == 0), stop=(n == TB - 1))
                if n == TB - 1:
                    m.then_inc(s["tT_in_psum"], 1)

            def vo_step(n):
                c, h = divmod(n, H)
                if h == 0:
                    pe.wait_ge(s["l1_shifted"], 3 + c)
                    pe.wait_ge(s["conv_copied"], CONV if c else 2 * -(-512 // WIN))
                pe.matmul(PS[:, 5 + c, :], VO[:, h, :], YT[:, h, c * 512:(c + 1) * 512], start=(h == 0), stop=False)

            for n in range(CONV_EARLY):
                conv_step(n)
            pe.wait_ge(s["g_copied"], 1)
            pe.wait_ge(s["z_ready"], 3)
            for stage in range(STAGES):
                it, st = divmod(stage, 4)
                if st == 0:
                    if it:
                        pe.wait_ge(s["pinv_z_ready"], it)
                        pe.wait_ge(s["zT_copied"], it)
                    for g in range(G):
                        pe.matmul(PS[:, 0, g * P:(g + 1) * P], xT_bd[:, g, :], z[:, g, :], start=True, stop=True)
                    for g in range(G):
                        m = pe.matmul(PS[:, 1, g * P:(g + 1) * P], z[:, g, :], xT_bd[:, g, :],
                                      start=True, stop=True)
                    m.then_inc(s["pinv_p_in_psum"], 1)
                elif st < 3:
                    pe.wait_ge(s["pT_copied"], it + 1)
                    pe.wait_ge(s["pinv_t_ready"], 3 * it + st)
                    for g in range(G):
                        m = pe.matmul(PS[:, 0, (st % 2) * 256 + g * P:(st % 2) * 256 + (g + 1) * P], pT[:, g, :],
                                      tt[:, st - 1, g, :], start=True, stop=True)
                    m.then_inc(s["pinv_t2_in_psum"], 1)
                else:
                    pe.wait_ge(s["pinv_t_ready"], 3 * it + 3)
                    for g in range(G):
                        pe.matmul(PS[:, 0, 256 + g * P:256 + (g + 1) * P], zT[:, g, :], tt[:, 2, g, :], start=True, stop=True)
                    for g in range(G):
                        m = pe.matmul(PS[:, 1, 256 + g * P:256 + (g + 1) * P], tt[:, 2, g, :], zT[:, g, :],
                                      start=True, stop=True)
                    m.then_inc(s["pinv_z_in_psum"], 1)
                for n in beside["l3"][stage]:
                    l3_step(n)
                for n in beside["l1"][stage]:
                    l1_step(n)
                for n in beside["conv"][stage]:
                    conv_step(n)
                for n in beside["e3T"][stage]:
                    e3T_step(n)
                for n in beside["a1T"][stage]:
                    a1T_step(n)
                for n in beside["tT"][stage]:
                    tT_step(n)
                for n in beside["vo"][stage]:
                    vo_step(n)
            pe.wait_ge(s["tT_copied"], 1)
            for h in range(H):
                q = h % 4
                m = pe.matmul(PS[q * LM:(q + 1) * LM, 4, (h // 4) * P:(h // 4 + 1) * P], TT_sb[:, h * LM:(h + 1) * LM],
                              VO[:, h, :], start=True, stop=True)
            m.then_inc(s["u_in_psum"], 1)
            pe.wait_ge(s["u_copied"], G)
            pe.wait_ge(s["zT_copied"], PINV_ITERS)
            for g in range(G):
                m = pe.matmul(PS[:, 3, g * P:(g + 1) * P], zT[:, g, :], U_sb[:, g, :], start=True, stop=True)
            m.then_inc(s["n_in_psum"], 1)
            pe.wait_ge(s["n_copied"], 1)
            pe.wait_ge(s["a1T_copied"], 4)
            for c in range(2):
                for g in range(G):
                    m = pe.matmul(PS[:, 5 + c, :], N_sb[:, g, :], A1T[:, g, c * 512:(c + 1) * 512], start=False,
                                  stop=(g == G - 1))
                m.then_inc(s["xg_in_psum"], 1)
            pe.wait_ge(s["small_loaded"], 64)
            pe.wait_ge(s["wqk_padded"], 1)
            for k in range(2):
                for c in range(2):
                    pe.wait_ge(s["encT_ready"], c + 1)
                    pe.matmul(PS[:, 2 * k + c, :], wqk_sb[:, k, :], encT[:, c * 512:(c + 1) * 512],
                              start=True, stop=True).then_inc(s["qk_in_psum"], 1)
            pe.wait_ge(s["qk_copied"], 4)
            for n in range(NPIECE):
                r, c = n // 2, n % 2
                if n >= 4:
                    pe.wait_ge(s["scores_copied"], n - 3)
                pe.matmul(PS[:, 4 + n % 4, :], qkT[:, 0, r * P:(r + 1) * P], qkT[:, 1, c * 512:(c + 1) * 512],
                          start=True, stop=True).then_inc(s["scores_in_psum"], 1)
            pe.wait_ge(s["ek_ready"], 1)
            for k in range(3):
                m = pe.transpose(PS[:, 0, 4 * QK + k * KE:4 * QK + (k + 1) * KE], ekrow[:, k, :], ident[0:KE, 0:KE])
            m.then_inc(s["ekT_in_psum"], 1)
            for n in range(TB // 2):
                for t in range(2):
                    m = pe.matmul(PS[:, n, t * 2 * QK:(t + 1) * 2 * QK], encT[:, (2 * n + t) * P:(2 * n + t + 1) * P],
                                  wqk_sb[:, :, 0:QK], start=True, stop=True)
                m.then_inc(s["qkt_in_psum"], 1)
            pe.wait_ge(s["ekT_copied"], 1)
            for n in range(2):
                for t in range(4):
                    m = pe.transpose(PS[:, n, t * P:(t + 1) * P], xgT[:, (4 * n + t) * P:(4 * n + t + 1) * P], ident[:])
                m.then_inc(s["xgtok_in_psum"], 1)
            for n in range(2 * NG):
                if n < 2:
                    pe.wait_ge(s["qkp_split"], TB // 2 - 1 + n)
                else:
                    pe.wait_ge(s["bc_copied"], n - 1)
                for c in range(2):
                    k = 2 * n + c
                    m = pe.matmul(PS[:, 2 + n % 2, c * 2 * P:(c + 1) * 2 * P], spread(ident_r[:, k:k + 1], 1, P), ek_r[:],
                                  start=True, stop=True)
                m.then_inc(s["bc_in_psum"], 1)
            for c in range(NT // CH):
                pe.wait_ge(s["scores_copied"], NPIECE)
                if c >= 4:
                    pe.wait_ge(s["value_ready"], c - 3)
                for t in range(CH):
                    tile = c * CH + t
                    m = pe.matmul(PS[:, 4 + c % 4, t * P:(t + 1) * P], xT[:, tile * P:(tile + 1) * P], wv_sb[:],
                                  start=True, stop=True)
                m.then_inc(s["value_in_psum"], 1)
            def pairs(g, slot):
                pe.wait_ge(s["oht_ready"], g + 1)
                after(pe, s["dots_done"], g - 1)
                for c in range(GE):
                    for kind in range(2):
                        for t in range(TB):
                            for part in range(3):
                                m = pe.matmul(PS[:, 4 + 2 * slot + kind, c * QK:(c + 1) * QK],
                                              oht[:, slot, kind, t, c * P:(c + 1) * P], qkp[:, part, t, kind, :],
                                              start=(t == 0 and part == 0), stop=(t == TB - 1 and part == 2))
                m.then_inc(s["pairs_in_psum"], 1)

            pe.wait_ge(s["qkp_ready"], TB // 2)
            pe.wait_ge(s["value_ready"], NT // CH)
            pairs(0, 0)
            pairs(1, 1)
            with pe.Fori(0, NG // 2 - 1) as it:
                for slot in range(2):
                    pairs(it * 2 + slot + 2, slot)
            pe.wait_ge(s["onehot_ready"], 4)
            pe.wait_ge(s["xgtok_copied"], 2)
            for j in range(EC):
                if j in (0, EC0):
                    pe.wait_ge(s["rhs3_ready"], 6 if j else 3)
                m = pe.matmul(PS[:, 0, 0:3 * TB], onehot[:, j, :], rhs3[:, j, :, :].rearrange("p k t -> p (k t)"),
                              start=(j == 0), stop=(j == EC - 1))
            m.then_inc(s["araw_in_psum"], 1)
            pe.wait_ge(s["ident_made"], 4)

            def x2_transposes(T):
                pe.wait_ge(s["x2_ready"], T + 1)
                after(pe, s["fin_ready"], T - 1)
                for t in range(CH):
                    m = pe.transpose(PS[:, 7, t * P:(t + 1) * P], yy[:, t, :], ident[:])
                m.then_inc(s["x2T_in_psum"], 1)

            def logits(T):
                pe.wait_ge(s["x2T_copied"], T + 1)
                for t in range(CH):
                    m = pe.matmul(PS[:, 7, t * E:(t + 1) * E], x2T[:, t * P:(t + 1) * P], colsT[:, GATE:GATE + E],
                                  start=True, stop=True)
                m.then_inc(s["logits_in_psum"], 1)

            def c_transposes(T):
                pe.wait_ge(s["c16_ready"], T + 1)
                for t in range(CH):
                    m = pe.transpose(PS[0:2 * E, 6, t * P:(t + 1) * P], c16[:, t, :].bitcast(F32), ident[:])
                m.then_inc(s["cT_in_psum"], 1)

            def up(T, slot, k):
                w = k - 1 if k else E
                m = step(T, k)
                for f in range(FC):
                    after(pe, s[f"high_done{f}" if f < HIGH_BY_ACT else f"gelu_done{f}"], m)
                    cols_ = slice(f * P, (f + 1) * P)
                    pe.matmul(PS[:, f, :], wsp[:, w, 0, cols_], x2hl[:, slot, 0, :], start=True, stop=False)
                    pe.matmul(PS[:, f, :], wsp[:, w, 0, cols_], x2hl[:, slot, 1, :], start=False, stop=False)
                    pe.matmul(PS[:, f, :], wsp[:, w, 1, cols_], x2hl[:, slot, 0, :], start=False, stop=True)\
                        .then_inc(s["h_in_psum"], 1)

            def down(T, slot, k):
                w = k - 1 if k else E
                m = step(T, k)
                g = (slot + k) % 2
                bank = PS[:, 4 + g, :]
                after(pe, s["y_used"], m - 1)
                for f in range(FC):
                    pe.wait_ge(s[f"low_done{f}"], m + 1)
                    cols_ = slice(f * P, (f + 1) * P)
                    pe.matmul(bank, wsp[:, w, 2, cols_], ghl[:, g, f, 0, :], start=(f == 0), stop=False)
                    pe.matmul(bank, wsp[:, w, 2, cols_], ghl[:, g, f, 1, :], start=False, stop=False)
                    i = pe.matmul(bank, wsp[:, w, 3, cols_], ghl[:, g, f, 0, :], start=False, stop=(f == FC - 1))
                i.then_inc(s["y_in_psum"], 1)

            def acc_transposes(T, slot):
                pe.wait_ge(s["prod_added"], T * E + E)
                for t in range(CH):
                    m = pe.transpose(PS[:, 7, t * P:(t + 1) * P], acc[:, slot, t * P:(t + 1) * P], ident[:])
                m.then_inc(s["accT_in_psum"], 1)

            def expert_steps(T, slot, first, last):
                pe.wait_ge(s["x2_split"], T + 1)
                for k in range(K9):
                    if first:
                        pe.wait_ge(s["w_low"], 2 * (k + 1))
                    up(T, slot, k)
                    if k == 2:
                        spread_weights(T, slot, 1)
                    if k >= 3:
                        spread_weights(T, slot, k)
                    if not last:
                        if k == 8:
                            logits(T + 1)
                    if k:
                        down(T, slot, k - 1)
                    elif not first:
                        down(T - 1, 1 - slot, K9 - 1)
                    if k == 7 and not last:
                        x2_transposes(T + 1)
                    if k == 1:
                        c_transposes(T)
                    if k == 2:
                        spread_weights(T, slot, 2)
                    if k == 1 and not first:
                        acc_transposes(T - 1, 1 - slot)

            def spread_weights(T, slot, k):
                pe.wait_ge(s["cT_copied"], T + 1)
                after(pe, s["cb_copied"], T * E + k - 1)
                pe.matmul(PS[:, 6, :], sel_r[:, k - 1, :], cT_r[:, slot, :], start=True, stop=True)\
                    .then_inc(s["cb_in_psum"], 1)

            x2_transposes(0)
            logits(0)
            over_chunks(pe, NT // CH, expert_steps)
            down(NT // CH - 1, 1, K9 - 1)
            acc_transposes(NT // CH - 1, 1)


_INS = ['L0_attn_dense', 'L0_attn_adj_rows', 'L0_attn_adj_cols', 'L0_attn_adj_vals', 'L0_attn_wq', 'L0_attn_wk',
        'L0_attn_wv_w', 'L0_attn_wv_b', 'L0_attn_qkv_w', 'L0_attn_out_w', 'L0_attn_out_b', 'L0_attn_conv_w',
        'L0_ffn_gate_w', 'L0_ffn_W1', 'L0_ffn_b1', 'L0_ffn_W2', 'L0_ffn_b2', 'L0_ffn_sW1', 'L0_ffn_sb1',
        'L0_ffn_sW2', 'L0_ffn_sb2']


def kernel(**inputs):
    import numpy as _np
    import concourse.bacc as _bacc
    from concourse import mybir as _mybir
    from concourse.bass_utils import run_bass_kernel_spmd as _run

    nc = _bacc.Bacc("TRN2", target_bir_lowering=False, num_devices=1)
    arrays, args = {}, []
    for name in _INS:
        a = _np.ascontiguousarray(inputs[name])
        arrays[f"in_{name}_dram"] = a
        args.append(nc.dram_tensor(f"in_{name}_dram", a.shape, _mybir.dt.from_np(a.dtype), kind="ExternalInput").ap())
    shape = inputs['L0_attn_dense'].shape
    args.append(nc.dram_tensor("out_0_dram", shape, _mybir.dt.float32, kind="ExternalOutput").ap())
    sandwich_kernel(nc, *args)
    r = _run(nc, [arrays], core_ids=[0])
    return r.results[0]["out_0_dram"]
```
